# Optimizing a Trainium2 kernel written in Bass

```python
import numpy as np
import jax
import jax.numpy as jnp

def _softmax(x, axis=-1):
    return jax.nn.softmax(x, axis=axis)

def _gelu(x):
    return jax.nn.gelu(x, approximate=True)

def _silu(x):
    return jax.nn.silu(x)

def _sigmoid(x):
    return jax.nn.sigmoid(x)

def _layernorm(x, axis=-1, eps=1e-05):
    m = jnp.mean(x, axis=axis, keepdims=True)
    v = jnp.var(x, axis=axis, keepdims=True)
    return (x - m) / jnp.sqrt(v + eps)

def _scatter_add(tgt, idx, src, axis=0):
    return tgt.at[idx].add(src)

def _segment_sum(src, seg, n):
    return jax.ops.segment_sum(src, seg, n)
kernel_name = 'mk_xattn_ffn_d4_seqx_r4_e61f0c'

def setup_inputs(seed: int=0):
    np.random.seed(seed)
    _w = jnp.asarray

    def _rec_inputs():
        import jax
        import jax.numpy as jnp
        _rk = jax.random.key(seed)
        x = -0.0003929 + 0.9999 * jax.random.normal(jax.random.fold_in(_rk, 1), (8, 112, 256), jnp.float32)
        _lenS = 112 - jax.random.randint(jax.random.fold_in(_rk, 7), (8,), 0, max(1, 112 // 4) + 1, jnp.int32)
        _lenS2 = 375 - jax.random.randint(jax.random.fold_in(_rk, 8), (8,), 0, max(1, 375 // 4) + 1, jnp.int32)
        _ctx_512P = jax.random.normal(jax.random.fold_in(_rk, 11), (8, 16, 128), jnp.float32)
        _ctx_512c = jax.random.dirichlet(jax.random.fold_in(_rk, 511), 0.3 * jnp.ones((16,), jnp.float32), (8, 375))
        _ctx_512t = jnp.einsum('bsk,bkd->bsd', _ctx_512c, _ctx_512P)
        _ctx_512t = _ctx_512t * jax.lax.rsqrt(jnp.mean(jnp.square(_ctx_512t)) + 1e-12) * 0.953939
        ctx_512 = -1.39393e-06 + 0.999914 * (_ctx_512t + 0.3 * jax.random.normal(jax.random.fold_in(_rk, 611), (8, 375, 128), jnp.float32))
        return (x, ctx_512)
    x, ctx_512 = _rec_inputs()

    def _L0_xattn_setup():
        import jax, jax.numpy as jnp
        import numpy as np
        HEADS = 16
        D_MODEL = 256
        IMG_MODEL = 128
        D_K = D_MODEL // HEADS
        key = jax.random.key(seed)
        ks = jax.random.split(key, 12)
        B, LQ, LKV = (8, 512, 256)
        s_dm = 1.0 / np.sqrt(D_MODEL)
        s_im = 1.0 / np.sqrt(IMG_MODEL)
        return {'q': jax.random.normal(ks[0], (B, LQ, D_MODEL), jnp.float32), 'k': jax.random.normal(ks[1], (B, LKV, IMG_MODEL), jnp.float32), 'v': jax.random.normal(ks[2], (B, LKV, IMG_MODEL), jnp.float32), 'Wq': jax.random.normal(ks[3], (D_MODEL, D_MODEL), jnp.float32) * s_dm, 'bq': jnp.zeros((D_MODEL,), jnp.float32), 'Wk': jax.random.normal(ks[4], (IMG_MODEL, D_MODEL), jnp.float32) * s_im, 'bk': jnp.zeros((D_MODEL,), jnp.float32), 'Wv': jax.random.normal(ks[5], (IMG_MODEL, D_MODEL), jnp.float32) * s_im, 'bv': jnp.zeros((D_MODEL,), jnp.float32), 'Wo': jax.random.normal(ks[6], (D_MODEL, D_MODEL), jnp.float32) * s_dm, 'bo': jnp.zeros((D_MODEL,), jnp.float32)}
    _L0_xattn_all = _L0_xattn_setup()
    _L0_xattn_in = {k: v for k, v in _L0_xattn_all.items() if k in ('Wq', 'bq', 'Wk', 'bk', 'Wv', 'bv', 'Wo', 'bo')}
    del _L0_xattn_all

    def _L0_ffn_setup():
        import jax, jax.numpy as jnp
        import numpy as np
        import math
        GOLDEN_CENTER = 1.0 / math.e
        GOLDEN_LOWER = 0.5 - math.log(4.0 / 3.0)
        GOLDEN_UPPER = 0.5
        B, T, D = (4, 512, 256)
        E = 8
        I = 1024 // (E // 2)

        def _routing_weights(x, Wr, temperature):
            inh = jax.nn.sigmoid(x @ Wr / temperature)
            in_zone = (inh >= GOLDEN_LOWER) & (inh <= GOLDEN_UPPER)
            dist = jnp.abs(inh - GOLDEN_CENTER)
            w = jnp.exp(-dist / 0.1) * in_zone.astype(x.dtype)
            wsum = w.sum(axis=-1, keepdims=True)
            no_expert = wsum < 1e-08
            fb = jnp.exp(-dist / 0.3)
            _, top2 = jax.lax.top_k(fb, 2)
            fb_mask = jax.nn.one_hot(top2, E, dtype=x.dtype).sum(axis=-2)
            fb_w = fb * fb_mask
            fb_w = fb_w / jnp.clip(fb_w.sum(axis=-1, keepdims=True), 1e-08)
            w = jnp.where(no_expert, fb_w, w)
            wsum = w.sum(axis=-1, keepdims=True)
            return w / jnp.clip(wsum, 1e-08)
        key = jax.random.key(seed)
        k = jax.random.split(key, 6)
        s_d = 1.0 / math.sqrt(D)
        s_i = 1.0 / math.sqrt(I)
        return {'x': jax.random.normal(k[0], (B, T, D), jnp.float32), 'Wg': jax.random.normal(k[1], (E, D, I), jnp.float32) * s_d, 'Wu': jax.random.normal(k[2], (E, D, I), jnp.float32) * s_d, 'Wd': jax.random.normal(k[3], (E, I, D), jnp.float32) * s_i, 'Wr': jax.random.normal(k[4], (D, E), jnp.float32) * s_d, 'temperature': jnp.ones((1,), jnp.float32)}
    _L0_ffn_all = _L0_ffn_setup()
    _L0_ffn_in = {k: v for k, v in _L0_ffn_all.items() if k in ('Wg', 'Wu', 'Wd', 'Wr', 'temperature')}
    del _L0_ffn_all

    def _L1_xattn_setup():
        import jax, jax.numpy as jnp
        import numpy as np
        H, D, C1, C2, S, M, B, W = (16, 32, 256, 128, 512, 128, 2, 4)

        def _ln(x, g, b):
            m = jnp.mean(x, -1, keepdims=True)
            v = jnp.var(x, -1, keepdims=True)
            return (x - m) * jax.lax.rsqrt(v + 1e-05) * g + b

        def _mha(x, y, wq, wk, wv, li1_w, li1_b, lnx_g, lnx_b, lny_g, lny_b, ln3_g, ln3_b, li2_w, li2_b, li3_w, li3_b, causal):
            xn = _ln(x, lnx_g, lnx_b)
            yn = _ln(y, lny_g, lny_b)
            q = jnp.einsum('bsc,hcd->bhsd', xn, wq)
            k = jnp.einsum('btc,hcd->bhtd', yn, wk)
            v = jnp.einsum('btc,hcd->bhtd', yn, wv)
            a = jax.nn.softmax(jnp.einsum('bhsd,bhtd->bhst', q, k) * D ** (-0.5), axis=-1)
            if causal:
                s, t = (a.shape[-2], a.shape[-1])
                mask = (jnp.arange(t)[None, :] > jnp.arange(s)[:, None]).astype(a.dtype)
                a = a * mask
            o = jnp.einsum('bhst,bhtd->bhsd', a, v)
            o = o.transpose(0, 2, 1, 3).reshape(x.shape[0], x.shape[1], H * D)
            x_out = x + o @ li1_w + li1_b
            h = jax.nn.gelu(_ln(x_out, ln3_g, ln3_b) @ li2_w + li2_b, approximate=False)
            return x_out + h @ li3_w + li3_b
        key = jax.random.key(seed)
        ks = iter(jax.random.split(key, 64))

        def w(shape, scale=0.02):
            return jax.random.normal(next(ks), shape, jnp.float32) * scale
        inp = {'xx': jax.random.normal(next(ks), (B, S, C1), jnp.float32), 'ee': jax.random.normal(next(ks), (B, M, C2), jnp.float32), 'ln1_g': jnp.ones(C1, jnp.float32), 'ln1_b': jnp.zeros(C1, jnp.float32), 'ln2_g': jnp.ones(C1, jnp.float32), 'ln2_b': jnp.zeros(C1, jnp.float32)}
        for pfx, cy in (('a1', C1), ('a2', C2)):
            inp[pfx + '_wq'] = w((H, C1, D))
            inp[pfx + '_wk'] = w((H, cy, D))
            inp[pfx + '_wv'] = w((H, cy, D))
            inp[pfx + '_li1_w'] = w((H * D, C1))
            inp[pfx + '_li1_b'] = jnp.zeros(C1, jnp.float32)
            inp[pfx + '_lnx_g'] = jnp.ones(C1, jnp.float32)
            inp[pfx + '_lnx_b'] = jnp.zeros(C1, jnp.float32)
            inp[pfx + '_lny_g'] = jnp.ones(cy, jnp.float32)
            inp[pfx + '_lny_b'] = jnp.zeros(cy, jnp.float32)
            inp[pfx + '_ln3_g'] = jnp.ones(C1, jnp.float32)
            inp[pfx + '_ln3_b'] = jnp.zeros(C1, jnp.float32)
            inp[pfx + '_li2_w'] = w((C1, C1 * W))
            inp[pfx + '_li2_b'] = jnp.zeros(C1 * W, jnp.float32)
            inp[pfx + '_li3_w'] = w((C1 * W, C1))
            inp[pfx + '_li3_b'] = jnp.zeros(C1, jnp.float32)
        inp['training'] = 0
        return inp
    _L1_xattn_all = _L1_xattn_setup()
    _L1_xattn_in = {k: v for k, v in _L1_xattn_all.items() if k in ('ln1_g', 'ln1_b', 'ln2_g', 'ln2_b', 'a1_wq', 'a1_wk', 'a1_wv', 'a1_li1_w', 'a1_li1_b', 'a1_lnx_g', 'a1_lnx_b', 'a1_lny_g', 'a1_lny_b', 'a1_ln3_g', 'a1_ln3_b', 'a1_li2_w', 'a1_li2_b', 'a1_li3_w', 'a1_li3_b', 'a2_wq', 'a2_wk', 'a2_wv', 'a2_li1_w', 'a2_li1_b', 'a2_lnx_g', 'a2_lnx_b', 'a2_lny_g', 'a2_lny_b', 'a2_ln3_g', 'a2_ln3_b', 'a2_li2_w', 'a2_li2_b', 'a2_li3_w', 'a2_li3_b')}
    del _L1_xattn_all

    def _L1_ffn_setup():
        import jax, jax.numpy as jnp
        import numpy as np
        B, S, D = (1, 512, 256)
        E, K, F = (64, 8, 192)
        SF = 192
        C = 128
        ROUTED_SCALE = 1.0

        def _moe_forward(x, router_w, w_gate, w_up, w_down, ws_gate_up, ws_down):
            T = x.shape[0]
            logits = x.astype(jnp.float32) @ router_w.T
            probs = jax.nn.softmax(logits, axis=-1)
            topk_w, topk_ids = jax.lax.top_k(probs, K)
            topk_w = topk_w / jnp.sum(topk_w, axis=-1, keepdims=True)
            topk_w = topk_w.astype(x.dtype)
            N = T * K
            flat_e = topk_ids.reshape(-1)
            flat_w = topk_w.reshape(-1)
            tok = jnp.arange(N) // K
            onehot = flat_e[:, None] == jnp.arange(E)[None, :]
            pos = jnp.cumsum(onehot, axis=0)[jnp.arange(N), flat_e] - 1
            valid = pos < C
            idx = jnp.where(valid, flat_e * C + pos, E * C)
            x_buf = jnp.zeros((E * C + 1, x.shape[1]), x.dtype).at[idx].set(x[tok])
            xb = x_buf[:E * C].reshape(E, C, -1)
            g = jnp.einsum('ecd,edf->ecf', xb, w_gate)
            u = jnp.einsum('ecd,edf->ecf', xb, w_up)
            h = jax.nn.silu(g) * u
            y = jnp.einsum('ecf,efd->ecd', h, w_down).reshape(E * C, -1)
            safe = jnp.where(valid, idx, 0)
            contrib = y[safe] * (flat_w * valid.astype(flat_w.dtype))[:, None]
            routed = jax.ops.segment_sum(contrib, tok, num_segments=T)
            routed = routed * ROUTED_SCALE
            gu = x @ ws_gate_up
            sg, su = (gu[:, :SF], gu[:, SF:])
            shared = jax.nn.silu(sg) * su @ ws_down
            return routed + shared
        key = jax.random.key(seed)
        ks = jax.random.split(key, 7)
        w = 0.02
        return {'hidden_states': jax.random.normal(ks[0], (B, S, D), jnp.float32), 'router_w': jax.random.normal(ks[1], (E, D), jnp.float32) * w, 'w_gate': jax.random.normal(ks[2], (E, D, F), jnp.float32) * w, 'w_up': jax.random.normal(ks[3], (E, D, F), jnp.float32) * w, 'w_down': jax.random.normal(ks[4], (E, F, D), jnp.float32) * w, 'ws_gate_up': jax.random.normal(ks[5], (D, 2 * SF), jnp.float32) * w, 'ws_down': jax.random.normal(ks[6], (SF, D), jnp.float32) * w}
    _L1_ffn_all = _L1_ffn_setup()
    _L1_ffn_in = {k: v for k, v in _L1_ffn_all.items() if k in ('router_w', 'w_gate', 'w_up', 'w_down', 'ws_gate_up', 'ws_down')}
    del _L1_ffn_all

    def _L2_xattn_setup():
        import jax, jax.numpy as jnp
        import numpy as np
        DIM = 256
        LATENT_DIM = 128
        NUM_HEADS = 16
        HEAD_DIM = DIM // NUM_HEADS
        SCALE = HEAD_DIM ** (-0.5)
        key = jax.random.key(seed)
        k1, k2, k3, k4, k5 = jax.random.split(key, 5)
        B, xN, zN = (2, 512, 512)
        x = jax.random.normal(k1, (B, xN, DIM), dtype=jnp.float32)
        z = jax.random.normal(k2, (B, zN, LATENT_DIM), dtype=jnp.float32)
        Wq = jax.random.normal(k3, (DIM, DIM), dtype=jnp.float32) * DIM ** (-0.5)
        Wkv = jax.random.normal(k4, (2 * DIM, LATENT_DIM), dtype=jnp.float32) * LATENT_DIM ** (-0.5)
        Wo = jax.random.normal(k5, (DIM, DIM), dtype=jnp.float32) * DIM ** (-0.5)
        return {'x': x, 'z': z, 'Wq': Wq, 'Wkv': Wkv, 'Wo': Wo}
    _L2_xattn_all = _L2_xattn_setup()
    _L2_xattn_in = {k: v for k, v in _L2_xattn_all.items() if k in ('Wq', 'Wkv', 'Wo')}
    del _L2_xattn_all

    def _L2_ffn_setup():
        import jax, jax.numpy as jnp
        import numpy as np
        TOP_K = 2
        key = jax.random.key(seed)
        ks = jax.random.split(key, 8)
        B, S, D = (2, 512, 256)
        N_r, N_s = (16, 2)
        u = jax.random.normal(ks[0], (B, S, D), dtype=jnp.float32)
        centroids = jax.random.normal(ks[1], (N_r, D), dtype=jnp.float32)
        expert_biases = jnp.zeros((N_r,), dtype=jnp.float32)
        Wr = jax.random.normal(ks[2], (N_r, D, D), dtype=jnp.float32) * (1.0 / np.sqrt(D))
        br = jax.random.normal(ks[3], (N_r, D), dtype=jnp.float32) * 0.01
        Ws = jax.random.normal(ks[4], (N_s, D, D), dtype=jnp.float32) * (1.0 / np.sqrt(D))
        bs = jax.random.normal(ks[5], (N_s, D), dtype=jnp.float32) * 0.01
        return {'u': u, 'centroids': centroids, 'expert_biases': expert_biases, 'Wr': Wr, 'br': br, 'Ws': Ws, 'bs': bs}
    _L2_ffn_all = _L2_ffn_setup()
    _L2_ffn_in = {k: v for k, v in _L2_ffn_all.items() if k in ('centroids', 'expert_biases', 'Wr', 'br', 'Ws', 'bs')}
    del _L2_ffn_all

    def _L3_xattn_setup():
        import jax, jax.numpy as jnp
        import numpy as np
        B, LQ, LK = (8, 512, 512)
        QD, KD, VD = (256, 128, 128)
        key = jax.random.key(seed)
        ks = jax.random.split(key, 9)
        s = 0.02
        return {'query': jax.random.normal(ks[0], (B, LQ, QD), jnp.float32), 'key': jax.random.normal(ks[1], (B, LK, KD), jnp.float32), 'value': jax.random.normal(ks[2], (B, LK, VD), jnp.float32), 'Wq': jax.random.normal(ks[3], (QD, QD), jnp.float32) * s, 'bq': jnp.zeros((QD,), jnp.float32), 'Wk': jax.random.normal(ks[4], (KD, QD), jnp.float32) * s, 'bk': jnp.zeros((QD,), jnp.float32), 'Wv': jax.random.normal(ks[5], (VD, QD), jnp.float32) * s, 'bv': jnp.zeros((QD,), jnp.float32)}
    _L3_xattn_all = _L3_xattn_setup()
    _L3_xattn_in = {k: v for k, v in _L3_xattn_all.items() if k in ('Wq', 'bq', 'Wk', 'bk', 'Wv', 'bv')}
    del _L3_xattn_all

    def _L3_ffn_setup():
        import jax, jax.numpy as jnp
        import numpy as np
        DIM = 256
        HIDDEN = 768
        SCALE = 1.0 / 127.0

        def _dequant(w_int, dtype):
            return w_int.astype(dtype) * jnp.asarray(SCALE, dtype)
        key = jax.random.key(seed)
        k_x, k_g, k_u, k_d = jax.random.split(key, 4)
        x = jax.random.normal(k_x, (4, 512, DIM), dtype=jnp.float32)
        w_gate = jax.random.randint(k_g, (HIDDEN, DIM), -127, 128, dtype=jnp.int32)
        w_up = jax.random.randint(k_u, (HIDDEN, DIM), -127, 128, dtype=jnp.int32)
        w_down = jax.random.randint(k_d, (DIM, HIDDEN), -127, 128, dtype=jnp.int32)
        return {'x': x, 'w_gate': w_gate, 'w_up': w_up, 'w_down': w_down}
    _L3_ffn_all = _L3_ffn_setup()
    _L3_ffn_in = {k: v for k, v in _L3_ffn_all.items() if k in ('w_gate', 'w_up', 'w_down')}
    del _L3_ffn_all
    return {'x': x, 'ctx_512': ctx_512, 'L0_xattn_Wq': _L0_xattn_in['Wq'], 'L0_xattn_bq': _L0_xattn_in['bq'], 'L0_xattn_Wk': _L0_xattn_in['Wk'], 'L0_xattn_bk': _L0_xattn_in['bk'], 'L0_xattn_Wv': _L0_xattn_in['Wv'], 'L0_xattn_bv': _L0_xattn_in['bv'], 'L0_xattn_Wo': _L0_xattn_in['Wo'], 'L0_xattn_bo': _L0_xattn_in['bo'], 'L0_ffn_Wg': _L0_ffn_in['Wg'], 'L0_ffn_Wu': _L0_ffn_in['Wu'], 'L0_ffn_Wd': _L0_ffn_in['Wd'], 'L0_ffn_Wr': _L0_ffn_in['Wr'], 'L0_ffn_temperature': _L0_ffn_in['temperature'], 'L1_xattn_ln1_g': _L1_xattn_in['ln1_g'], 'L1_xattn_ln1_b': _L1_xattn_in['ln1_b'], 'L1_xattn_ln2_g': _L1_xattn_in['ln2_g'], 'L1_xattn_ln2_b': _L1_xattn_in['ln2_b'], 'L1_xattn_a1_wq': _L1_xattn_in['a1_wq'], 'L1_xattn_a1_wk': _L1_xattn_in['a1_wk'], 'L1_xattn_a1_wv': _L1_xattn_in['a1_wv'], 'L1_xattn_a1_li1_w': _L1_xattn_in['a1_li1_w'], 'L1_xattn_a1_li1_b': _L1_xattn_in['a1_li1_b'], 'L1_xattn_a1_lnx_g': _L1_xattn_in['a1_lnx_g'], 'L1_xattn_a1_lnx_b': _L1_xattn_in['a1_lnx_b'], 'L1_xattn_a1_lny_g': _L1_xattn_in['a1_lny_g'], 'L1_xattn_a1_lny_b': _L1_xattn_in['a1_lny_b'], 'L1_xattn_a1_ln3_g': _L1_xattn_in['a1_ln3_g'], 'L1_xattn_a1_ln3_b': _L1_xattn_in['a1_ln3_b'], 'L1_xattn_a1_li2_w': _L1_xattn_in['a1_li2_w'], 'L1_xattn_a1_li2_b': _L1_xattn_in['a1_li2_b'], 'L1_xattn_a1_li3_w': _L1_xattn_in['a1_li3_w'], 'L1_xattn_a1_li3_b': _L1_xattn_in['a1_li3_b'], 'L1_xattn_a2_wq': _L1_xattn_in['a2_wq'], 'L1_xattn_a2_wk': _L1_xattn_in['a2_wk'], 'L1_xattn_a2_wv': _L1_xattn_in['a2_wv'], 'L1_xattn_a2_li1_w': _L1_xattn_in['a2_li1_w'], 'L1_xattn_a2_li1_b': _L1_xattn_in['a2_li1_b'], 'L1_xattn_a2_lnx_g': _L1_xattn_in['a2_lnx_g'], 'L1_xattn_a2_lnx_b': _L1_xattn_in['a2_lnx_b'], 'L1_xattn_a2_lny_g': _L1_xattn_in['a2_lny_g'], 'L1_xattn_a2_lny_b': _L1_xattn_in['a2_lny_b'], 'L1_xattn_a2_ln3_g': _L1_xattn_in['a2_ln3_g'], 'L1_xattn_a2_ln3_b': _L1_xattn_in['a2_ln3_b'], 'L1_xattn_a2_li2_w': _L1_xattn_in['a2_li2_w'], 'L1_xattn_a2_li2_b': _L1_xattn_in['a2_li2_b'], 'L1_xattn_a2_li3_w': _L1_xattn_in['a2_li3_w'], 'L1_xattn_a2_li3_b': _L1_xattn_in['a2_li3_b'], 'L1_ffn_router_w': _L1_ffn_in['router_w'], 'L1_ffn_w_gate': _L1_ffn_in['w_gate'], 'L1_ffn_w_up': _L1_ffn_in['w_up'], 'L1_ffn_w_down': _L1_ffn_in['w_down'], 'L1_ffn_ws_gate_up': _L1_ffn_in['ws_gate_up'], 'L1_ffn_ws_down': _L1_ffn_in['ws_down'], 'L2_xattn_Wq': _L2_xattn_in['Wq'], 'L2_xattn_Wkv': _L2_xattn_in['Wkv'], 'L2_xattn_Wo': _L2_xattn_in['Wo'], 'L2_ffn_centroids': _L2_ffn_in['centroids'], 'L2_ffn_expert_biases': _L2_ffn_in['expert_biases'], 'L2_ffn_Wr': _L2_ffn_in['Wr'], 'L2_ffn_br': _L2_ffn_in['br'], 'L2_ffn_Ws': _L2_ffn_in['Ws'], 'L2_ffn_bs': _L2_ffn_in['bs'], 'L3_xattn_Wq': _L3_xattn_in['Wq'], 'L3_xattn_bq': _L3_xattn_in['bq'], 'L3_xattn_Wk': _L3_xattn_in['Wk'], 'L3_xattn_bk': _L3_xattn_in['bk'], 'L3_xattn_Wv': _L3_xattn_in['Wv'], 'L3_xattn_bv': _L3_xattn_in['bv'], 'L3_ffn_w_gate': _L3_ffn_in['w_gate'], 'L3_ffn_w_up': _L3_ffn_in['w_up'], 'L3_ffn_w_down': _L3_ffn_in['w_down']}

def reference(x, ctx_512, L0_xattn_Wq, L0_xattn_bq, L0_xattn_Wk, L0_xattn_bk, L0_xattn_Wv, L0_xattn_bv, L0_xattn_Wo, L0_xattn_bo, L0_ffn_Wg, L0_ffn_Wu, L0_ffn_Wd, L0_ffn_Wr, L0_ffn_temperature, L1_xattn_ln1_g, L1_xattn_ln1_b, L1_xattn_ln2_g, L1_xattn_ln2_b, L1_xattn_a1_wq, L1_xattn_a1_wk, L1_xattn_a1_wv, L1_xattn_a1_li1_w, L1_xattn_a1_li1_b, L1_xattn_a1_lnx_g, L1_xattn_a1_lnx_b, L1_xattn_a1_lny_g, L1_xattn_a1_lny_b, L1_xattn_a1_ln3_g, L1_xattn_a1_ln3_b, L1_xattn_a1_li2_w, L1_xattn_a1_li2_b, L1_xattn_a1_li3_w, L1_xattn_a1_li3_b, L1_xattn_a2_wq, L1_xattn_a2_wk, L1_xattn_a2_wv, L1_xattn_a2_li1_w, L1_xattn_a2_li1_b, L1_xattn_a2_lnx_g, L1_xattn_a2_lnx_b, L1_xattn_a2_lny_g, L1_xattn_a2_lny_b, L1_xattn_a2_ln3_g, L1_xattn_a2_ln3_b, L1_xattn_a2_li2_w, L1_xattn_a2_li2_b, L1_xattn_a2_li3_w, L1_xattn_a2_li3_b, L1_ffn_router_w, L1_ffn_w_gate, L1_ffn_w_up, L1_ffn_w_down, L1_ffn_ws_gate_up, L1_ffn_ws_down, L2_xattn_Wq, L2_xattn_Wkv, L2_xattn_Wo, L2_ffn_centroids, L2_ffn_expert_biases, L2_ffn_Wr, L2_ffn_br, L2_ffn_Ws, L2_ffn_bs, L3_xattn_Wq, L3_xattn_bq, L3_xattn_Wk, L3_xattn_bk, L3_xattn_Wv, L3_xattn_bv, L3_ffn_w_gate, L3_ffn_w_up, L3_ffn_w_down):
    import jax
    import jax.numpy as jnp

    def _L0_xattn_ref(q, k, v, Wq, bq, Wk, bk, Wv, bv, Wo, bo):
        import jax, jax.numpy as jnp
        import numpy as np
        HEADS = 16
        D_MODEL = 256
        IMG_MODEL = 128
        D_K = D_MODEL // HEADS
        B, LQ, _ = q.shape
        LKV = k.shape[1]
        qh = (q @ Wq + bq).reshape(B, LQ, HEADS, D_K).transpose(0, 2, 1, 3)
        kh = (k @ Wk + bk).reshape(B, LKV, HEADS, D_K).transpose(0, 2, 1, 3)
        vh = (v @ Wv + bv).reshape(B, LKV, HEADS, D_K).transpose(0, 2, 1, 3)
        scale = 1.0 / np.sqrt(D_K)
        scores = jnp.einsum('bhqd,bhkd->bhqk', qh, kh) * scale
        attn = jax.nn.softmax(scores, axis=-1)
        out = jnp.einsum('bhqk,bhkd->bhqd', attn, vh)
        concat = out.transpose(0, 2, 1, 3).reshape(B, LQ, D_MODEL)
        return concat @ Wo + bo

    def _L0_ffn_ref(x, Wg, Wu, Wd, Wr, temperature):
        import jax, jax.numpy as jnp
        import numpy as np
        import math
        GOLDEN_CENTER = 1.0 / math.e
        GOLDEN_LOWER = 0.5 - math.log(4.0 / 3.0)
        GOLDEN_UPPER = 0.5
        B, T, D = (4, 512, 256)
        E = 8
        I = 1024 // (E // 2)

        def _routing_weights(x, Wr, temperature):
            inh = jax.nn.sigmoid(x @ Wr / temperature)
            in_zone = (inh >= GOLDEN_LOWER) & (inh <= GOLDEN_UPPER)
            dist = jnp.abs(inh - GOLDEN_CENTER)
            w = jnp.exp(-dist / 0.1) * in_zone.astype(x.dtype)
            wsum = w.sum(axis=-1, keepdims=True)
            no_expert = wsum < 1e-08
            fb = jnp.exp(-dist / 0.3)
            _, top2 = jax.lax.top_k(fb, 2)
            fb_mask = jax.nn.one_hot(top2, E, dtype=x.dtype).sum(axis=-2)
            fb_w = fb * fb_mask
            fb_w = fb_w / jnp.clip(fb_w.sum(axis=-1, keepdims=True), 1e-08)
            w = jnp.where(no_expert, fb_w, w)
            wsum = w.sum(axis=-1, keepdims=True)
            return w / jnp.clip(wsum, 1e-08)
        weights = _routing_weights(x, Wr, temperature)
        gate = jnp.einsum('btd,edi->beti', x, Wg)
        up = jnp.einsum('btd,edi->beti', x, Wu)
        h = jax.nn.silu(gate) * up
        e_out = jnp.einsum('beti,eid->betd', h, Wd)
        out = jnp.einsum('bte,betd->btd', weights, e_out)
        return out

    def _L1_xattn_ref(xx, ee, ln1_g, ln1_b, ln2_g, ln2_b, a1_wq, a1_wk, a1_wv, a1_li1_w, a1_li1_b, a1_lnx_g, a1_lnx_b, a1_lny_g, a1_lny_b, a1_ln3_g, a1_ln3_b, a1_li2_w, a1_li2_b, a1_li3_w, a1_li3_b, a2_wq, a2_wk, a2_wv, a2_li1_w, a2_li1_b, a2_lnx_g, a2_lnx_b, a2_lny_g, a2_lny_b, a2_ln3_g, a2_ln3_b, a2_li2_w, a2_li2_b, a2_li3_w, a2_li3_b, training):
        import jax, jax.numpy as jnp
        import numpy as np
        H, D, C1, C2, S, M, B, W = (16, 32, 256, 128, 512, 128, 2, 4)

        def _ln(x, g, b):
            m = jnp.mean(x, -1, keepdims=True)
            v = jnp.var(x, -1, keepdims=True)
            return (x - m) * jax.lax.rsqrt(v + 1e-05) * g + b

        def _mha(x, y, wq, wk, wv, li1_w, li1_b, lnx_g, lnx_b, lny_g, lny_b, ln3_g, ln3_b, li2_w, li2_b, li3_w, li3_b, causal):
            xn = _ln(x, lnx_g, lnx_b)
            yn = _ln(y, lny_g, lny_b)
            q = jnp.einsum('bsc,hcd->bhsd', xn, wq)
            k = jnp.einsum('btc,hcd->bhtd', yn, wk)
            v = jnp.einsum('btc,hcd->bhtd', yn, wv)
            a = jax.nn.softmax(jnp.einsum('bhsd,bhtd->bhst', q, k) * D ** (-0.5), axis=-1)
            if causal:
                s, t = (a.shape[-2], a.shape[-1])
                mask = (jnp.arange(t)[None, :] > jnp.arange(s)[:, None]).astype(a.dtype)
                a = a * mask
            o = jnp.einsum('bhst,bhtd->bhsd', a, v)
            o = o.transpose(0, 2, 1, 3).reshape(x.shape[0], x.shape[1], H * D)
            x_out = x + o @ li1_w + li1_b
            h = jax.nn.gelu(_ln(x_out, ln3_g, ln3_b) @ li2_w + li2_b, approximate=False)
            return x_out + h @ li3_w + li3_b
        x = _ln(xx, ln1_g, ln1_b)
        x = x + _mha(x, x, a1_wq, a1_wk, a1_wv, a1_li1_w, a1_li1_b, a1_lnx_g, a1_lnx_b, a1_lny_g, a1_lny_b, a1_ln3_g, a1_ln3_b, a1_li2_w, a1_li2_b, a1_li3_w, a1_li3_b, causal=True)
        x = _ln(x, ln2_g, ln2_b)
        return x + _mha(x, ee, a2_wq, a2_wk, a2_wv, a2_li1_w, a2_li1_b, a2_lnx_g, a2_lnx_b, a2_lny_g, a2_lny_b, a2_ln3_g, a2_ln3_b, a2_li2_w, a2_li2_b, a2_li3_w, a2_li3_b, causal=False)

    def _L1_ffn_ref(hidden_states, router_w, w_gate, w_up, w_down, ws_gate_up, ws_down):
        import jax, jax.numpy as jnp
        import numpy as np
        B, S, D = (1, 512, 256)
        E, K, F = (64, 8, 192)
        SF = 192
        C = 128
        ROUTED_SCALE = 1.0

        def _moe_forward(x, router_w, w_gate, w_up, w_down, ws_gate_up, ws_down):
            T = x.shape[0]
            logits = x.astype(jnp.float32) @ router_w.T
            probs = jax.nn.softmax(logits, axis=-1)
            topk_w, topk_ids = jax.lax.top_k(probs, K)
            topk_w = topk_w / jnp.sum(topk_w, axis=-1, keepdims=True)
            topk_w = topk_w.astype(x.dtype)
            N = T * K
            flat_e = topk_ids.reshape(-1)
            flat_w = topk_w.reshape(-1)
            tok = jnp.arange(N) // K
            onehot = flat_e[:, None] == jnp.arange(E)[None, :]
            pos = jnp.cumsum(onehot, axis=0)[jnp.arange(N), flat_e] - 1
            valid = pos < C
            idx = jnp.where(valid, flat_e * C + pos, E * C)
            x_buf = jnp.zeros((E * C + 1, x.shape[1]), x.dtype).at[idx].set(x[tok])
            xb = x_buf[:E * C].reshape(E, C, -1)
            g = jnp.einsum('ecd,edf->ecf', xb, w_gate)
            u = jnp.einsum('ecd,edf->ecf', xb, w_up)
            h = jax.nn.silu(g) * u
            y = jnp.einsum('ecf,efd->ecd', h, w_down).reshape(E * C, -1)
            safe = jnp.where(valid, idx, 0)
            contrib = y[safe] * (flat_w * valid.astype(flat_w.dtype))[:, None]
            routed = jax.ops.segment_sum(contrib, tok, num_segments=T)
            routed = routed * ROUTED_SCALE
            gu = x @ ws_gate_up
            sg, su = (gu[:, :SF], gu[:, SF:])
            shared = jax.nn.silu(sg) * su @ ws_down
            return routed + shared
        b, s, d = hidden_states.shape
        x = hidden_states.reshape(-1, d)
        out = _moe_forward(x, router_w, w_gate, w_up, w_down, ws_gate_up, ws_down)
        return out.reshape(b, s, d)

    def _L2_xattn_ref(x, z, Wq, Wkv, Wo):
        import jax, jax.numpy as jnp
        import numpy as np
        DIM = 256
        LATENT_DIM = 128
        NUM_HEADS = 16
        HEAD_DIM = DIM // NUM_HEADS
        SCALE = HEAD_DIM ** (-0.5)
        B, xN, _ = x.shape
        _, zN, _ = z.shape
        Q = (x @ Wq.T).reshape(B, xN, NUM_HEADS, HEAD_DIM)
        KV = (z @ Wkv.T).reshape(B, zN, 2, NUM_HEADS, HEAD_DIM)
        K = KV[:, :, 0]
        V = KV[:, :, 1]
        attn = jnp.einsum('bqhd,bkhd->bhqk', Q, K) * SCALE
        attn = jax.nn.softmax(attn, axis=-1)
        O = jnp.einsum('bhqk,bkhd->bqhd', attn, V).reshape(B, xN, DIM)
        return O @ Wo.T

    def _L2_ffn_ref(u, centroids, expert_biases, Wr, br, Ws, bs):
        import jax, jax.numpy as jnp
        import numpy as np
        TOP_K = 2
        N_r = centroids.shape[0]
        N_s = Ws.shape[0]
        raw_scores = jnp.einsum('bsd,ed->bse', u, centroids)
        s = jax.nn.softmax(raw_scores + expert_biases, axis=-1)
        topk_vals, topk_idx = jax.lax.top_k(s, TOP_K)
        g_topk = jnp.sum(jax.nn.one_hot(topk_idx, N_r, dtype=s.dtype) * topk_vals[..., None], axis=-2)
        xe = jnp.einsum('bsd,eod->bseo', u, Wr) + br
        routed = jnp.einsum('bse,bseo->bso', g_topk, xe)
        shared = (jnp.einsum('bsd,eod->bso', u, Ws) + jnp.sum(bs, axis=0)) / N_s
        return u + routed + shared

    def _L3_xattn_ref(query, key, value, Wq, bq, Wk, bk, Wv, bv):
        import jax, jax.numpy as jnp
        import numpy as np
        B, LQ, LK = (8, 512, 512)
        QD, KD, VD = (256, 128, 128)
        q = jnp.einsum('bld,de->ble', query, Wq) + bq
        k = jnp.einsum('bld,de->ble', key, Wk) + bk
        v = jnp.einsum('bld,de->ble', value, Wv) + bv
        scores = jnp.einsum('bqe,bke->bqk', q, k)
        attn = jax.nn.softmax(scores, axis=-1)
        out = jnp.einsum('bqk,bke->bqe', attn, v)
        return out

    def _L3_ffn_ref(x, w_gate, w_up, w_down):
        import jax, jax.numpy as jnp
        import numpy as np
        DIM = 256
        HIDDEN = 768
        SCALE = 1.0 / 127.0

        def _dequant(w_int, dtype):
            return w_int.astype(dtype) * jnp.asarray(SCALE, dtype)
        wg = _dequant(w_gate, x.dtype)
        wu = _dequant(w_up, x.dtype)
        wd = _dequant(w_down, x.dtype)
        gate = jnp.einsum('bsd,hd->bsh', x, wg)
        up = jnp.einsum('bsd,hd->bsh', x, wu)
        h = jax.nn.silu(gate) * up
        return jnp.einsum('bsh,dh->bsd', h, wd)
    x = x + _L0_xattn_ref(_layernorm(x, axis=-1), ctx_512, ctx_512, L0_xattn_Wq, L0_xattn_bq, L0_xattn_Wk, L0_xattn_bk, L0_xattn_Wv, L0_xattn_bv, L0_xattn_Wo, L0_xattn_bo)
    x = x + _L0_ffn_ref(_layernorm(x, axis=-1), L0_ffn_Wg, L0_ffn_Wu, L0_ffn_Wd, L0_ffn_Wr, L0_ffn_temperature)
    x = x + _L1_xattn_ref(_layernorm(x, axis=-1), ctx_512, L1_xattn_ln1_g, L1_xattn_ln1_b, L1_xattn_ln2_g, L1_xattn_ln2_b, L1_xattn_a1_wq, L1_xattn_a1_wk, L1_xattn_a1_wv, L1_xattn_a1_li1_w, L1_xattn_a1_li1_b, L1_xattn_a1_lnx_g, L1_xattn_a1_lnx_b, L1_xattn_a1_lny_g, L1_xattn_a1_lny_b, L1_xattn_a1_ln3_g, L1_xattn_a1_ln3_b, L1_xattn_a1_li2_w, L1_xattn_a1_li2_b, L1_xattn_a1_li3_w, L1_xattn_a1_li3_b, L1_xattn_a2_wq, L1_xattn_a2_wk, L1_xattn_a2_wv, L1_xattn_a2_li1_w, L1_xattn_a2_li1_b, L1_xattn_a2_lnx_g, L1_xattn_a2_lnx_b, L1_xattn_a2_lny_g, L1_xattn_a2_lny_b, L1_xattn_a2_ln3_g, L1_xattn_a2_ln3_b, L1_xattn_a2_li2_w, L1_xattn_a2_li2_b, L1_xattn_a2_li3_w, L1_xattn_a2_li3_b, 0)
    x = x + _L1_ffn_ref(_layernorm(x, axis=-1), L1_ffn_router_w, L1_ffn_w_gate, L1_ffn_w_up, L1_ffn_w_down, L1_ffn_ws_gate_up, L1_ffn_ws_down)
    x = x + _L2_xattn_ref(_layernorm(x, axis=-1), ctx_512, L2_xattn_Wq, L2_xattn_Wkv, L2_xattn_Wo)
    x = x + _L2_ffn_ref(_layernorm(x, axis=-1), L2_ffn_centroids, L2_ffn_expert_biases, L2_ffn_Wr, L2_ffn_br, L2_ffn_Ws, L2_ffn_bs)
    x = x + _L3_xattn_ref(_layernorm(x, axis=-1), ctx_512, ctx_512, L3_xattn_Wq, L3_xattn_bq, L3_xattn_Wk, L3_xattn_bk, L3_xattn_Wv, L3_xattn_bv)
    x = x + _L3_ffn_ref(_layernorm(x, axis=-1), L3_ffn_w_gate, L3_ffn_w_up, L3_ffn_w_down)
    return x

_drawn_inputs = setup_inputs


def setup_inputs(seed=0):
    import zlib

    import numpy as np

    out = dict(_drawn_inputs(seed))
    spreads = {'L0_xattn_bq': (0.0, 0.1),
     'L0_xattn_bk': (0.0, 2.0),
     'L0_xattn_bv': (0.0, 0.1),
     'L0_xattn_bo': (0.0, 0.1),
     'L1_xattn_ln1_g': (1.0, 0.2),
     'L1_xattn_ln1_b': (0.0, 0.1),
     'L1_xattn_ln2_g': (1.0, 0.2),
     'L1_xattn_ln2_b': (0.0, 0.1),
     'L1_xattn_a1_li1_b': (0.0, 0.1),
     'L1_xattn_a1_lnx_g': (1.0, 0.6),
     'L1_xattn_a1_lnx_b': (0.0, 0.8),
     'L1_xattn_a1_lny_g': (1.0, 0.6),
     'L1_xattn_a1_lny_b': (0.0, 0.8),
     'L1_xattn_a1_ln3_g': (1.0, 0.6),
     'L1_xattn_a1_ln3_b': (0.0, 0.8),
     'L1_xattn_a1_li2_b': (0.0, 0.429),
     'L1_xattn_a1_li3_b': (0.0, 0.1),
     'L1_xattn_a2_li1_b': (0.0, 0.1),
     'L1_xattn_a2_lnx_g': (1.0, 0.6),
     'L1_xattn_a2_lnx_b': (0.0, 0.8),
     'L1_xattn_a2_lny_g': (1.0, 0.6),
     'L1_xattn_a2_lny_b': (0.0, 0.8),
     'L1_xattn_a2_ln3_g': (1.0, 0.6),
     'L1_xattn_a2_ln3_b': (0.0, 0.8),
     'L1_xattn_a2_li2_b': (0.0, 0.399),
     'L1_xattn_a2_li3_b': (0.0, 0.1),
     'L2_ffn_expert_biases': (0.0, 2.0),
     'L3_xattn_bq': (0.0, 0.8),
     'L3_xattn_bk': (0.0, 2.0),
     'L3_xattn_bv': (0.0, 0.525)}
    factors = {'L1_xattn_a1_wq': 8.0,
     'L1_xattn_a1_wk': 8.0,
     'L1_xattn_a2_wq': 8.0,
     'L1_xattn_a2_wk': 8.0,
     'L1_ffn_router_w': 8.0,
     'L1_ffn_w_gate': 8.0,
     'L1_ffn_w_up': 8.0,
     'L1_ffn_w_down': 8.0,
     'L1_ffn_ws_gate_up': 6.692,
     'L1_ffn_ws_down': 6.626,
     'L2_ffn_br': 38.895,
     'L2_ffn_bs': 53.971,
     'L3_xattn_Wq': 3.097,
     'L3_xattn_Wk': 2.911}
    for name, (base, spread) in spreads.items():
        noise = np.random.default_rng([zlib.crc32(name.encode()), seed]).standard_normal(out[name].shape)
        drawn = base * np.exp(spread * noise) if base else spread * noise
        out[name] = jnp.asarray(drawn.astype(out[name].dtype))
    for name, factor in factors.items():
        out[name] = (out[name] * factor).astype(out[name].dtype)
    return out
```

```python
from contextlib import ExitStack

import concourse.bass as bass
from concourse import mybir

ALU = mybir.AluOpType
ACT = mybir.ActivationFunctionType
F32 = mybir.dt.float32
I32 = mybir.dt.int32
U32 = mybir.dt.uint32
AX_X = mybir.AxisListType.X

NB, TQ, DM = 8, 112, 256
TK, DC, KP = 375, 128, 125
KJ = TK // KP
NT = NB * TQ
NH = 16
E0, E1, E2 = 8, 64, 16
TOP1 = 8
F1 = 192
FH = F1 // 2
CAP = 128
NSLOT = E1 * CAP
DROPPED = float(1 << 20)
RING = 4
EPS = 1e-5
MAGIC = float(0x5f3759df - (1 << 22) - (1 << 31))
CENTER = 0.36787944117144233
LOWER, UPPER = 0.21231792754821915, 0.5


def layout(fields):
    at, out = 0, {}
    for name, n in fields:
        out[name] = (at, n)
        at += n
    return out, at


WA, WA_N = layout([("q0", 512), ("k0", 256), ("v0", 256), ("o0", 512), ("r0", 16)]
                  + [(f"e{e}", 1536) for e in range(E0)]
                  + [("q1", 1024), ("k1", 1024), ("v1", 1024), ("o1", 1024), ("f1", 2048), ("g1", 2048)]
                  + [("q2", 1024), ("k2", 512), ("v2", 512), ("o2", 1024), ("f2", 2048), ("g2", 2048)]
                  + [("r1", 128), ("s1", 768), ("d1", 512)])
WC, WC_N = layout([("q3", 512), ("k3", 256), ("v3", 256), ("o3", 512), ("c2", 32)]
                  + [(f"p{e}", 1024) for e in range(E2 // 2)]
                  + [("ws", 1024), ("br", 256), ("q4", 512), ("k4", 256), ("v4", 256)])
WI_N = 3 * 1536
RING_N = 1280
RA, RA_N = layout([(n, DM) for n in ("bv0", "bo0", "ln1g", "ln1b", "ln2g", "ln2b", "o1b", "g1b", "o2b", "g2b")])
RC, RC_N = layout([(n, DM) for n in ("bs0", "bs1", "bv4")] + [("ebias", DM)])
CO, CO_N = layout([("bq0", 2), ("bk0", 2), ("x1g", 2), ("x1b", 2), ("y1g", 2), ("y1b", 2), ("n1g", 2), ("n1b", 2),
                   ("f1b", 8), ("x2g", 2), ("x2b", 2), ("y2g", 1), ("y2b", 1), ("n2g", 2), ("n2b", 2), ("f2b", 8),
                   ("bq4", 2), ("bk4", 2), ("even", 1), ("odd", 1), ("temp", 1)])
CS, CS_N = layout([("ident", 128), ("before", 128), ("after", 128), ("iota", E1)])


class Signal:

    def __init__(self, sem, step=1):
        self.sem, self.step = sem, step
        self.restart()

    def restart(self):
        self.sent, self.seen = 0, {}

    def by(self, ins):
        self.sent += 1
        ins.then_inc(self.sem, self.step)

    def wait(self, eng, n=1):
        self.skip(eng, n)
        eng.wait_ge(self.sem, self.seen[eng.engine] * self.step)

    def skip(self, eng, n=1):
        self.seen[eng.engine] = self.seen.get(eng.engine, 0) + n



class Slot:
    pass


def build(nc, T):
    x_d = T["x"].rearrange("b t d -> (b t) d")
    ctx_d = T["ctx"].rearrange("b (j p) d -> b p j d", p=KP)
    out_d = T["out"].rearrange("b t d -> (b t) d")

    with ExitStack() as ctx:
        def sb(name, shape, dt=F32):
            return ctx.enter_context(nc.sbuf_tensor(name, shape, dt))

        def sem(name):
            return ctx.enter_context(nc.semaphore(name))

        def dram(name, shape, dt=F32):
            return nc.dram_tensor(name, shape, dt, kind="Internal").ap()

        xmid_d = dram("xmid", [NT, DM])
        xn1_d = dram("xn1", [NT, DM])
        token_d = dram("token", [NSLOT, 1], U32)
        y_d = dram("y", [NSLOT, DM])
        slot_d = dram("slot", [NT, TOP1], U32)
        gate_d = dram("gate", [NT, TOP1])

        W = sb("W", [128, WA_N + RA_N])
        cols = sb("cols", [128, CO_N])
        consts = sb("consts", [128, CS_N])
        taken = sb("taken", [TQ, E1])
        ones = sb("ones", [TQ, TQ])
        rtemp = sb("rtemp", [TQ, 1])

        def w(name, a=None, table=WA):
            at, n = table[name]
            v = W[:, at:at + n]
            return v if a is None else v.rearrange("p (a b) -> p a b", a=a)

        def wc(name, a=None):
            return w(name, a, WC)

        def row(name, p=TQ, table=RA, base=WA_N):
            at, n = table[name]
            return W[0:p, base + at:base + at + n]

        INT0 = WC_N
        FLT0 = INT0 + WI_N
        RC0 = FLT0 + WI_N
        RING0 = RC0 + RC_N
        TOK0 = RING0 + RING * RING_N
        B0 = TOK0 + E1

        def work(n):
            nonlocal B0
            B0 += n
            assert B0 <= WA_N + RA_N
            return W[:, B0 - n:B0]
        ewg = [W[:, RING0 + r * RING_N:RING0 + r * RING_N + 768].rearrange("p (c n) -> p c n", c=2) for r in range(RING)]
        ewd = [W[0:FH, RING0 + r * RING_N + 768:RING0 + (r + 1) * RING_N].rearrange("p (c n) -> p c n", c=2) for r in range(RING)]
        expert_tokens = W[:, TOK0:TOK0 + E1].bitcast(U32)
        xg = [work(DM) for r in range(RING)]
        xidx = [work(1).bitcast(U32) for r in range(RING)]
        ey = [work(DM) for r in range(RING)]
        eT = [work(2 * CAP).rearrange("p (c t) -> p c t", c=2) for r in range(2)]
        eth, eh = [[work(2 * CAP)[0:FH].rearrange("p (c t) -> p c t", c=2) for r in range(2)] for _ in range(2)]
        ea = [work(2 * CAP)[0:FH].rearrange("p (c t) -> p c t", c=2) for r in range(2)]
        w3 = [W[:, FLT0 + 1536 * n:FLT0 + 1536 * (n + 1)] for n in range(3)]

        def col(name, c=0, p=128):
            at = CO[name][0] + c
            return cols[0:p, at:at + 1]

        def const(name):
            at, n = CS[name]
            return consts[:, at:at + n]
        ident = const("ident")

        banks = [ctx.enter_context(nc.psum_tensor(f"bank{n}", [128, 512], F32)) for n in range(8)]

        slots = []
        loop_sems = []
        for s in range(2):
            S = Slot()
            S.s = s
            slots.append(S)

            def signal(name, step=1):
                loop_sems.append(Signal(sem(f"{name}_{s}"), step))
                return loop_sems[-1]
            S.ctx_sums, S.ctxT_ready, S.z_ready, S.xn_ready = [
                signal(n) for n in ("ctx_sums", "ctxT_ready", "z_ready", "xn_ready")]
            S.xnT_sums, S.xnT_ready, S.proj_v_sums, S.proj_v_done = [
                signal(n) for n in ("xnT_sums", "xnT_ready", "proj_v_sums", "proj_v_done")]
            S.proj_s_sums, S.proj_s_done, S.score_sums, S.nmax_ready = [
                signal(n) for n in ("proj_s_sums", "proj_s_done", "score_sums", "nmax_ready")]
            S.probs_ready, S.probsT_sums, S.probsT_ready, S.av_sums = [
                signal(n) for n in ("probs_ready", "probsT_sums", "probsT_ready", "av_sums")]
            S.o_ready, S.oT_sums, S.oT_ready, S.out_sums = [
                signal(n) for n in ("o_ready", "oT_sums", "oT_ready", "out_sums")]
            S.gu_sums, S.tanh_ready, S.h_ready, S.down_sums = [
                signal(n) for n in ("gu_sums", "tanh_ready", "h_ready", "down_sums")]
            S.acc_done, S.f1_sums, S.gelu_ready, S.f2_sums = [
                signal(n) for n in ("acc_done", "f1_sums", "gelu_ready", "f2_sums")]
            S.logit_sums, S.logits_ready, S.exp_ready, S.mask_ready = [
                signal(n) for n in ("logit_sums", "logits_ready", "exp_ready", "mask_ready")]
            S.pos_sums, S.slots_ready, S.gate_ready, S.gateT_sums = [
                signal(n) for n in ("pos_sums", "slots_ready", "gate_ready", "gateT_sums")]
            S.gateT_ready, S.pair_sums, S.pair_done, S.x_ready = [
                signal(n) for n in ("gateT_ready", "pair_sums", "pair_done", "x_ready")]
            S.loaded, S.stored = signal("loaded", 16), signal("stored", 16)
            S.A, S.B, S.O, S.T = [banks[4 * s + n] for n in range(4)]
            f = lambda n, shape, dt=F32: sb(f"{n}_{s}", shape, dt)
            S.x, S.xn, S.x1, S.xo = f("x", [TQ, DM]), f("xn", [TQ, DM]), f("x1", [TQ, DM]), f("xo", [TQ, DM])
            S.xnT, S.ynT = f("xnT", [128, 2, TQ]), f("ynT", [128, 2, TQ])
            S.oc = f("oc", [128, 512])
            S.ctx = S.oc[0:KP, 0:KJ * DC].rearrange("p (j d) -> p j d", j=KJ)
            S.o = S.oc[0:TQ, :]
            S.ctxT, S.yT = f("ctxT", [128, TK]), f("yT", [128, TK])
            S.kv = f("kv", [128, 4 * TK + KJ * 512])
            S.K = S.kv[:, 0:4 * TK].rearrange("p (c k) -> p c k", c=4)
            S.V = S.kv[:, 4 * TK:].rearrange("p (j n) -> p j n", j=KJ)
            S.hT = S.kv[:, 0:8 * TQ].rearrange("p (c t) -> p c t", c=8)
            S.th = S.kv[:, 8 * TQ:12 * TQ].rearrange("p (c t) -> p c t", c=4)
            S.a = S.kv[:, 12 * TQ:14 * TQ].rearrange("p (c t) -> p c t", c=2)
            S.y8 = S.kv[0:TQ, 0:TOP1 * DM].rearrange("p (k d) -> p k d", k=TOP1)
            S.Q = f("Q", [128, 4, TQ])
            S.P = f("P", [128, 2, TK])
            S.z = S.P[0:KP, :, :].rearrange("p a b -> p (a b)")[:, 0:KJ * DC].rearrange("p (j d) -> p j d", j=KJ)
            S.PT = f("PT", [128, 2, KJ, TQ])
            S.oT = f("oT", [128, 4, TQ])
            S.st, S.mv, S.hv = f("st", [128, 6]), f("mv", [128, KJ, 2]), f("hv", [128, KJ])
            S.rstd, S.nt = f("rstd", [128, KJ]), f("nt", [128, KJ])
            S.nmax, S.rs, S.rinv = f("nmax", [TQ, NH]), f("rs", [TQ, NH]), f("rinv", [TQ, NH])
            S.r = [f(f"r{n}", [TQ, E1]) for n in range(4)]
            S.g8 = f("g8", [TQ, 8])
            S.i8 = f("i8", [TQ, 8], U32)
            S.slotf, S.idf, S.w8 = f("slotf", [TQ, 8]), f("idf", [TQ, 8]), f("w8", [TQ, 8])
            S.scat, S.slot = f("scat", [TQ, 8], U32), f("slotu", [TQ, 8], U32)
            S.tok = f("tok", [TQ, 1], U32)
            S.sc = f("sc", [TQ, 8])
            S.gT = f("gT", [E2, TQ])

        def K_self(S):
            return S.kv[:, 0:4 * TQ].rearrange("p (c t) -> p c t", c=4)
        vstep = Signal(sem("vector_step"))
        sstep = Signal(sem("scalar_step"))
        arrived = Signal(sem("arrived"))
        loop_sems += [vstep, sstep, arrived]
        lo, hi = min(g.sem.num for g in loop_sems), max(g.sem.num for g in loop_sems)
        assert hi - lo + 1 == len(loop_sems)
        go = {e.engine: sem(f"go{n}") for n, e in enumerate((nc.sync, nc.tensor, nc.vector, nc.scalar))}
        const_in, vconst, ztab_in = sem("const_in"), sem("vconst"), sem("ztab_in")
        w_in = {n: sem(f"w_in_{n}") for n in ("attn0", "ffn0", "attn1", "attn2", "route1")}
        wc_in, wi_in, w3_ready = sem("wc_in"), sem("wi_in"), sem("w3_ready")
        for S in slots:
            S.scattered, S.gathered = sem(f"scattered_{S.s}"), sem(f"gathered_{S.s}")
        rtemp_ready = sem("rtemp_ready")
        slots_in = sem("slots_in")
        idx_ready = sem("idx_ready")
        ew_in = [sem(f"expert_w_in{r}") for r in range(RING)]
        xg_in = [sem(f"rows_in{r}") for r in range(RING)]
        rows_used = [sem(f"rows_used{r}") for r in range(RING)]
        y_out = [sem(f"y_out{r}") for r in range(RING)]
        eT_sums, eT_ready, egu_sums, etanh, eh_ready, ey_sums, ey_ready, ea_ready = [
            sem(n) for n in ("expert_xT_sums", "expert_xT_ready", "expert_gu_sums", "expert_tanh", "expert_h_ready",
                             "expert_y_sums", "expert_y_ready", "expert_a_ready")]

        def restart():
            for g in loop_sems:
                g.restart()

        def iteration_end(eng):
            eng.drain().then_inc(arrived.sem, 1)
            eng.wait_ge(go[eng.engine], 1)
            eng.sem_clear(go[eng.engine])

        def run_pair(program, *args):
            live = [program(S, *args) for S in slots]
            while live:
                for g in list(live):
                    if next(g, live) is live:
                        live.remove(g)

        block = ctx.enter_context(nc.Block())

        @block.sync
        def _(sp):
            sp.dma_start(cols[:], T["cols"]).then_inc(const_in, 16)
            sp.dma_start(consts[:], T["consts"]).then_inc(const_in, 16)
            restart()
            with sp.Fori(0, NB // 2) as i:
                for S in slots:
                    S.loaded.by(sp.dma_start(S.x[:], x_d[bass.ds(i * 2 * TQ + S.s * TQ, TQ), :]))
                    S.loaded.by(sp.dma_start(S.ctx, ctx_d[bass.ds(i * 2 + S.s, 1)].rearrange("o p j d -> (o p) j d")))
                    S.loaded.by(sp.dma_start(S.tok[:], T["tokens"][bass.ds(i * 2 * TQ + S.s * TQ, TQ), :]))
                for S in slots:
                    rows = bass.ds(i * 2 * TQ + S.s * TQ, TQ)
                    S.slots_ready.wait(sp)
                    S.stored.by(sp.dma_start(xn1_d[rows, :], S.xn[:]))
                    S.stored.by(sp.dma_start(slot_d[rows, :], S.slot[:]))
                    S.stored.by(sp.dma_start(gate_d[rows, :], S.w8[:]))
                for S in slots:
                    rows = bass.ds(i * 2 * TQ + S.s * TQ, TQ)
                    S.x_ready.wait(sp)
                    sp.wait_ge(S.scattered, i * 16 * TOP1 + 16 * TOP1)
                    S.stored.by(sp.dma_start(xmid_d[rows, :], S.x[:]))
                for S in slots:
                    S.stored.wait(sp, 4)
                iteration_end(sp)
            def expert_weights(r, e):
                one = not isinstance(e, int)
                for dst, src in ((ewg[r], T["eg"]), (ewd[r], T["ed"])):
                    src = src[bass.ds(e, 1)].rearrange("o p n -> (o p) n") if one else src[e]
                    sp.dma_start(dst.rearrange("p c n -> p (c n)"), src).then_inc(ew_in[r], 16)

            def store_y(r, i):
                sp.wait_ge(ey_ready, i * RING + r + 1)
                y3 = y_d.rearrange("(p e) d -> p e d", e=E1)
                e = i * RING + r
                dst = y3[:, e, :] if isinstance(i, int) else y3[:, bass.ds(e, 1), :].rearrange("p o d -> p (o d)")
                sp.dma_start(dst, ey[r]).then_inc(y_out[r], 16)
            for r in range(RING):
                expert_weights(r, r)
            sp.dma_start(W[:, 0:WC_N], T["wc"]).then_inc(wc_in, 16)
            sp.dma_start(W[:, INT0:INT0 + WI_N].bitcast(I32), T["wi"]).then_inc(wi_in, 16)
            sp.dma_start(W[:, RC0:RC0 + RC_N], T["rc"].partition_broadcast(128)).then_inc(wc_in, 16)
            with sp.Fori(0, E1 // RING - 1) as i:
                for r in range(RING):
                    sp.wait_ge(ey_sums, i * RING + r + 1)
                    expert_weights(r, i * RING + RING + r)
                    store_y(r, i)
            for r in range(RING):
                store_y(r, E1 // RING - 1)
            restart()
            with sp.Fori(0, NB // 2) as i:
                for S in slots:
                    rows = bass.ds(i * 2 * TQ + S.s * TQ, TQ)
                    S.loaded.by(sp.dma_start(S.slot[:], slot_d[rows, :]))
                    S.loaded.by(sp.dma_start(S.w8[:], gate_d[rows, :]))
                    S.loaded.by(sp.dma_start(S.x[:], xmid_d[rows, :]))
                    S.loaded.by(sp.dma_start(S.ctx, ctx_d[bass.ds(i * 2 + S.s, 1)].rearrange("o p j d -> (o p) j d")))
                for S in slots:
                    S.x_ready.wait(sp)
                    S.stored.by(sp.dma_start(out_d[bass.ds(i * 2 * TQ + S.s * TQ, TQ), :], S.x[:]))
                for S in slots:
                    S.stored.wait(sp)
                iteration_end(sp)

        @block.gpsimd
        def _(pool):
            def release():
                pool.drain()
                pool.wait_ge(arrived.sem, 4)
                pool.sem_clear(range(lo, hi + 1))
                for g in go.values():
                    pool.sem_inc(g, 1)

            zero = slots[0].P[:, 0, 0:NSLOT // 128].bitcast(U32)
            pool.memset(zero, 0).then_inc(vconst, 1)
            pool.memset(ones[:], 1.0).then_inc(vconst, 1)
            pool.wait_ge(vconst, 1)
            pool.dma_start(token_d.rearrange("(p c) o -> p (c o)", p=128), zero).then_inc(ztab_in, 16)
            pool.wait_ge(ztab_in, 16)
            pool.memset(taken[:], 0.0).then_inc(vconst, 1)
            restart()
            with pool.Fori(0, NB // 2) as i:
                for S in slots:
                    S.loaded.wait(pool, 3)
                    S.slots_ready.wait(pool)
                    for k in range(TOP1):
                        pool.indirect_dma_start(
                            token_d, bass.IndirectOffsetOnAxis(ap=S.scat[:, k:k + 1], axis=0), S.tok[:], None,
                            bounds_check=NSLOT - 1, oob_is_err=False).then_inc(S.scattered, 16)
                release()

            pool.dma_start(expert_tokens, token_d.rearrange("(p e) o -> p (e o)", e=E1)).then_inc(slots_in, 16)
            pool.wait_ge(slots_in, 16)

            def gather(r, at):
                pool.indirect_dma_start(xg[r], None, xn1_d, bass.IndirectOffsetOnAxis(ap=at, axis=0)).then_inc(xg_in[r], 16)
            for r in range(RING):
                gather(r, expert_tokens[:, r:r + 1])
            with pool.Fori(0, E1 // RING - 1) as i:
                for r in range(RING):
                    pool.tensor_copy(xidx[r], W[:, bass.ds(i * RING + (TOK0 + RING + r), 1)].bitcast(U32)).then_inc(idx_ready, 1)
                    pool.wait_ge(idx_ready, 1)
                    pool.sem_clear(idx_ready)
                    pool.wait_ge(rows_used[r], 1)
                    pool.sem_clear(rows_used[r])
                    gather(r, xidx[r])
            for r in range(RING):
                pool.wait_ge(y_out[r], 16 * (E1 // RING + 1))
            restart()
            with pool.Fori(0, NB // 2) as i:
                for S in slots:
                    S.loaded.wait(pool, 4)
                    for k in range(TOP1):
                        pool.indirect_dma_start(
                            S.y8[:, k, :], None, y_d, bass.IndirectOffsetOnAxis(ap=S.slot[:, k:k + 1], axis=0)
                        ).then_inc(S.gathered, 16)
                release()

        @block.tensor
        def _(pe):
            def mm(out, pairs, close=True):
                last = None
                for n, (l, r) in enumerate(pairs):
                    last = nc.tensor.matmul(out, l, r, start=n == 0, stop=n == len(pairs) - 1)
                return last

            def transpose_x(S):
                S.xn_ready.wait(pe)
                for c in range(2):
                    last = nc.tensor.transpose(S.T[:, c * TQ:(c + 1) * TQ], S.xn[:, c * 128:(c + 1) * 128], ident[0:TQ, 0:TQ])
                S.xnT_sums.by(last)

            def transpose_context(S, rows, ready, n):
                ready.wait(pe, n)
                for j in range(KJ):
                    last = nc.tensor.transpose(S.T[:, j * KP:(j + 1) * KP], rows[:, j, :], ident[0:KP, 0:KP])
                S.ctx_sums.by(last)

            def project(S, results):
                for n, make in enumerate(results):
                    done, sums = [(S.proj_v_done, S.proj_v_sums), (S.proj_s_done, S.proj_s_sums)][n % 2]
                    if n >= 4:
                        done.wait(pe)
                    sums.by(make([S.A, S.B, S.O, S.T][n % 4]))
                nv, ns = (len(results) + 1) // 2, len(results) // 2
                S.proj_v_done.wait(pe, min(nv, 2))
                S.proj_s_done.wait(pe, min(ns, 2))

            def attention(S, D, wq, wk, wv, wo, context, keys):
                nc_ = NH * D // 128
                rows = [(0, keys)] if keys == TQ else [(j * KP, KP) for j in range(KJ)]
                cchunks = 1 if wk.shape[1] == NH * D else 2
                wk3 = wk.rearrange("p (c n) -> p c n", c=cchunks)
                wv3 = wv.rearrange("p (c n) -> p c n", c=cchunks)
                wq3 = wq.rearrange("p (c n) -> p c n", c=2)
                con = (lambda c, a, n: context[:, a:a + n]) if cchunks == 1 else (lambda c, a, n: context[:, c, a:a + n])
                S.xnT_ready.wait(pe)

                def q(bank):
                    for m in range(nc_):
                        last = mm(bank[:, m * TQ:(m + 1) * TQ],
                                  [(wq3[:, c, m * 128:(m + 1) * 128], S.xnT[:, c, :]) for c in range(2)])
                    return last

                def k(ms):
                    def make(bank):
                        for n, m in enumerate(ms):
                            last = mm(bank[:, n * keys:(n + 1) * keys],
                                      [(wk3[:, c, m * 128:(m + 1) * 128], con(c, 0, keys)) for c in range(cchunks)])
                        return last
                    return make

                def v(js):
                    def make(bank):
                        for n, j in enumerate(js):
                            a, cnt = rows[j]
                            last = mm(bank[0:cnt, n * NH * D:(n + 1) * NH * D],
                                      [(con(c, a, cnt), wv3[:, c, :]) for c in range(cchunks)])
                        return last
                    return make
                if keys == TQ:
                    project(S, [q, k(range(nc_)), v([0])])
                elif D == 16:
                    project(S, [q, k([0]), v([0, 1]), k([1]), v([2])])
                else:
                    project(S, [q, k([0]), v([0]), k([1]), v([1]), k([2]), v([2]), k([3])])
                yield

                def score(h):
                    c, g, par = (h // 8, (h % 8) // 2, h % 2) if D == 16 else (h // 4, h % 4, 0)
                    lanes = slice(32 * g, 32 * g + 32)
                    bank = [S.A, S.B][h % 2]
                    S.score_sums.by(nc.tensor.matmul(bank[0:TQ, 0:keys], S.Q[lanes, 2 * par + c, :] if D == 16 else S.Q[lanes, c, :],
                                                     S.K[lanes, c, 0:keys] if keys == TK else K_self(S)[lanes, c, :],
                                                     start=True, stop=True))

                def turn(h):
                    S.probs_ready.wait(pe)
                    for j, (a, cnt) in enumerate(rows):
                        last = nc.tensor.transpose(S.T[0:cnt, j * TQ:(j + 1) * TQ], S.P[0:TQ, h % 2, a:a + cnt], ident[0:TQ, 0:TQ])
                    S.probsT_sums.by(last)

                def av(h):
                    S.probsT_ready.wait(pe)
                    last = mm(S.O[0:TQ, h * D:(h + 1) * D],
                              [(S.PT[0:cnt, h % 2, j, :], S.V[0:cnt, j, h * D:(h + 1) * D]) for j, (a, cnt) in enumerate(rows)])
                    if h == NH - 1:
                        S.av_sums.by(last)
                score(0)
                for h in range(NH):
                    if h + 1 < NH:
                        score(h + 1)
                    if h >= 1:
                        av(h - 1)
                    turn(h)
                    yield
                av(NH - 1)
                yield
                S.o_ready.wait(pe)
                for c in range(nc_):
                    last = nc.tensor.transpose(S.T[:, c * TQ:(c + 1) * TQ], S.o[:, c * 128:(c + 1) * 128], ident[0:TQ, 0:TQ])
                S.oT_sums.by(last)
                yield
                S.oT_ready.wait(pe)
                wo3 = wo.rearrange("p (c n) -> p c n", c=nc_)
                S.out_sums.by(mm(S.A[0:TQ, 0:DM], [(S.oT[:, c, :], wo3[:, c, :]) for c in range(nc_)]))
                yield

            def glu(S, groups, M, per_group):
                def gate_up(g):
                    wg, wu, _ = groups[g]
                    bank = [S.A, S.B][g % 2]
                    for n in range(4):
                        wx = (wg, wu)[n // 2]
                        last = mm(bank[0:M, n * TQ:(n + 1) * TQ],
                                  [(wx[:, c, (n % 2) * M:(n % 2 + 1) * M], S.xnT[:, c, :]) for c in range(2)])
                    S.gu_sums.by(last)

                gate_up(0)
                for g in range(len(groups)):
                    if g + 1 < len(groups):
                        gate_up(g + 1)
                    yield
                    S.h_ready.wait(pe)
                    if per_group:
                        if g >= 2:
                            S.acc_done.wait(pe)
                        bank = [S.O, S.T][g % 2]
                        last = mm(bank[0:TQ, 0:DM], [(S.hT[0:M, 2 * (g % 2) + c, :], groups[g][2][0:M, c, :]) for c in range(2)])
                    else:
                        for c in range(2):
                            last = nc.tensor.matmul(S.O[0:TQ, 0:DM], S.hT[0:M, 2 * (g % 2) + c, :], groups[g][2][0:M, c, :],
                                                    start=g == 0 and c == 0, stop=g == len(groups) - 1 and c == 1)
                    S.down_sums.by(last)
                if per_group:
                    S.acc_done.skip(pe, 2)
                yield

            def mlp(S, w1, w2):
                S.xnT_ready.wait(pe)
                w13, w23 = w1.rearrange("p (c n) -> p c n", c=2), w2.rearrange("p (c n) -> p c n", c=8)
                for half in range(2):
                    for n in range(4):
                        m = 4 * half + n
                        last = mm([S.A, S.B][half][:, n * TQ:(n + 1) * TQ],
                                  [(w13[:, c, m * 128:(m + 1) * 128], S.xnT[:, c, :]) for c in range(2)])
                    S.f1_sums.by(last)
                yield
                for half in range(2):
                    S.gelu_ready.wait(pe)
                    for n in range(4):
                        m = 4 * half + n
                        last = nc.tensor.matmul(S.O[0:TQ, 0:DM], S.hT[:, m, :], w23[:, m, :], start=m == 0, stop=m == 7)
                S.f2_sums.by(last)
                yield

            def logits(S, wr, n):
                S.xnT_ready.wait(pe)
                w3_ = wr.rearrange("p (c n) -> p c n", c=2)
                S.logit_sums.by(mm(S.O[0:TQ, 0:n], [(S.xnT[:, c, :], w3_[:, c, :]) for c in range(2)]))

            def pair3(v, a):
                return v.rearrange("p (a b) -> p a b", a=a)

            def phase_a(S):
                pe.wait_ge(const_in, 32)
                transpose_context(S, S.ctx, S.loaded, 3)
                yield
                S.ctxT_ready.wait(pe)
                transpose_context(S, S.z, S.z_ready, 1)
                yield
                S.ctxT_ready.wait(pe)
                transpose_x(S)
                pe.wait_ge(w_in["attn0"], 32)
                yield
                yield from attention(S, 16, w("q0"), w("k0"), w("v0"), w("o0"), S.ctxT[:], TK)
                transpose_x(S)
                yield
                pe.wait_ge(w_in["ffn0"], 16)
                logits(S, w("r0"), E0)
                yield
                yield from glu(S, [tuple(pair3(w(f"e{e}")[:, n * 512:(n + 1) * 512], 2) for n in range(3)) for e in range(E0)],
                               128, True)
                transpose_x(S)
                yield
                pe.wait_ge(w_in["attn1"], 16)
                yield from attention(S, 32, w("q1"), w("k1"), w("v1"), w("o1"), S.ynT[:], TQ)
                transpose_x(S)
                yield
                yield from mlp(S, w("f1"), w("g1"))
                transpose_x(S)
                yield
                pe.wait_ge(w_in["attn2"], 16)
                yield from attention(S, 32, w("q2"), w("k2"), w("v2"), w("o2"), S.yT[:], TK)
                transpose_x(S)
                yield
                yield from mlp(S, w("f2"), w("g2"))
                transpose_x(S)
                yield
                pe.wait_ge(w_in["route1"], 16)
                logits(S, w("r1"), E1)
                s3, d3 = w("s1", 2), w("d1", 2)
                yield
                S.mask_ready.wait(pe)
                S.pos_sums.by(mm(S.T[0:TQ, 0:E1], [(const("before")[0:TQ, 0:TQ], S.r[1][:]), (ones[:], S.r[3][:])]))
                yield from glu(S, [(s3[:, :, 0:F1], s3[:, :, F1:2 * F1], d3)], FH, False)

            pe.wait_ge(vconst, 3)
            restart()
            with pe.Fori(0, NB // 2) as i:
                run_pair(phase_a)
                iteration_end(pe)

            def turn_rows(r, i, n):
                pe.wait_ge(xg_in[r], i * 16 + 16 * n)
                bank = banks[r % 2]
                for c in range(2):
                    last = nc.tensor.transpose(bank[:, c * 128:(c + 1) * 128], xg[r][:, c * 128:(c + 1) * 128], ident)
                last.then_inc(eT_sums, 1)

            def free_rows(r, i):
                pe.wait_ge(eT_ready, i * RING + r + 1)
                nc.tensor.nop().then_inc(rows_used[r], 1)

            def gate_up(r, i, n):
                pe.wait_ge(eT_ready, i * RING + RING * (n - 1) + r + 1)
                pe.wait_ge(ew_in[r], i * 32 + 32 * n)
                bank = banks[2 + r % 2]
                for m in range(4):
                    last = mm(bank[0:FH, m * 128:(m + 1) * 128],
                              [(ewg[r][:, c, m * FH:(m + 1) * FH], eT[r % 2][:, c, :]) for c in range(2)])
                last.then_inc(egu_sums, 1)

            def down(r, i, n):
                pe.wait_ge(eh_ready, i * RING + RING * (n - 1) + r + 1)
                last = mm(banks[4 + r % 2][:, 0:DM], [(eh[r % 2][:, c, :], ewd[r][:, c, :]) for c in range(2)])
                last.then_inc(ey_sums, 1)

            turn_rows(0, 0, 1)
            gate_up(0, 0, 1)
            turn_rows(1, 0, 1)
            with pe.Fori(0, E1 // RING - 1) as i:
                for r in range(RING):
                    gate_up((r + 1) % RING, i, 1 + (r + 1) // RING)
                    turn_rows((r + 2) % RING, i, 1 + (r + 2) // RING)
                    down(r, i, 1)
                    free_rows(r, i)
            for r in range(RING):
                if r + 1 < RING:
                    gate_up(r + 1, E1 // RING - 1, 1)
                if r + 2 < RING:
                    turn_rows(r + 2, E1 // RING - 1, 1)
                down(r, E1 // RING - 1, 1)

            def experts2(S):
                for e in range(E2 // 2):
                    if e == 3:
                        S.gateT_ready.wait(pe)
                    if e >= 4:
                        S.pair_done.wait(pe)
                    p3 = wc(f"p{e}", 2)
                    S.pair_sums.by(mm([S.B, S.O, S.A, S.T][e % 4][0:TQ, :], [(S.xnT[:, c, :], p3[:, c, :]) for c in range(2)]))
                    yield
                S.pair_done.wait(pe, 4)
                ws = wc("ws", 4)
                S.pair_sums.by(mm(S.B[0:TQ, 0:DM], [(S.xnT[:, c % 2, :], ws[:, c, :]) for c in range(4)]))
                S.pair_sums.by(mm(S.O[0:TQ, 0:DM], [(S.gT[:], wc("br")[0:E2, :])]))
                S.pair_done.wait(pe, 2)
                yield

            def attention_one(S):
                S.xnT_ready.wait(pe)
                wq, wk, wv = wc("q4", 2), wc("k4"), wc("v4")

                def q(bank):
                    for m in range(2):
                        last = mm(bank[:, m * TQ:(m + 1) * TQ],
                                  [(wq[:, c, m * 128:(m + 1) * 128], S.xnT[:, c, :]) for c in range(2)])
                    return last
                k = lambda m: lambda bank: mm(bank[:, 0:TK], [(wk[:, m * 128:(m + 1) * 128], S.ctxT[:])])

                def v(js):
                    def make(bank):
                        for n, j in enumerate(js):
                            last = mm(bank[0:KP, n * DM:(n + 1) * DM], [(S.ctxT[:, j * KP:(j + 1) * KP], wv)])
                        return last
                    return make
                project(S, [q, k(0), v([0, 1]), k(1), v([2])])
                S.score_sums.by(mm(S.A[0:TQ, 0:TK], [(S.Q[:, c, :], S.K[:, c, :]) for c in range(2)]))
                yield
                S.probs_ready.wait(pe)
                for j in range(KJ):
                    last = nc.tensor.transpose(S.T[0:KP, j * TQ:(j + 1) * TQ], S.P[0:TQ, 0, j * KP:(j + 1) * KP], ident[0:TQ, 0:TQ])
                S.probsT_sums.by(last)
                yield
                S.probsT_ready.wait(pe)
                S.av_sums.by(mm(S.O[0:TQ, 0:DM], [(S.PT[0:KP, 0, j, :], S.V[0:KP, j, 0:DM]) for j in range(KJ)]))
                yield

            def phase_c(S):
                transpose_context(S, S.ctx, S.loaded, 4)
                yield
                S.ctxT_ready.wait(pe)
                transpose_x(S)
                yield
                yield from attention(S, 16, wc("q3"), wc("k3"), wc("v3"), wc("o3"), S.ctxT[:], TK)
                transpose_x(S)
                yield
                logits(S, wc("c2"), E2)
                yield
                S.gate_ready.wait(pe)
                S.gateT_sums.by(nc.tensor.transpose(S.T[0:E2, 0:TQ], S.r[3][:, 0:E2], ident[0:TQ, 0:TQ]))
                yield from experts2(S)
                transpose_x(S)
                yield
                yield from attention_one(S)
                transpose_x(S)
                yield
                pe.wait_ge(w3_ready, 1)
                S.xnT_ready.wait(pe)
                g3, u3 = w3[0].rearrange("p (c n) -> p c n", c=2), w3[1].rearrange("p (c n) -> p c n", c=2)
                d3 = w3[2].rearrange("p (c n) -> p c n", c=6)
                yield from glu(S, [(g3[:, :, 256 * g:256 * g + 256], u3[:, :, 256 * g:256 * g + 256], d3[:, 2 * g:2 * g + 2, :])
                                   for g in range(3)], 128, False)

            pe.wait_ge(wc_in, 32)
            restart()
            with pe.Fori(0, NB // 2) as i:
                run_pair(phase_c)
                iteration_end(pe)

        @block.scalar
        def _(act):
            def load(name, a, b):
                act.dma_start(W[:, a:b], T["wa"][:, a:b]).then_inc(w_in[name], 16)
            load("attn0", 0, WA["r0"][0])
            act.dma_start(W[:, WA_N:WA_N + RA_N], T["ra"].partition_broadcast(128)).then_inc(w_in["attn0"], 16)
            load("ffn0", WA["r0"][0], WA["q1"][0])
            load("attn1", WA["q1"][0], WA["q2"][0])
            load("attn2", WA["q2"][0], WA["r1"][0])
            load("route1", WA["r1"][0], WA_N)

            def keys(S, nk, out, bias):
                S.proj_s_sums.wait(act)
                bank = [S.B, S.T][nk % 2]
                if bias is None:
                    S.proj_s_done.by(nc.scalar.activation(out, bank[:, 0:TK], ACT.Copy))
                else:
                    S.proj_s_done.by(nc.scalar.activation(out, bank[:, 0:TK], ACT.Identity, bias=bias))

            def softmax(S, heads, nkeys):
                for h in range(heads):
                    S.nmax_ready.wait(act)
                    S.probs_ready.by(nc.scalar.activation(
                        S.P[0:TQ, h % 2, 0:nkeys], [S.A, S.B][h % 2][0:TQ, 0:nkeys], ACT.Exp,
                        bias=S.nmax[:, h:h + 1], accum_out=S.rs[:, h:h + 1]))
                    yield

            def tanh(S, groups, M):
                for g in range(groups):
                    S.gu_sums.wait(act)
                    bank = [S.A, S.B][g % 2]
                    S.tanh_ready.by(nc.scalar.activation(S.th[0:M, 2 * (g % 2):2 * (g % 2) + 2, :],
                                                         bank[0:M, 0:2 * TQ].rearrange("p (c t) -> p c t", c=2), ACT.Tanh, scale=0.5))
                    yield

            def gelu(S, bias):
                for half in range(2):
                    S.f1_sums.wait(act)
                    for n in range(4):
                        m = 4 * half + n
                        last = nc.scalar.activation(S.hT[:, m, :], [S.A, S.B][half][:, n * TQ:(n + 1) * TQ], ACT.Gelu,
                                                    bias=col(bias, m))
                    S.gelu_ready.by(last)
                yield

            def phase_a(S):
                act.wait_ge(const_in, 32)
                for m in range(2):
                    keys(S, m, S.K[:, m, :], col("bk0", m))
                yield
                yield from softmax(S, NH, TK)
                S.logits_ready.wait(act)
                S.exp_ready.by(nc.scalar.activation(S.r[1][:, 0:E0], S.r[0][:, 0:E0], ACT.Tanh, scale=0.5))
                yield
                S.logits_ready.wait(act)
                nc.scalar.activation(S.r[2][:, 0:E0], S.r[0][:, 0:E0], ACT.Exp, scale=-1.0 / 0.1)
                S.exp_ready.by(nc.scalar.activation(S.r[3][:, 0:E0], S.r[0][:, 0:E0], ACT.Exp, scale=-1.0 / 0.3))
                yield
                yield from tanh(S, E0, 128)
                S.proj_s_sums.wait(act)
                S.proj_s_done.by(nc.scalar.activation(K_self(S), S.B[:, 0:4 * TQ].rearrange("p (c t) -> p c t", c=4), ACT.Copy))
                yield
                yield from softmax(S, NH, TQ)
                yield from gelu(S, "f1b")
                for m in range(4):
                    keys(S, m, S.K[:, m, :], None)
                yield
                yield from softmax(S, NH, TK)
                yield from gelu(S, "f2b")
                S.logits_ready.wait(act)
                S.exp_ready.by(nc.scalar.activation(S.r[0][:], S.O[0:TQ, 0:E1], ACT.Exp, bias=S.sc[:, 0:1], accum_out=S.sc[:, 1:2]))
                yield
                yield from tanh(S, 1, FH)

            restart()
            with act.Fori(0, NB // 2) as i:
                run_pair(phase_a)
                iteration_end(act)

            def expert(r, i):
                act.wait_ge(egu_sums, i * RING + r + 1)
                nc.scalar.activation(eth[r % 2], banks[2 + r % 2][0:FH, 0:256].rearrange("p (c t) -> p c t", c=2),
                                     ACT.Tanh, scale=0.5).then_inc(etanh, 1)

            def output(r, i):
                act.wait_ge(ey_sums, i * RING + r + 1)
                act.wait_ge(y_out[r], i * 16 + 16)
                nc.scalar.activation(ey[r], banks[4 + r % 2][:, 0:DM], ACT.Copy).then_inc(ey_ready, 1)

            for r in range(RING):
                act.sem_inc(y_out[r], 16)
            expert(0, 0)
            with act.Fori(0, E1 // RING - 1) as i:
                for r in range(RING):
                    if r + 1 < RING:
                        expert(r + 1, i)
                    else:
                        expert(0, i + 1)
                    output(r, i)
            for r in range(RING):
                if r + 1 < RING:
                    expert(r + 1, E1 // RING - 1)
                output(r, E1 // RING - 1)
            def phase_c(S):
                for m in range(2):
                    keys(S, m, S.K[:, m, :], None)
                yield
                yield from softmax(S, NH, TK)
                S.logits_ready.wait(act)
                S.exp_ready.by(nc.scalar.activation(S.r[0][:, 0:E2], S.r[1][:, 0:E2], ACT.Exp, bias=S.sc[:, 0:1], accum_out=S.sc[:, 1:2]))
                yield
                for m in range(2):
                    keys(S, m, S.K[:, m, :], col("bk4", m))
                yield
                yield from softmax(S, 1, TK)
                yield from tanh(S, 3, 128)

            restart()
            with act.Fori(0, NB // 2) as i:
                run_pair(phase_c)
                iteration_end(act)

        @block.vector
        def _(v):
            def then(ins):
                vstep.by(ins)
                vstep.wait(v)

            def inverse_std(S, p, n):
                var, hv, y, t = S.mv[0:p, 0:n, 1], S.hv[0:p, 0:n], S.rstd[0:p, 0:n], S.nt[0:p, 0:n]
                then(v.tensor_scalar(hv, var, EPS, 0.5, ALU.add, ALU.mult))
                then(v.tensor_scalar(y.bitcast(I32), hv.bitcast(I32), -0.5, MAGIC, ALU.mult, ALU.add))
                for _ in range(3):
                    if n == 1:
                        then(v.scalar_tensor_tensor(t, y, hv, y, ALU.mult, ALU.mult))
                    else:
                        then(v.tensor_tensor(t, y, y, ALU.mult))
                        then(v.tensor_tensor(t, t, hv, ALU.mult))
                    then(v.scalar_tensor_tensor(y, t, 1.5, y, ALU.subtract, ALU.mult))

            def normalise(S, src, dst):
                then(v.bn_stats(S.st[0:TQ, :], src))
                then(v.bn_aggr(S.mv[0:TQ, 0, :], S.st[0:TQ, :]))
                inverse_std(S, TQ, 1)
                return v.tensor_scalar(dst, src, S.mv[0:TQ, 0, 0:1], S.rstd[0:TQ, 0:1], ALU.subtract, ALU.mult)

            def norm_turn(S, src, affine=()):
                S.xn_ready.by(normalise(S, src, S.xn[:]))
                yield
                S.xnT_sums.wait(v)
                if not affine:
                    last = v.tensor_copy(S.xnT[:], S.T[:, 0:2 * TQ].rearrange("p (c t) -> p c t", c=2))
                for dst, g, b in affine:
                    for c in range(2):
                        last = v.tensor_scalar(dst[:, c, :], S.T[:, c * TQ:(c + 1) * TQ], col(g, c), col(b, c), ALU.mult, ALU.add)
                S.xnT_ready.by(last)

            def queries(S, D, bias, scale):
                S.proj_v_sums.wait(v)
                if D == 16:
                    for par, side in enumerate(("even", "odd")):
                        for c in range(2):
                            src, dst = S.A[:, c * TQ:(c + 1) * TQ], S.Q[:, 2 * par + c, :]
                            if bias:
                                last = v.tensor_scalar(dst, src, col(bias, c), col(side), ALU.add, ALU.mult)
                            else:
                                last = v.tensor_scalar(dst, src, col(side), None, ALU.mult)
                elif D == 32:
                    last = v.tensor_scalar(S.Q[:], S.A[:, 0:4 * TQ].rearrange("p (c t) -> p c t", c=4), scale, None, ALU.mult)
                else:
                    for c in range(2):
                        last = v.tensor_scalar(S.Q[:, c, :], S.A[:, c * TQ:(c + 1) * TQ], col(bias, c), None, ALU.add)
                S.proj_v_done.by(last)

            def values(S, js, width, bank, p, bias=None):
                S.proj_v_sums.wait(v)
                src = bank[0:p, 0:len(js) * width].rearrange("p (j n) -> p j n", j=len(js))
                dst = S.V[0:p, js[0]:js[-1] + 1, 0:width]
                if bias is None:
                    last = v.tensor_copy(dst, src)
                else:
                    for n in range(len(js)):
                        last = v.tensor_tensor(dst[:, n, :], src[:, n, :], bias, ALU.add)
                S.proj_v_done.by(last)

            def heads(S, D, nkeys, nheads=NH):
                rows = [(0, nkeys)] if nkeys == TQ else [(j * KP, KP) for j in range(KJ)]
                p = rows[0][1]

                def nmax(h):
                    S.score_sums.wait(v)
                    S.nmax_ready.by(v.tensor_reduce(S.nmax[:, h:h + 1], [S.A, S.B][h % 2][0:TQ, 0:nkeys], AX_X, ALU.max, negate=True))

                def turned(h):
                    S.probsT_sums.wait(v)
                    if nkeys == TQ:
                        last = v.tensor_tensor(S.PT[0:TQ, h % 2, 0, :], S.T[0:TQ, 0:TQ], const("after")[0:TQ, 0:TQ], ALU.mult)
                    else:
                        last = v.tensor_copy(S.PT[0:p, h % 2, :, :], S.T[0:p, 0:KJ * TQ].rearrange("p (j t) -> p j t", j=KJ))
                    S.probsT_ready.by(last)
                nmax(0)
                for h in range(nheads):
                    if h + 1 < nheads:
                        nmax(h + 1)
                    yield
                    turned(h)
                S.av_sums.wait(v)
                then(v.reciprocal(S.rinv[:, 0:nheads], S.rs[:, 0:nheads]))

            def attention_end(S, D):
                n = NH * D
                S.o_ready.by(v.tensor_tensor(S.o[:, 0:n].rearrange("p (h d) -> p h d", h=NH),
                                             S.O[0:TQ, 0:n].rearrange("p (h d) -> p h d", h=NH),
                                             S.rinv[:].unsqueeze(2).broadcast_to([TQ, NH, D]), ALU.mult))
                yield
                S.oT_sums.wait(v)
                c = n // 128
                S.oT_ready.by(v.tensor_copy(S.oT[:, 0:c, :], S.T[:, 0:c * TQ].rearrange("p (c t) -> p c t", c=c)))
                yield
                S.out_sums.wait(v)

            def glu(S, groups, M, per_group, weights=None):
                def added(g):
                    S.down_sums.wait(v)
                    if per_group:
                        ins = v.scalar_tensor_tensor(S.x[:], [S.O, S.T][g % 2][0:TQ, 0:DM], weights[:, g:g + 1], S.x[:], ALU.mult, ALU.add)
                        S.acc_done.by(ins)
                        S.acc_done.wait(v)
                    elif g == groups - 1:
                        then(v.tensor_tensor(S.x[:], S.x[:], S.O[0:TQ, 0:DM], ALU.add))
                for g in range(groups):
                    bank = [S.A, S.B][g % 2]
                    gate, up = [bank[0:M, n * 2 * TQ:(n + 1) * 2 * TQ].rearrange("p (c t) -> p c t", c=2) for n in range(2)]
                    S.tanh_ready.wait(v)
                    then(v.scalar_tensor_tensor(S.a[0:M], S.th[0:M, 2 * (g % 2):2 * (g % 2) + 2, :], 1.0, gate, ALU.add, ALU.mult))
                    S.h_ready.by(v.scalar_tensor_tensor(S.hT[0:M, 2 * (g % 2):2 * (g % 2) + 2, :], S.a[0:M], 0.5, up, ALU.mult, ALU.mult))
                    yield
                    if g >= 1:
                        added(g - 1)
                added(groups - 1)

            def top_mask(S, src, n, k, mask):
                v8 = S.g8[:]
                if k < 8:
                    then(v.memset(src[:, n:n + 8], -1.0))
                    then(v.max(v8, src[:, 0:n + 8]))
                    then(v.memset(v8[:, k:8], -1.0))
                    width = n + 8
                else:
                    then(v.max(v8, src))
                    width = n
                then(v.match_replace(mask[:, 0:width], v8, src[:, 0:width], -2.0))
                then(v.tensor_scalar(mask[:, 0:n], mask[:, 0:n], -2.0, None, ALU.is_equal))

            def reduce(out, src):
                then(v.tensor_reduce(out, src, AX_X, ALU.add))

            def route0(S):
                r0, r1, r2, r3 = [t[:, 0:E0] for t in S.r]
                c = lambda n: S.sc[:, n:n + 1]
                S.logit_sums.wait(v)
                S.logits_ready.by(v.tensor_scalar(r0, S.O[0:TQ, 0:E0], rtemp[:], None, ALU.mult))
                yield
                S.exp_ready.wait(v)
                then(v.tensor_scalar(r1, r1, 0.5, 0.5, ALU.mult, ALU.add))
                then(v.tensor_scalar(r2, r1, CENTER, None, ALU.subtract))
                S.logits_ready.by(v.scalar_tensor_tensor(r0, r2, -1.0, r2, ALU.mult, ALU.max))
                then(v.tensor_scalar(S.idf[:], r1, LOWER, None, ALU.is_ge))
                then(v.scalar_tensor_tensor(S.idf[:], r1, UPPER, S.idf[:], ALU.is_le, ALU.mult))
                yield
                S.exp_ready.wait(v)
                then(v.tensor_tensor(S.w8[:], r2, S.idf[:], ALU.mult))
                reduce(c(0), S.w8[:])
                then(v.tensor_scalar(c(0), c(0), 1e-8, None, ALU.is_lt))
                top_mask(S, S.r[3][:], E0, 2, S.r[1][:])
                then(v.tensor_tensor(r3, r3, r1, ALU.mult))
                reduce(c(1), r3)
                then(v.tensor_scalar(c(1), c(1), 1e-8, None, ALU.max))
                then(v.reciprocal(c(1), c(1)))
                then(v.tensor_scalar(r3, r3, c(1), None, ALU.mult))
                then(v.tensor_tensor(r3, r3, S.w8[:], ALU.subtract))
                then(v.scalar_tensor_tensor(S.w8[:], r3, c(0), S.w8[:], ALU.mult, ALU.add))
                reduce(c(2), S.w8[:])
                then(v.tensor_scalar(c(2), c(2), 1e-8, None, ALU.max))
                then(v.reciprocal(c(2), c(2)))
                then(v.tensor_scalar(S.w8[:], S.w8[:], c(2), None, ALU.mult))

            def route1(S):
                S.logit_sums.wait(v)
                S.logits_ready.by(v.tensor_reduce(S.sc[:, 0:1], S.O[0:TQ, 0:E1], AX_X, ALU.max, negate=True))
                yield
                S.exp_ready.wait(v)
                then(v.reciprocal(S.sc[:, 2:3], S.sc[:, 1:2]))
                then(v.tensor_scalar(S.r[0][:], S.r[0][:], S.sc[:, 2:3], None, ALU.mult))
                then(v.max(S.g8[:], S.r[0][:]))
                then(v.max_index(S.i8[:], S.g8[:], S.r[0][:]))
                then(v.match_replace(S.r[1][:], S.g8[:], S.r[0][:], -2.0))
                then(v.tensor_scalar(S.r[1][:], S.r[1][:], -2.0, None, ALU.is_equal))
                then(v.tensor_copy(S.r[3][:], taken[:]))
                ins = v.tensor_tensor(taken[:], taken[:], S.r[1][:], ALU.add)
                S.mask_ready.by(ins)
                S.mask_ready.wait(v)
                reduce(S.sc[:, 3:4], S.g8[:])
                then(v.reciprocal(S.sc[:, 3:4], S.sc[:, 3:4]))
                then(v.tensor_scalar(S.w8[:], S.g8[:], S.sc[:, 3:4], None, ALU.mult))
                then(v.tensor_copy(S.idf[:], S.i8[:]))
                yield
                S.pos_sums.wait(v)
                then(v.tensor_scalar(S.r[0][:], S.T[0:TQ, 0:E1], float(CAP), DROPPED, ALU.is_ge, ALU.mult))
                then(v.scalar_tensor_tensor(S.r[2][:], S.T[0:TQ, 0:E1], float(E1), S.r[0][:], ALU.mult, ALU.add))
                then(v.tensor_tensor(S.r[2][:], S.r[2][:], const("iota")[0:TQ, :], ALU.add))
                for k in range(TOP1):
                    then(v.scalar_tensor_tensor(S.r[0][:], const("iota")[0:TQ, :], S.idf[:, k:k + 1], S.r[2][:],
                                                ALU.is_equal, ALU.mult, accum_out=S.slotf[:, k:k + 1]))
                then(v.tensor_copy(S.scat[:], S.slotf[:]))
                then(v.tensor_scalar(S.idf[:], S.slotf[:], float(NSLOT), None, ALU.is_lt))
                then(v.tensor_tensor(S.w8[:], S.w8[:], S.idf[:], ALU.mult))
                then(v.tensor_tensor(S.slotf[:], S.slotf[:], S.idf[:], ALU.mult))
                S.slots_ready.by(v.tensor_copy(S.slot[:], S.slotf[:]))

            def add_row(S, dst, bank, name, base):
                then(v.tensor_tensor(dst, bank[0:TQ, 0:DM], base, ALU.add))
                if name:
                    then(v.tensor_tensor(dst, dst, row(name), ALU.add))

            def phase_a(S):
                v.wait_ge(const_in, 32)
                S.loaded.wait(v, 3)
                for j in range(KJ):
                    then(v.bn_stats(S.st[0:KP, :], S.ctx[:, j, :]))
                    then(v.bn_aggr(S.mv[0:KP, j, :], S.st[0:KP, :]))
                inverse_std(S, KP, KJ)
                for j in range(KJ):
                    ins = v.tensor_scalar(S.z[:, j, :], S.ctx[:, j, :], S.mv[0:KP, j, 0:1], S.rstd[0:KP, j:j + 1],
                                           ALU.subtract, ALU.mult)
                S.z_ready.by(ins)
                S.ctx_sums.wait(v)
                ins = v.tensor_copy(S.ctxT[:], S.T[:, 0:TK])
                S.ctxT_ready.by(ins)
                S.ctxT_ready.wait(v)
                yield
                S.ctx_sums.wait(v)
                ins = v.tensor_scalar(S.yT[:], S.T[:, 0:TK], col("y2g"), col("y2b"), ALU.mult, ALU.add)
                S.ctxT_ready.by(ins)
                S.ctxT_ready.wait(v)
                yield from norm_turn(S, S.x[:])
                v.wait_ge(w_in["attn0"], 32)
                yield
                queries(S, 16, "bq0", 0.25)
                values(S, [0, 1], DM, S.O, KP, row("bv0", KP))
                values(S, [2], DM, S.A, KP, row("bv0", KP))
                yield
                yield from heads(S, 16, TK)
                yield from attention_end(S, 16)
                add_row(S, S.x[:], S.A, "bo0", S.x[:])
                yield from norm_turn(S, S.x[:])
                yield
                yield from route0(S)
                yield
                yield from glu(S, E0, 128, True, S.w8)
                then(normalise(S, S.x[:], S.xo[:]))
                then(normalise(S, S.xo[:], S.x1[:]))
                then(v.tensor_tensor(S.x1[:], S.x1[:], row("ln1g"), ALU.mult))
                then(v.tensor_tensor(S.x1[:], S.x1[:], row("ln1b"), ALU.add))
                yield from norm_turn(S, S.x1[:], [(S.xnT, "x1g", "x1b"), (S.ynT, "y1g", "y1b")])
                yield
                queries(S, 32, None, 32.0 ** -0.5)
                values(S, [0], 512, S.O, TQ)
                yield
                yield from heads(S, 32, TQ)
                yield from attention_end(S, 32)
                add_row(S, S.xo[:], S.A, "o1b", S.x1[:])
                yield from norm_turn(S, S.xo[:], [(S.xnT, "n1g", "n1b")])
                yield
                S.f2_sums.wait(v)
                add_row(S, S.xo[:], S.O, "g1b", S.xo[:])
                then(v.tensor_tensor(S.xo[:], S.xo[:], S.x1[:], ALU.add))
                then(normalise(S, S.xo[:], S.x1[:]))
                then(v.tensor_tensor(S.x1[:], S.x1[:], row("ln2g"), ALU.mult))
                then(v.tensor_tensor(S.x1[:], S.x1[:], row("ln2b"), ALU.add))
                yield from norm_turn(S, S.x1[:], [(S.xnT, "x2g", "x2b")])
                yield
                queries(S, 32, None, 32.0 ** -0.5)
                for j in range(KJ):
                    values(S, [j], 512, [S.O, S.A][j % 2], KP)
                yield
                yield from heads(S, 32, TK)
                yield from attention_end(S, 32)
                add_row(S, S.xo[:], S.A, "o2b", S.x1[:])
                yield from norm_turn(S, S.xo[:], [(S.xnT, "n2g", "n2b")])
                yield
                S.f2_sums.wait(v)
                add_row(S, S.xo[:], S.O, "g2b", S.xo[:])
                then(v.tensor_tensor(S.xo[:], S.xo[:], S.x1[:], ALU.add))
                then(v.tensor_tensor(S.x[:], S.x[:], S.xo[:], ALU.add))
                yield from norm_turn(S, S.x[:])
                yield
                yield from route1(S)
                yield from glu(S, 1, FH, False)
                S.x_ready.by(v.tensor_copy(S.sc[:, 0:1], S.x[:, 0:1]))

            v.wait_ge(const_in, 32)
            v.wait_ge(vconst, 3)
            v.reciprocal(rtemp[:], col("temp", p=TQ)).then_inc(rtemp_ready, 1)
            v.wait_ge(rtemp_ready, 1)
            restart()
            with v.Fori(0, NB // 2) as i:
                run_pair(phase_a)
                iteration_end(v)

            def rows(r, i, n):
                v.wait_ge(eT_sums, i * RING + RING * (n - 1) + r + 1)
                v.tensor_copy(eT[r % 2], banks[r % 2][:, 0:256].rearrange("p (c t) -> p c t", c=2)).then_inc(eT_ready, 1)

            def hidden(r, i):
                gate, up = [banks[2 + r % 2][0:FH, n * 256:(n + 1) * 256].rearrange("p (c t) -> p c t", c=2) for n in range(2)]
                v.wait_ge(etanh, i * RING + r + 1)
                v.scalar_tensor_tensor(ea[r % 2], eth[r % 2], 1.0, gate, ALU.add, ALU.mult).then_inc(ea_ready, 1)
                v.wait_ge(ea_ready, i * RING + r + 1)
                v.scalar_tensor_tensor(eh[r % 2], ea[r % 2], 0.5, up, ALU.mult, ALU.mult).then_inc(eh_ready, 1)

            rows(0, 0, 1)
            rows(1, 0, 1)
            with v.Fori(0, E1 // RING - 1) as i:
                for r in range(RING):
                    hidden(r, i)
                    rows((r + 2) % RING, i, 1 + (r + 2) // RING)
            for r in range(RING):
                hidden(r, E1 // RING - 1)
                if r + 2 < RING:
                    rows(r + 2, E1 // RING - 1, 1)
            v.wait_ge(wi_in, 16)
            v.tensor_scalar(W[:, FLT0:FLT0 + WI_N], W[:, INT0:INT0 + WI_N].bitcast(I32), 1.0 / 127.0, None,
                            ALU.mult).then_inc(w3_ready, 1)

            def route2(S):
                r0, r1, r3 = S.r[0], S.r[1], S.r[3]
                S.logit_sums.wait(v)
                then(v.tensor_tensor(r1[:, 0:E2], S.O[0:TQ, 0:E2], row("ebias", TQ, RC, RC0)[:, 0:E2], ALU.add))
                S.logits_ready.by(v.tensor_reduce(S.sc[:, 0:1], r1[:, 0:E2], AX_X, ALU.max, negate=True))
                yield
                S.exp_ready.wait(v)
                then(v.reciprocal(S.sc[:, 2:3], S.sc[:, 1:2]))
                then(v.tensor_scalar(r0[:, 0:E2], r0[:, 0:E2], S.sc[:, 2:3], None, ALU.mult))
                top_mask(S, r0[:], E2, 2, r3[:])
                S.gate_ready.by(v.tensor_tensor(r3[:, 0:E2], r3[:, 0:E2], r0[:, 0:E2], ALU.mult))
                S.gate_ready.wait(v)
                S.gateT_sums.wait(v)
                S.gateT_ready.by(v.tensor_copy(S.gT[:], S.T[0:E2, 0:TQ]))
                then(v.tensor_tensor(S.x[:], S.x[:], S.xn[:], ALU.add))

            def phase_c(S, i):
                S.loaded.wait(v, 4)
                v.wait_ge(S.gathered, i * 16 * TOP1 + 16 * TOP1)
                for k in range(TOP1):
                    then(v.scalar_tensor_tensor(S.x[:], S.y8[:, k, :], S.w8[:, k:k + 1], S.x[:], ALU.mult, ALU.add))
                S.ctx_sums.wait(v)
                S.ctxT_ready.by(v.tensor_copy(S.ctxT[:], S.T[:, 0:TK]))
                yield
                yield from norm_turn(S, S.x[:])
                yield
                queries(S, 16, None, 0.25)
                values(S, [0, 1], DM, S.O, KP)
                values(S, [2], DM, S.A, KP)
                yield
                yield from heads(S, 16, TK)
                yield from attention_end(S, 16)
                add_row(S, S.x[:], S.A, None, S.x[:])
                yield from norm_turn(S, S.x[:])
                yield
                yield from route2(S)
                for e in range(E2):
                    bank = [S.B, S.O, S.A, S.T][(e // 2) % 4]
                    if e % 2 == 0:
                        S.pair_sums.wait(v)
                    ins = v.scalar_tensor_tensor(S.x[:], bank[0:TQ, (e % 2) * DM:(e % 2 + 1) * DM], S.r[3][:, e:e + 1], S.x[:],
                                                 ALU.mult, ALU.add)
                    if e % 2:
                        S.pair_done.by(ins)
                        S.pair_done.wait(v)
                        yield
                    else:
                        then(ins)
                S.pair_sums.wait(v, 2)
                S.pair_done.by(v.scalar_tensor_tensor(S.xo[:], S.B[0:TQ, 0:DM], 1.0, row("bs0", TQ, RC, RC0), ALU.mult, ALU.add))
                S.pair_done.wait(v)
                then(v.tensor_tensor(S.xo[:], S.xo[:], row("bs1", TQ, RC, RC0), ALU.add))
                then(v.scalar_tensor_tensor(S.x[:], S.xo[:], 0.5, S.x[:], ALU.mult, ALU.add))
                S.pair_done.by(v.tensor_tensor(S.x[:], S.x[:], S.O[0:TQ, 0:DM], ALU.add))
                S.pair_done.wait(v)
                yield from norm_turn(S, S.x[:])
                queries(S, DM, "bq4", None)
                values(S, [0, 1], DM, S.O, KP, row("bv4", KP, RC, RC0))
                values(S, [2], DM, S.A, KP, row("bv4", KP, RC, RC0))
                yield from heads(S, DM, TK, 1)
                then(v.scalar_tensor_tensor(S.x[:], S.O[0:TQ, 0:DM], S.rinv[:, 0:1], S.x[:], ALU.mult, ALU.add))
                yield from norm_turn(S, S.x[:])
                yield
                yield from glu(S, 3, 128, False)
                S.x_ready.by(v.tensor_copy(S.sc[:, 0:1], S.x[:, 0:1]))

            v.wait_ge(wc_in, 32)
            restart()
            with v.Fori(0, NB // 2) as i:
                run_pair(phase_c, i)
                iteration_end(v)


def kernel(**inputs):
    import numpy as np
    import concourse.bacc as bacc
    from concourse.bass_utils import run_bass_kernel_spmd as run

    g = {n: np.ascontiguousarray(a) for n, a in inputs.items()}

    def chunks(a, p=128):
        k, n = a.shape
        out = np.zeros((128, (k // p) * n), a.dtype)
        out[0:p] = a.reshape(k // p, p, n).transpose(1, 0, 2).reshape(p, -1)
        return out

    def heads(a):
        return a.transpose(1, 0, 2).reshape(a.shape[1], -1)

    def column(a):
        return a.reshape(-1, 128).T

    def wide(a, n):
        out = np.zeros((a.shape[0], n), a.dtype)
        out[:, 0:a.shape[1]] = a
        return out

    wa = [chunks(g["L0_xattn_Wq"]), g["L0_xattn_Wk"], g["L0_xattn_Wv"], chunks(g["L0_xattn_Wo"]), chunks(g["L0_ffn_Wr"])]
    for e in range(E0):
        wa += [chunks(g[f"L0_ffn_W{n}"][e]) for n in "gud"]
    for a in ("a1", "a2"):
        wa += [chunks(heads(g[f"L1_xattn_{a}_w{n}"])) for n in "qkv"]
        wa += [chunks(g[f"L1_xattn_{a}_li{n}_w"]) for n in (1, 2, 3)]
    wa += [chunks(g["L1_ffn_router_w"].T), chunks(g["L1_ffn_ws_gate_up"]), chunks(g["L1_ffn_ws_down"], FH)]
    wr = g["L2_ffn_Wr"].transpose(0, 2, 1)
    wc = [chunks(g["L2_xattn_Wq"].T), chunks(g["L2_xattn_Wkv"].T[:, 0:DM]), chunks(g["L2_xattn_Wkv"].T[:, DM:]),
          chunks(g["L2_xattn_Wo"].T), chunks(g["L2_ffn_centroids"].T)]
    wc += [chunks(np.concatenate([wr[2 * e], wr[2 * e + 1]], 1)) for e in range(E2 // 2)]
    wc += [chunks(g["L2_ffn_Ws"][n].T) for n in range(2)]
    br = np.zeros((128, DM), np.float32)
    br[0:E2] = g["L2_ffn_br"]
    wc += [br, chunks(g["L3_xattn_Wq"]), g["L3_xattn_Wk"], g["L3_xattn_Wv"]]
    wi = [chunks(g["L3_ffn_w_gate"].T), chunks(g["L3_ffn_w_up"].T), chunks(g["L3_ffn_w_down"].T)]
    L1 = "L1_xattn_"
    ra = [g["L0_xattn_bv"], g["L0_xattn_bo"]] + [g[L1 + n] for n in (
        "ln1_g", "ln1_b", "ln2_g", "ln2_b", "a1_li1_b", "a1_li3_b", "a2_li1_b", "a2_li3_b")]
    rc = [g["L2_ffn_bs"][0], g["L2_ffn_bs"][1], g["L3_xattn_bv"], wide(g["L2_ffn_expert_biases"].reshape(1, -1), DM)[0]]
    even = np.zeros((128, 1), np.float32)
    even.reshape(4, 2, 16)[:, 0] = 0.25
    odd = np.zeros((128, 1), np.float32)
    odd.reshape(4, 2, 16)[:, 1] = 0.25
    cols = [column(g["L0_xattn_bq"]), column(g["L0_xattn_bk"])]
    for a in ("a1", "a2"):
        cols += [column(g[L1 + f"{a}_{n}"]) for n in ("lnx_g", "lnx_b", "lny_g", "lny_b", "ln3_g", "ln3_b", "li2_b")]
    cols += [column(g["L3_xattn_bq"]), column(g["L3_xattn_bk"]), even, odd,
             np.broadcast_to(g["L0_ffn_temperature"].reshape(1, 1), (128, 1))]
    n = np.arange(128)
    consts = [np.eye(128), n[:, None] < n[None, :], n[:, None] > n[None, :], np.tile(np.arange(E1), (128, 1))]
    arrays = {
        "x": g["x"], "ctx": g["ctx_512"],
        "wa": np.concatenate(wa, 1), "wc": np.concatenate(wc, 1), "wi": np.concatenate(wi, 1),
        "ra": np.concatenate(ra), "rc": np.concatenate(rc), "cols": np.concatenate(cols, 1),
        "consts": np.concatenate([c.astype(np.float32) for c in consts], 1),
        "eg": np.concatenate([g["L1_ffn_w_gate"].reshape(E1, 2, 128, F1), g["L1_ffn_w_up"].reshape(E1, 2, 128, F1)], 3)
                .transpose(0, 2, 1, 3).reshape(E1, 128, 4 * F1),
        "ed": g["L1_ffn_w_down"].reshape(E1, 2, FH, DM).transpose(0, 2, 1, 3).reshape(E1, FH, 2 * DM),
        "tokens": np.arange(NT, dtype=np.uint32).reshape(NT, 1),
    }
    arrays = {n: np.ascontiguousarray(a) for n, a in arrays.items()}
    assert arrays["wa"].shape[1] == WA_N and arrays["wc"].shape[1] == WC_N and arrays["cols"].shape[1] == CO_N
    nc = bacc.Bacc("TRN2", target_bir_lowering=False, num_devices=1)
    arrays = {f"in_{n}": a for n, a in arrays.items()}
    tensors = {n[3:]: nc.dram_tensor(n, a.shape, mybir.dt.from_np(a.dtype), kind="ExternalInput").ap() for n, a in arrays.items()}
    tensors["out"] = nc.dram_tensor("out", (NB, TQ, DM), F32, kind="ExternalOutput").ap()
    build(nc, tensors)
    return run(nc, [arrays], core_ids=[0]).results[0]["out"]
```

```python
from contextlib import ExitStack

import concourse.bass as bass
from concourse import mybir

ALU = mybir.AluOpType
ACT = mybir.ActivationFunctionType
F32 = mybir.dt.float32
I32 = mybir.dt.int32
U32 = mybir.dt.uint32
AX_X = mybir.AxisListType.X

NB, TQ, DM = 8, 112, 256
TK, DC, KP = 375, 128, 125
KJ = TK // KP
NT = NB * TQ
NH = 16
E0, E1, E2 = 8, 64, 16
TOP1 = 8
F1 = 192
FH = F1 // 2
CAP = 128
NSLOT = E1 * CAP
DROPPED = float(1 << 20)
RING = 4
EPS = 1e-5
MAGIC = float(0x5f3759df - (1 << 22) - (1 << 31))
CENTER = 0.36787944117144233
LOWER, UPPER = 0.21231792754821915, 0.5


LENGTH = {"ctx": 4, "turn": 1.5, "proj": 7, "head": 2, "av": 1, "out": 5, "logits": 3, "route": 3, "glu": 2.8,
          "end": 5, "f1": 4, "f2": 6, "pair": 1.2, "skip": 0.1}
LAG = 9


def head_order(D):
    return list(range(NH)) if D == 32 else [8 * c + 2 * g + p for c in range(2) for p in range(2) for g in range(4)]


def layout(fields):
    at, out = 0, {}
    for name, n in fields:
        out[name] = (at, n)
        at += n
    return out, at


WA, WA_N = layout([("q0", 512), ("k0", 256), ("v0", 256), ("o0", 512), ("r0", 16)]
                  + [(f"e{e}", 1536) for e in range(E0)]
                  + [("q1", 1024), ("k1", 1024), ("v1", 1024), ("o1", 1024), ("f1", 2048), ("g1", 2048)]
                  + [("q2", 1024), ("k2", 512), ("v2", 512), ("o2", 1024), ("f2", 2048), ("g2", 2048)]
                  + [("r1", 128), ("s1", 768), ("d1", 512)])
WC, WC_N = layout([("q3", 512), ("k3", 256), ("v3", 256), ("o3", 512), ("c2", 32)]
                  + [(f"p{e}", 1024) for e in range(E2 // 2)]
                  + [("ws", 1024), ("br", 256), ("q4", 512), ("k4", 256), ("v4", 256)])
WI_N = 3 * 1536
RING_N = 1280
RA, RA_N = layout([(n, DM) for n in ("bv0", "bo0", "ln1g", "ln1b", "ln2g", "ln2b", "o1b", "g1b", "o2b", "g2b")])
RC, RC_N = layout([(n, DM) for n in ("bs0", "bs1", "bv4")] + [("ebias", DM)])
CO, CO_N = layout([("bq0", 2), ("bk0", 2), ("x1g", 2), ("x1b", 2), ("y1g", 2), ("y1b", 2), ("n1g", 2), ("n1b", 2),
                   ("f1b", 8), ("x2g", 2), ("x2b", 2), ("y2g", 1), ("y2b", 1), ("n2g", 2), ("n2b", 2), ("f2b", 8),
                   ("bq4", 2), ("bk4", 2), ("even", 1), ("odd", 1), ("temp", 1)])
CS, CS_N = layout([("ident", 128), ("before", 128), ("after", 128), ("iota", E1)])


class Signal:

    def __init__(self, sem, step=1):
        self.sem, self.step = sem, step
        self.restart()

    def restart(self):
        self.sent, self.seen = 0, {}

    def by(self, ins):
        self.sent += 1
        ins.then_inc(self.sem, self.step)

    def wait(self, eng, n=1):
        self.skip(eng, n)
        eng.wait_ge(self.sem, self.seen[eng.engine] * self.step)

    def skip(self, eng, n=1):
        self.seen[eng.engine] = self.seen.get(eng.engine, 0) + n



class Slot:
    pass


def build(nc, T):
    x_d = T["x"].rearrange("b t d -> (b t) d")
    ctx_d = T["ctx"].rearrange("b (j p) d -> b p j d", p=KP)
    out_d = T["out"].rearrange("b t d -> (b t) d")

    with ExitStack() as ctx:
        def sb(name, shape, dt=F32):
            return ctx.enter_context(nc.sbuf_tensor(name, shape, dt))

        def sem(name):
            return ctx.enter_context(nc.semaphore(name))

        def dram(name, shape, dt=F32):
            return nc.dram_tensor(name, shape, dt, kind="Internal").ap()

        xmid_d = dram("xmid", [NT + 2 * TQ, DM])
        xn1_d = dram("xn1", [NT, DM])
        token_d = dram("token", [NSLOT, 1], U32)
        y_d = dram("y", [NSLOT, DM])

        W = sb("W", [128, WA_N + RA_N])
        cols = sb("cols", [128, CO_N])
        consts = sb("consts", [128, CS_N])
        taken = sb("taken", [TQ, E1])
        ones = sb("ones", [TQ, TQ])
        rtemp = sb("rtemp", [TQ, 1])
        slot_all = sb("slot_all", [TQ, (NB + 2) * TOP1], U32)
        gate_all = sb("gate_all", [TQ, (NB + 2) * TOP1])

        def w(name, a=None, table=WA):
            at, n = table[name]
            v = W[:, at:at + n]
            return v if a is None else v.rearrange("p (a b) -> p a b", a=a)

        def wc(name, a=None):
            return w(name, a, WC)

        def row(name, p=TQ, table=RA, base=WA_N):
            at, n = table[name]
            return W[0:p, base + at:base + at + n]

        INT0 = WC_N
        FLT0 = INT0 + WI_N
        RC0 = FLT0 + WI_N
        RING0 = RC0 + RC_N
        TOK0 = RING0 + RING * RING_N
        B0 = TOK0 + E1

        def work(n):
            nonlocal B0
            B0 += n
            assert B0 <= WA_N + RA_N
            return W[:, B0 - n:B0]
        ewg = [W[:, RING0 + r * RING_N:RING0 + r * RING_N + 768].rearrange("p (c n) -> p c n", c=2) for r in range(RING)]
        ewd = [W[0:FH, RING0 + r * RING_N + 768:RING0 + (r + 1) * RING_N].rearrange("p (c n) -> p c n", c=2) for r in range(RING)]
        expert_tokens = W[:, TOK0:TOK0 + E1].bitcast(U32)
        xg = [work(DM) for r in range(RING)]
        xidx = [work(1).bitcast(U32) for r in range(RING)]
        ey = [work(DM) for r in range(RING)]
        eT = [work(2 * CAP).rearrange("p (c t) -> p c t", c=2) for r in range(2)]
        eth, eh = [[work(2 * CAP)[0:FH].rearrange("p (c t) -> p c t", c=2) for r in range(2)] for _ in range(2)]
        ea = [work(2 * CAP)[0:FH].rearrange("p (c t) -> p c t", c=2) for r in range(2)]
        w3 = [W[:, FLT0 + 1536 * n:FLT0 + 1536 * (n + 1)] for n in range(3)]

        def col(name, c=0, p=128):
            at = CO[name][0] + c
            return cols[0:p, at:at + 1]

        def const(name):
            at, n = CS[name]
            return consts[:, at:at + n]
        ident = const("ident")

        banks = [ctx.enter_context(nc.psum_tensor(f"bank{n}", [128, 512], F32)) for n in range(8)]

        slots = []
        loop_sems = []
        for s in range(2):
            S = Slot()
            S.s = s
            slots.append(S)

            def signal(name, step=1):
                loop_sems.append(Signal(sem(f"{name}_{s}"), step))
                return loop_sems[-1]
            S.ctx_sums, S.ctxT_ready, S.z_ready, S.xn_ready = [
                signal(n) for n in ("ctx_sums", "ctxT_ready", "z_ready", "xn_ready")]
            S.xnT_sums, S.xnT_ready, S.proj_v_sums, S.proj_v_done = [
                signal(n) for n in ("xnT_sums", "xnT_ready", "proj_v_sums", "proj_v_done")]
            S.proj_s_sums, S.proj_s_done, S.score_sums, S.nmax_ready = [
                signal(n) for n in ("proj_s_sums", "proj_s_done", "score_sums", "nmax_ready")]
            S.probs_ready, S.probsT_sums, S.probsT_ready, S.av_sums = [
                signal(n) for n in ("probs_ready", "probsT_sums", "probsT_ready", "av_sums")]
            S.o_ready, S.oT_sums, S.oT_ready, S.out_sums = [
                signal(n) for n in ("o_ready", "oT_sums", "oT_ready", "out_sums")]
            S.gu_sums, S.tanh_ready, S.h_ready, S.down_sums = [
                signal(n) for n in ("gu_sums", "tanh_ready", "h_ready", "down_sums")]
            S.acc_done, S.f1_sums, S.gelu_ready, S.f2_sums = [
                signal(n) for n in ("acc_done", "f1_sums", "gelu_ready", "f2_sums")]
            S.logit_sums, S.logits_ready, S.exp_ready, S.mask_ready = [
                signal(n) for n in ("logit_sums", "logits_ready", "exp_ready", "mask_ready")]
            S.pos_sums, S.slots_ready, S.gate_ready, S.gateT_sums = [
                signal(n) for n in ("pos_sums", "slots_ready", "gate_ready", "gateT_sums")]
            S.gateT_ready, S.pair_sums, S.pair_done, S.x_ready = [
                signal(n) for n in ("gateT_ready", "pair_sums", "pair_done", "x_ready")]
            S.probsT_s_sums, S.probsT_s_ready = [signal(n) for n in ("probsT_s_sums", "probsT_s_ready")]
            S.xin_free, S.y8_free = [signal(n) for n in ("xin_free", "y8_free")]
            S.noted = signal("noted")
            S.loaded, S.stored, S.tok_in = signal("loaded", 16), signal("stored", 16), signal("tok_in", 16)
            S.A, S.B, S.O, S.T = [banks[4 * s + n] for n in range(4)]
            f = lambda n, shape, dt=F32: sb(f"{n}_{s}", shape, dt)
            S.xin = f("xin", [TQ, DM])
            S.x, S.xn, S.x1, S.xo = f("x", [TQ, DM]), f("xn", [TQ, DM]), f("x1", [TQ, DM]), f("xo", [TQ, DM])
            S.xnT, S.ynT = f("xnT", [128, 2, TQ]), f("ynT", [128, 2, TQ])
            S.oc = f("oc", [128, 512])
            S.ctx = S.oc[0:KP, 0:KJ * DC].rearrange("p (j d) -> p j d", j=KJ)
            S.o = S.oc[0:TQ, :]
            S.yT = f("yT", [128, TK])
            S.kv = f("kv", [128, 4 * TK + KJ * 512])
            S.K = S.kv[:, 0:4 * TK].rearrange("p (c k) -> p c k", c=4)
            S.V = S.kv[:, 4 * TK:].rearrange("p (j n) -> p j n", j=KJ)
            S.hT = S.kv[:, 0:8 * TQ].rearrange("p (c t) -> p c t", c=8)
            S.th = S.kv[:, 8 * TQ:12 * TQ].rearrange("p (c t) -> p c t", c=4)
            S.a = [S.kv[:, n * TQ:(n + 2) * TQ].rearrange("p (c t) -> p c t", c=2) for n in (12, 14)]
            y0 = INT0 + s * TOP1 * DM
            S.y8 = W[0:TQ, y0:y0 + TOP1 * DM].rearrange("p (k d) -> p k d", k=TOP1)
            S.Q = f("Q", [128, 4, 4, TQ])
            S.P = f("P", [128, 2, TK])
            S.z = S.P[0:KP, :, :].rearrange("p a b -> p (a b)")[:, 0:KJ * DC].rearrange("p (j d) -> p j d", j=KJ)
            pt = f("PT", [128, 2 * KJ * TQ])
            S.PT = pt[:].rearrange("p (a j t) -> p a j t", a=2, j=KJ)
            S.ctxT = pt[:, 0:TK]
            S.Q1 = pt[:, TK:TK + 2 * TQ].rearrange("p (c t) -> p c t", c=2)
            S.oT = S.kv[:, 4 * TK + KJ * 512 - 4 * TQ:].rearrange("p (c t) -> p c t", c=4)
            S.st, S.mv, S.hv = f("st", [128, 6]), f("mv", [128, KJ, 2]), f("hv", [128, KJ])
            S.rstd, S.nt = f("rstd", [128, KJ]), f("nt", [128, KJ])
            S.nmax, S.rs, S.rinv = f("nmax", [TQ, NH]), f("rs", [TQ, NH]), f("rinv", [TQ, NH])
            S.r = [f(f"r{n}", [TQ, E1]) for n in range(4)]
            S.g8 = f("g8", [TQ, 8])
            S.i8 = f("i8", [TQ, 8], U32)
            S.slotf, S.idf, S.w8 = f("slotf", [TQ, 8]), f("idf", [TQ, 8]), f("w8", [TQ, 8])
            S.scat, S.slot = f("scat", [TQ, 8], U32), f("slotu", [TQ, 8], U32)
            S.tok = f("tok", [TQ, 1], U32)
            S.myscat = f("myscat", [TQ, 8], U32)
            S.myslot, S.myw = f("myslot", [TQ, 8], U32), f("myw", [TQ, 8])
            S.sc = f("sc", [TQ, 8])
            S.gT = f("gT", [E2, TQ])

        def scalar_turns(keys):
            return lambda h: keys == TK and h % 3 == 2

        def K_self(S):
            return S.kv[:, 0:4 * TQ].rearrange("p (c t) -> p c t", c=4)
        vstep = Signal(sem("vector_step"))
        sstep = Signal(sem("scalar_step"))
        arrived = Signal(sem("arrived"))
        loop_sems += [vstep, sstep, arrived]
        lo, hi = min(g.sem.num for g in loop_sems), max(g.sem.num for g in loop_sems)
        assert hi - lo + 1 == len(loop_sems)
        go = {e.engine: sem(f"go{n}") for n, e in enumerate((nc.sync, nc.tensor, nc.vector, nc.scalar))}
        const_in, vconst = sem("const_in"), sem("vconst")
        first_in, spare_in, notes = sem("first_in"), sem("spare_in"), sem("notes")
        w_in = {n: sem(f"w_in_{n}") for n in ("attn0", "ffn0", "attn1", "attn2", "route1")}
        wc_in, wi_in, w3_ready = sem("wc_in"), sem("wi_in"), sem("w3_ready")
        for S in slots:
            S.scattered, S.gathered = sem(f"scattered_{S.s}"), sem(f"gathered_{S.s}")
        rtemp_ready = sem("rtemp_ready")
        fetch_notes = [sem(f"fetch_notes{n}") for n in range(2)]
        slots_in = sem("slots_in")
        idx_ready = sem("idx_ready")
        ew_in = [sem(f"expert_w_in{r}") for r in range(RING)]
        xg_in = [sem(f"rows_in{r}") for r in range(RING)]
        rows_used = [sem(f"rows_used{r}") for r in range(RING)]
        y_out = [sem(f"y_out{r}") for r in range(RING)]
        eT_sums, eT_ready, egu_sums, etanh, eh_ready, ey_sums, ey_ready, ea_ready = [
            sem(n) for n in ("expert_xT_sums", "expert_xT_ready", "expert_gu_sums", "expert_tanh", "expert_h_ready",
                             "expert_y_sums", "expert_y_ready", "expert_a_ready")]

        steps = {}

        def restart():
            for g in loop_sems:
                g.restart()

        def iteration_end(eng):
            eng.drain().then_inc(arrived.sem, 1)
            eng.wait_ge(go[eng.engine], 1)
            eng.sem_clear(go[eng.engine])

        def run_pair(program, *args):
            live = {S.s: program(S, *args) for S in slots}
            clock = {S.s: LAG * S.s for S in slots}
            kinds = {S.s: [] for S in slots}
            while live:
                s = min(live, key=lambda n: (clock[n], n))
                kind = next(live[s], None)
                if kind is None:
                    del live[s]
                else:
                    clock[s] += LENGTH[kind]
                    kinds[s].append(kind)
            same = steps.setdefault(program.__name__, kinds)
            assert same == kinds, [(n, a, b) for n, (a, b) in enumerate(zip(same[0], kinds[0])) if a != b][:3]

        block = ctx.enter_context(nc.Block())

        @block.sync
        def _(sp):
            def refill(S, src, i, attentions):
                S.oT_ready.wait(sp, attentions)
                S.loaded.by(sp.dma_start(S.ctx, ctx_d[bass.ds(i * 2 + (2 + S.s), 1)].rearrange("o p j d -> (o p) j d")))
                S.xin_free.wait(sp)
                S.loaded.by(sp.dma_start(S.xin[:], src[bass.ds(i * 2 * TQ + (2 + S.s) * TQ, TQ), :]))

            def first(S, src):
                sp.dma_start(S.ctx, ctx_d[S.s]).then_inc(first_in, 16)
                sp.dma_start(S.xin[:], src[S.s * TQ:(S.s + 1) * TQ, :]).then_inc(first_in, 16)

            for S in slots:
                first(S, x_d)
            sp.dma_start(consts[:], T["consts"]).then_inc(const_in, 16)
            sp.dma_start(cols[:], T["cols"]).then_inc(const_in, 16)
            sp.dma_start(xmid_d[NT:NT + 2 * TQ, :], x_d[NT:NT + 2 * TQ, :]).then_inc(spare_in, 16)
            sp.wait_ge(spare_in, 16)
            restart()
            with sp.Fori(0, NB // 2) as i:
                for S in slots:
                    sp.wait_ge(S.scattered, i * 16 * TOP1 + 16)
                    S.tok_in.by(sp.dma_start(S.tok[:], T["tokens"][bass.ds(i * 2 * TQ + S.s * TQ, TQ), :]))
                for S in slots:
                    refill(S, x_d, i, 3)
                for S in slots:
                    S.slots_ready.wait(sp)
                    S.stored.by(sp.dma_start(xn1_d[bass.ds(i * 2 * TQ + S.s * TQ, TQ), :], S.xn[:]))
                for S in slots:
                    S.x_ready.wait(sp)
                    S.stored.by(sp.dma_start(xmid_d[bass.ds(i * 2 * TQ + S.s * TQ, TQ), :], S.x[:]))
                for S in slots:
                    S.loaded.wait(sp, 2)
                    S.stored.wait(sp, 2)
                iteration_end(sp)
            def expert_weights(r, e):
                one = not isinstance(e, int)
                for dst, src in ((ewg[r], T["eg"]), (ewd[r], T["ed"])):
                    src = src[bass.ds(e, 1)].rearrange("o p n -> (o p) n") if one else src[e]
                    sp.dma_start(dst.rearrange("p c n -> p (c n)"), src).then_inc(ew_in[r], 16)

            def store_y(r, i):
                sp.wait_ge(ey_ready, i * RING + r + 1)
                y3 = y_d.rearrange("(p e) d -> p e d", e=E1)
                e = i * RING + r
                dst = y3[:, e, :] if isinstance(i, int) else y3[:, bass.ds(e, 1), :].rearrange("p o d -> p (o d)")
                sp.dma_start(dst, ey[r]).then_inc(y_out[r], 16)
            for r in range(RING):
                expert_weights(r, r)
            sp.dma_start(W[:, INT0:INT0 + WI_N].bitcast(I32), T["wi"]).then_inc(wi_in, 16)
            sp.dma_start(W[:, 0:WC_N], T["wc"]).then_inc(wc_in, 16)
            sp.dma_start(W[:, RC0:RC0 + RC_N], T["rc"].partition_broadcast(128)).then_inc(wc_in, 16)
            for S in slots:
                first(S, xmid_d)
            with sp.Fori(0, E1 // RING - 1) as i:
                for r in range(RING):
                    sp.wait_ge(ey_sums, i * RING + r + 1)
                    expert_weights(r, i * RING + RING + r)
                    store_y(r, i)
            for r in range(RING):
                store_y(r, E1 // RING - 1)
            restart()
            with sp.Fori(0, NB // 2) as i:
                for S in slots:
                    refill(S, xmid_d, i, 1)
                for S in slots:
                    S.x_ready.wait(sp)
                    S.stored.by(sp.dma_start(out_d[bass.ds(i * 2 * TQ + S.s * TQ, TQ), :], S.x[:]))
                for S in slots:
                    S.loaded.wait(sp, 2)
                    S.stored.wait(sp)
                iteration_end(sp)

        @block.gpsimd
        def _(pool):
            def release():
                pool.drain()
                pool.wait_ge(arrived.sem, 4)
                pool.sem_clear(range(lo, hi + 1))
                for g in go.values():
                    pool.sem_inc(g, 1)

            zero = slots[0].P[:, 0, 0:NSLOT // 128].bitcast(U32)
            pool.memset(zero, 0).then_inc(vconst, 1)
            pool.memset(ones[:], 1.0).then_inc(vconst, 1)
            pool.wait_ge(vconst, 1)
            for S in slots:
                half = slice(S.s * NSLOT // 2, (S.s + 1) * NSLOT // 2)
                pool.dma_start(token_d[half].rearrange("(p c) o -> p (c o)", p=128), zero[:, 0:NSLOT // 256]).then_inc(S.scattered, 16)
            for S in slots:
                pool.wait_ge(S.scattered, 16)
            pool.memset(taken[:], 0.0).then_inc(vconst, 1)
            for S in slots:
                pool.memset(S.Q[:], 0.0).then_inc(vconst, 1)
            pool.memset(slot_all[:], 0).then_inc(notes, 1)
            pool.memset(gate_all[:], 0.0).then_inc(notes, 1)
            pool.wait_ge(notes, 2)

            def note(S, i):
                S.slots_ready.wait(pool)
                S.tok_in.wait(pool)
                at = bass.ds(i * 2 * TOP1 + S.s * TOP1, TOP1)
                pool.tensor_copy(slot_all[:, at], S.slot[:])
                pool.tensor_copy(gate_all[:, at], S.w8[:])
                S.noted.by(pool.tensor_copy(S.myscat[:], S.scat[:]))
                S.noted.wait(pool)

            def scatter(S):
                for k in range(TOP1):
                    pool.indirect_dma_start(
                        token_d, bass.IndirectOffsetOnAxis(ap=S.myscat[:, k:k + 1], axis=0), S.tok[:], None,
                        bounds_check=NSLOT - 1, oob_is_err=False).then_inc(S.scattered, 16)
            restart()
            with pool.Fori(0, NB // 2) as i:
                note(slots[0], i)
                scatter(slots[0])
                note(slots[1], i)
                release()
                scatter(slots[1])

            for S in slots:
                pool.wait_ge(S.scattered, 16 * TOP1 * (NB // 2) + 16)
            pool.dma_start(expert_tokens, token_d.rearrange("(p e) o -> p (e o)", e=E1)).then_inc(slots_in, 16)
            pool.wait_ge(slots_in, 16)

            def gather(r, at):
                pool.indirect_dma_start(xg[r], None, xn1_d, bass.IndirectOffsetOnAxis(ap=at, axis=0)).then_inc(xg_in[r], 16)
            for r in range(RING):
                gather(r, expert_tokens[:, r:r + 1])
            with pool.Fori(0, E1 // RING - 1) as i:
                for r in range(RING):
                    pool.tensor_copy(xidx[r], W[:, bass.ds(i * RING + (TOK0 + RING + r), 1)].bitcast(U32)).then_inc(idx_ready, 1)
                    pool.wait_ge(idx_ready, 1)
                    pool.sem_clear(idx_ready)
                    pool.wait_ge(rows_used[r], 1)
                    pool.sem_clear(rows_used[r])
                    gather(r, xidx[r])
            for r in range(RING):
                pool.wait_ge(y_out[r], 16 * (E1 // RING + 1))
            def fetch(S, batch):
                at = bass.ds(batch * TOP1, TOP1) if not isinstance(batch, int) else slice(batch * TOP1, (batch + 1) * TOP1)
                pool.tensor_copy(S.myslot[:], slot_all[:, at]).then_inc(fetch_notes[S.s], 1)
                pool.tensor_copy(S.myw[:], gate_all[:, at]).then_inc(fetch_notes[S.s], 1)
                pool.wait_ge(fetch_notes[S.s], 2)
                pool.sem_clear(fetch_notes[S.s])
                for k in range(TOP1):
                    pool.indirect_dma_start(
                        S.y8[:, k, :], None, y_d, bass.IndirectOffsetOnAxis(ap=S.myslot[:, k:k + 1], axis=0)
                    ).then_inc(S.gathered, 16)
            pool.wait_ge(w3_ready, 1)
            for S in slots:
                fetch(S, S.s)
            restart()
            with pool.Fori(0, NB // 2) as i:
                for S in slots:
                    S.y8_free.wait(pool)
                    fetch(S, i * 2 + (2 + S.s))
                release()
            for S in slots:
                pool.wait_ge(S.gathered, 16 * TOP1 * (NB // 2 + 1))

        @block.tensor
        def _(pe):
            def mm(out, pairs, close=True):
                last = None
                for n, (l, r) in enumerate(pairs):
                    last = nc.tensor.matmul(out, l, r, start=n == 0, stop=n == len(pairs) - 1)
                return last

            def transpose_x(S):
                S.xn_ready.wait(pe)
                for c in range(2):
                    last = nc.tensor.transpose(S.T[:, c * TQ:(c + 1) * TQ], S.xn[:, c * 128:(c + 1) * 128], ident[0:TQ, 0:TQ])
                S.xnT_sums.by(last)

            def transpose_context(S, rows, ready, n):
                if ready:
                    ready.wait(pe, n)
                for j in range(KJ):
                    last = nc.tensor.transpose(S.T[:, j * KP:(j + 1) * KP], rows[:, j, :], ident[0:KP, 0:KP])
                S.ctx_sums.by(last)

            def project(S, results):
                for n, make in enumerate(results):
                    done, sums = [(S.proj_v_done, S.proj_v_sums), (S.proj_s_done, S.proj_s_sums)][n % 2]
                    if n >= 4:
                        done.wait(pe)
                    sums.by(make([S.A, S.B, S.O, S.T][n % 4]))
                nv, ns = (len(results) + 1) // 2, len(results) // 2
                S.proj_v_done.wait(pe, min(nv, 2))
                S.proj_s_done.wait(pe, min(ns, 2))

            def attention(S, D, wq, wk, wv, wo, context, keys):
                nc_ = NH * D // 128
                rows = [(0, keys)] if keys == TQ else [(j * KP, KP) for j in range(KJ)]
                cchunks = 1 if wk.shape[1] == NH * D else 2
                wk3 = wk.rearrange("p (c n) -> p c n", c=cchunks)
                wv3 = wv.rearrange("p (c n) -> p c n", c=cchunks)
                wq3 = wq.rearrange("p (c n) -> p c n", c=2)
                con = (lambda c, a, n: context[:, a:a + n]) if cchunks == 1 else (lambda c, a, n: context[:, c, a:a + n])
                S.xnT_ready.wait(pe)

                def q(bank):
                    for m in range(nc_):
                        last = mm(bank[:, m * TQ:(m + 1) * TQ],
                                  [(wq3[:, c, m * 128:(m + 1) * 128], S.xnT[:, c, :]) for c in range(2)])
                    return last

                def k(ms):
                    def make(bank):
                        for n, m in enumerate(ms):
                            last = mm(bank[:, n * keys:(n + 1) * keys],
                                      [(wk3[:, c, m * 128:(m + 1) * 128], con(c, 0, keys)) for c in range(cchunks)])
                        return last
                    return make

                def v(js):
                    def make(bank):
                        for n, j in enumerate(js):
                            a, cnt = rows[j]
                            last = mm(bank[0:cnt, n * NH * D:(n + 1) * NH * D],
                                      [(con(c, a, cnt), wv3[:, c, :]) for c in range(cchunks)])
                        return last
                    return make
                if keys == TQ:
                    project(S, [q, k(range(nc_)), v([0])])
                elif D == 16:
                    project(S, [q, k([0]), v([0, 1]), k([1]), v([2])])
                else:
                    project(S, [q, k([0]), v([0]), k([1]), v([1]), k([2]), v([2]), k([3])])

                order = head_order(D)

                def score(n):
                    h = order[n]
                    c, g, par = (h // 8, (h % 8) // 2, h % 2) if D == 16 else (h // 4, h % 4, 0)
                    bank = [S.A, S.B][n % 2]
                    S.score_sums.by(nc.tensor.matmul(bank[0:TQ, 0:keys], S.Q[:, 2 * par + c, g, :],
                                                     S.K[:, c, 0:keys] if keys == TK else K_self(S)[:, c, :],
                                                     start=True, stop=True))
                by_scalar = scalar_turns(keys)

                def turn(n):
                    S.probs_ready.wait(pe)
                    for j, (a, cnt) in enumerate(rows):
                        last = nc.tensor.transpose(S.T[0:cnt, j * TQ:(j + 1) * TQ], S.P[0:TQ, n % 2, a:a + cnt], ident[0:TQ, 0:TQ])
                    (S.probsT_s_sums if by_scalar(n) else S.probsT_sums).by(last)

                def av(n):
                    h = order[n]
                    (S.probsT_s_ready if by_scalar(n) else S.probsT_ready).wait(pe)
                    last = mm(S.O[0:TQ, h * D:(h + 1) * D],
                              [(S.PT[0:cnt, n % 2, j, :], S.V[0:cnt, j, h * D:(h + 1) * D]) for j, (a, cnt) in enumerate(rows)])
                    if n == NH - 1:
                        S.av_sums.by(last)
                score(0)
                score(1)
                yield "proj"
                for n in range(NH):
                    if n >= 1:
                        av(n - 1)
                    turn(n)
                    if n + 2 < NH:
                        score(n + 2)
                    yield "head"
                av(NH - 1)
                yield "av"
                S.o_ready.wait(pe)
                for c in range(nc_):
                    last = nc.tensor.transpose(S.T[:, c * TQ:(c + 1) * TQ], S.o[:, c * 128:(c + 1) * 128], ident[0:TQ, 0:TQ])
                S.oT_sums.by(last)
                yield "turn"
                S.oT_ready.wait(pe)
                wo3 = wo.rearrange("p (c n) -> p c n", c=nc_)
                S.out_sums.by(mm(S.A[0:TQ, 0:DM], [(S.oT[:, c, :], wo3[:, c, :]) for c in range(nc_)]))
                yield "out"
                transpose_x(S)
                yield "turn"

            def gate_up(S, groups, M, g):
                bank = [S.A, S.B][g % 2]
                for n in range(4):
                    wx = groups[g][n // 2]
                    last = mm(bank[0:M, n * TQ:(n + 1) * TQ],
                              [(wx[:, c, (n % 2) * M:(n % 2 + 1) * M], S.xnT[:, c, :]) for c in range(2)])
                S.gu_sums.by(last)

            def glu(S, groups, M, per_group):
                for g in range(len(groups)):
                    S.h_ready.wait(pe)
                    if per_group:
                        if g >= 2:
                            S.acc_done.wait(pe)
                        bank = [S.O, S.T][g % 2]
                        last = mm(bank[0:TQ, 0:DM], [(S.hT[0:M, 2 * (g % 2) + c, :], groups[g][2][0:M, c, :]) for c in range(2)])
                    else:
                        for c in range(2):
                            last = nc.tensor.matmul(S.O[0:TQ, 0:DM], S.hT[0:M, 2 * (g % 2) + c, :], groups[g][2][0:M, c, :],
                                                    start=g == 0 and c == 0, stop=g == len(groups) - 1 and c == 1)
                    S.down_sums.by(last)
                    if g + 2 < len(groups):
                        gate_up(S, groups, M, g + 2)
                    yield "glu"
                if per_group:
                    S.acc_done.skip(pe, 2)
                yield "end"
                transpose_x(S)
                yield "turn"

            def mlp(S, w1, w2):
                S.xnT_ready.wait(pe)
                w13, w23 = w1.rearrange("p (c n) -> p c n", c=2), w2.rearrange("p (c n) -> p c n", c=8)
                for half in range(2):
                    for n in range(4):
                        m = 4 * half + n
                        last = mm([S.A, S.B][half][:, n * TQ:(n + 1) * TQ],
                                  [(w13[:, c, m * 128:(m + 1) * 128], S.xnT[:, c, :]) for c in range(2)])
                    S.f1_sums.by(last)
                yield "f1"
                for half in range(2):
                    S.gelu_ready.wait(pe)
                    for n in range(4):
                        m = 4 * half + n
                        last = nc.tensor.matmul(S.O[0:TQ, 0:DM], S.hT[:, m, :], w23[:, m, :], start=m == 0, stop=m == 7)
                S.f2_sums.by(last)
                yield "f2"
                transpose_x(S)
                yield "turn"

            def logits(S, wr, n):
                S.xnT_ready.wait(pe)
                w3_ = wr.rearrange("p (c n) -> p c n", c=2)
                S.logit_sums.by(mm(S.O[0:TQ, 0:n], [(S.xnT[:, c, :], w3_[:, c, :]) for c in range(2)]))

            def pair3(v, a):
                return v.rearrange("p (a b) -> p a b", a=a)

            def phase_a(S):
                transpose_context(S, S.ctx, None, 0)
                yield "ctx"
                S.ctxT_ready.wait(pe)
                transpose_context(S, S.z, S.z_ready, 1)
                yield "end"
                S.ctxT_ready.wait(pe)
                transpose_x(S)
                yield "turn"
                pe.wait_ge(w_in["attn0"], 32)
                yield from attention(S, 16, w("q0"), w("k0"), w("v0"), w("o0"), S.ctxT[:], TK)
                pe.wait_ge(w_in["ffn0"], 16)
                logits(S, w("r0"), E0)
                groups = [tuple(pair3(w(f"e{e}")[:, n * 512:(n + 1) * 512], 2) for n in range(3)) for e in range(E0)]
                gate_up(S, groups, 128, 0)
                gate_up(S, groups, 128, 1)
                yield "logits"
                yield "route"
                yield "route"
                yield from glu(S, groups, 128, True)
                pe.wait_ge(w_in["attn1"], 16)
                yield from attention(S, 32, w("q1"), w("k1"), w("v1"), w("o1"), S.ynT[:], TQ)
                yield from mlp(S, w("f1"), w("g1"))
                pe.wait_ge(w_in["attn2"], 16)
                yield from attention(S, 32, w("q2"), w("k2"), w("v2"), w("o2"), S.yT[:], TK)
                yield from mlp(S, w("f2"), w("g2"))
                pe.wait_ge(w_in["route1"], 16)
                logits(S, w("r1"), E1)
                s3, d3 = w("s1", 2), w("d1", 2)
                shared = [(s3[:, :, 0:F1], s3[:, :, F1:2 * F1], d3)]
                gate_up(S, shared, FH, 0)
                yield "logits"
                yield "route"
                S.mask_ready.wait(pe)
                S.pos_sums.by(mm(S.T[0:TQ, 0:E1], [(const("before")[0:TQ, 0:TQ], S.r[1][:]), (ones[:], S.r[3][:])]))
                yield "route"
                g = glu(S, shared, FH, False)
                yield next(g)
                yield next(g)

            pe.wait_ge(const_in, 32)
            pe.wait_ge(first_in, 64)
            pe.wait_ge(vconst, 5)
            restart()
            with pe.Fori(0, NB // 2) as i:
                run_pair(phase_a)
                iteration_end(pe)

            def turn_rows(r, i, n):
                pe.wait_ge(xg_in[r], i * 16 + 16 * n)
                bank = banks[r % 2]
                for c in range(2):
                    last = nc.tensor.transpose(bank[:, c * 128:(c + 1) * 128], xg[r][:, c * 128:(c + 1) * 128], ident)
                last.then_inc(eT_sums, 1)

            def free_rows(r, i):
                pe.wait_ge(eT_ready, i * RING + r + 1)
                nc.tensor.nop().then_inc(rows_used[r], 1)

            def expert_gate_up(r, i, n):
                pe.wait_ge(eT_ready, i * RING + RING * (n - 1) + r + 1)
                pe.wait_ge(ew_in[r], i * 32 + 32 * n)
                bank = banks[2 + r % 2]
                for m in range(4):
                    last = mm(bank[0:FH, m * 128:(m + 1) * 128],
                              [(ewg[r][:, c, m * FH:(m + 1) * FH], eT[r % 2][:, c, :]) for c in range(2)])
                last.then_inc(egu_sums, 1)

            def down(r, i, n):
                pe.wait_ge(eh_ready, i * RING + RING * (n - 1) + r + 1)
                last = mm(banks[4 + r % 2][:, 0:DM], [(eh[r % 2][:, c, :], ewd[r][:, c, :]) for c in range(2)])
                last.then_inc(ey_sums, 1)

            turn_rows(0, 0, 1)
            expert_gate_up(0, 0, 1)
            turn_rows(1, 0, 1)
            with pe.Fori(0, E1 // RING - 1) as i:
                for r in range(RING):
                    expert_gate_up((r + 1) % RING, i, 1 + (r + 1) // RING)
                    turn_rows((r + 2) % RING, i, 1 + (r + 2) // RING)
                    down(r, i, 1)
                    free_rows(r, i)
            for r in range(RING):
                if r + 1 < RING:
                    expert_gate_up(r + 1, E1 // RING - 1, 1)
                if r + 2 < RING:
                    turn_rows(r + 2, E1 // RING - 1, 1)
                down(r, E1 // RING - 1, 1)

            def experts2(S, n):
                if n == 3:
                    S.gateT_ready.wait(pe)
                if n >= 4:
                    S.pair_done.wait(pe)
                bank = [S.B, S.A, S.O, S.T][n % 4]
                if n < E2 // 2:
                    p3 = wc(f"p{n}", 2)
                    S.pair_sums.by(mm(bank[0:TQ, :], [(S.xnT[:, c, :], p3[:, c, :]) for c in range(2)]))
                elif n == E2 // 2:
                    ws = wc("ws", 4)
                    S.pair_sums.by(mm(bank[0:TQ, 0:DM], [(S.xnT[:, c % 2, :], ws[:, c, :]) for c in range(4)]))
                else:
                    S.pair_sums.by(mm(bank[0:TQ, 0:DM], [(S.gT[:], wc("br")[0:E2, :])]))

            def attention_one(S):
                S.xnT_ready.wait(pe)
                wq, wk, wv = wc("q4", 2), wc("k4"), wc("v4")

                def q(bank):
                    for m in range(2):
                        last = mm(bank[:, m * TQ:(m + 1) * TQ],
                                  [(wq[:, c, m * 128:(m + 1) * 128], S.xnT[:, c, :]) for c in range(2)])
                    return last
                k = lambda m: lambda bank: mm(bank[:, 0:TK], [(wk[:, m * 128:(m + 1) * 128], S.yT[:])])

                def v(js):
                    def make(bank):
                        for n, j in enumerate(js):
                            last = mm(bank[0:KP, n * DM:(n + 1) * DM], [(S.yT[:, j * KP:(j + 1) * KP], wv)])
                        return last
                    return make
                project(S, [q, k(0), v([0, 1]), k(1), v([2])])
                S.score_sums.by(mm(S.A[0:TQ, 0:TK], [(S.Q1[:, c, :], S.K[:, c, :]) for c in range(2)]))
                yield "proj"
                S.probs_ready.wait(pe)
                for j in range(KJ):
                    last = nc.tensor.transpose(S.T[0:KP, j * TQ:(j + 1) * TQ], S.P[0:TQ, 0, j * KP:(j + 1) * KP], ident[0:TQ, 0:TQ])
                S.probsT_sums.by(last)
                yield "head"
                S.probsT_ready.wait(pe)
                S.av_sums.by(mm(S.O[0:TQ, 0:DM], [(S.PT[0:KP, 0, j, :], S.V[0:KP, j, 0:DM]) for j in range(KJ)]))
                yield "out"
                transpose_x(S)
                yield "turn"

            def phase_c(S):
                transpose_context(S, S.ctx, None, 0)
                yield "ctx"
                S.ctxT_ready.wait(pe)
                transpose_x(S)
                yield "turn"
                yield from attention(S, 16, wc("q3"), wc("k3"), wc("v3"), wc("o3"), S.yT[:], TK)
                logits(S, wc("c2"), E2)
                experts2(S, 0)
                experts2(S, 1)
                yield "logits"
                S.gate_ready.wait(pe)
                S.gateT_sums.by(nc.tensor.transpose(S.T[0:E2, 0:TQ], S.r[3][:, 0:E2], ident[0:TQ, 0:TQ]))
                yield "route"
                for n in range(E2 // 2 + 2):
                    if n + 2 < E2 // 2 + 2:
                        experts2(S, n + 2)
                    yield "pair"
                S.pair_done.wait(pe, 4)
                transpose_x(S)
                yield "turn"
                yield from attention_one(S)
                pe.wait_ge(w3_ready, 1)
                S.xnT_ready.wait(pe)
                g3, u3 = w3[0].rearrange("p (c n) -> p c n", c=2), w3[1].rearrange("p (c n) -> p c n", c=2)
                d3 = w3[2].rearrange("p (c n) -> p c n", c=6)
                groups = [(g3[:, :, 256 * g:256 * g + 256], u3[:, :, 256 * g:256 * g + 256], d3[:, 2 * g:2 * g + 2, :])
                          for g in range(3)]
                gate_up(S, groups, 128, 0)
                gate_up(S, groups, 128, 1)
                yield "f1"
                down = glu(S, groups, 128, False)
                for n in range(4):
                    yield next(down)

            pe.wait_ge(first_in, 128)
            pe.wait_ge(wc_in, 32)
            restart()
            with pe.Fori(0, NB // 2) as i:
                run_pair(phase_c)
                iteration_end(pe)

        @block.scalar
        def _(act):
            def load(name, a, b):
                act.dma_start(W[:, a:b], T["wa"][:, a:b]).then_inc(w_in[name], 16)
            load("attn0", 0, WA["r0"][0])
            act.dma_start(W[:, WA_N:WA_N + RA_N], T["ra"].partition_broadcast(128)).then_inc(w_in["attn0"], 16)
            act.wait_ge(first_in, 64)
            act.wait_ge(const_in, 32)
            load("ffn0", WA["r0"][0], WA["q1"][0])
            load("attn1", WA["q1"][0], WA["q2"][0])
            load("attn2", WA["q2"][0], WA["r1"][0])
            load("route1", WA["r1"][0], WA_N)

            def keys(S, nk, out, bias):
                S.proj_s_sums.wait(act)
                bank = [S.B, S.T][nk % 2]
                if bias is None:
                    S.proj_s_done.by(nc.scalar.activation(out, bank[:, 0:TK], ACT.Copy))
                else:
                    S.proj_s_done.by(nc.scalar.activation(out, bank[:, 0:TK], ACT.Identity, bias=bias))

            def softmax(S, heads, nkeys, D):
                order = head_order(D) if heads == NH else [0]

                def exp(n):
                    S.nmax_ready.wait(act)
                    S.probs_ready.by(nc.scalar.activation(
                        S.P[0:TQ, n % 2, 0:nkeys], [S.A, S.B][n % 2][0:TQ, 0:nkeys], ACT.Exp,
                        bias=S.nmax[:, n:n + 1], accum_out=S.rs[:, order[n]:order[n] + 1]))
                by_scalar = scalar_turns(nkeys)
                for n in range(min(heads, 2)):
                    exp(n)
                yield "proj"
                for n in range(heads):
                    if by_scalar(n):
                        S.probsT_s_sums.wait(act)
                        S.probsT_s_ready.by(nc.scalar.activation(
                            S.PT[0:KP, n % 2, :, :], S.T[0:KP, 0:KJ * TQ].rearrange("p (j t) -> p j t", j=KJ), ACT.Copy))
                    if n + 2 < heads:
                        exp(n + 2)
                    yield "head"
                if heads == NH:
                    yield "av"
                    yield "turn"
                yield "out"
                yield "turn"

            def tanh(S, g, M):
                S.gu_sums.wait(act)
                bank = [S.A, S.B][g % 2]
                S.tanh_ready.by(nc.scalar.activation(S.th[0:M, 2 * (g % 2):2 * (g % 2) + 2, :],
                                                     bank[0:M, 0:2 * TQ].rearrange("p (c t) -> p c t", c=2), ACT.Tanh, scale=0.5))

            def glu(S, groups, M):
                for g in range(groups):
                    if g + 2 < groups:
                        tanh(S, g + 2, M)
                    yield "glu"
                yield "end"
                yield "turn"

            def gelu(S, bias):
                for half in range(2):
                    S.f1_sums.wait(act)
                    for n in range(4):
                        m = 4 * half + n
                        last = nc.scalar.activation(S.hT[:, m, :], [S.A, S.B][half][:, n * TQ:(n + 1) * TQ], ACT.Gelu,
                                                    bias=col(bias, m))
                    S.gelu_ready.by(last)
                yield "f1"
                yield "f2"
                yield "turn"

            def phase_a(S):
                yield "ctx"
                yield "end"
                yield "turn"
                for m in range(2):
                    keys(S, m, S.K[:, m, :], col("bk0", m))
                yield from softmax(S, NH, TK, 16)
                S.logits_ready.wait(act)
                S.exp_ready.by(nc.scalar.activation(S.r[1][:, 0:E0], S.r[0][:, 0:E0], ACT.Tanh, scale=0.5))
                tanh(S, 0, 128)
                tanh(S, 1, 128)
                yield "logits"
                S.logits_ready.wait(act)
                nc.scalar.activation(S.r[2][:, 0:E0], S.r[0][:, 0:E0], ACT.Exp, scale=-1.0 / 0.1)
                S.exp_ready.by(nc.scalar.activation(S.r[3][:, 0:E0], S.r[0][:, 0:E0], ACT.Exp, scale=-1.0 / 0.3))
                yield "route"
                yield "route"
                yield from glu(S, E0, 128)
                S.proj_s_sums.wait(act)
                S.proj_s_done.by(nc.scalar.activation(K_self(S), S.B[:, 0:4 * TQ].rearrange("p (c t) -> p c t", c=4), ACT.Copy))
                yield from softmax(S, NH, TQ, 32)
                yield from gelu(S, "f1b")
                for m in range(4):
                    keys(S, m, S.K[:, m, :], None)
                yield from softmax(S, NH, TK, 32)
                yield from gelu(S, "f2b")
                S.logits_ready.wait(act)
                S.exp_ready.by(nc.scalar.activation(S.r[0][:], S.O[0:TQ, 0:E1], ACT.Exp, bias=S.sc[:, 0:1], accum_out=S.sc[:, 1:2]))
                tanh(S, 0, FH)
                yield "logits"
                yield "route"
                yield "route"
                yield "glu"
                yield "end"

            act.wait_ge(const_in, 32)
            restart()
            with act.Fori(0, NB // 2) as i:
                run_pair(phase_a)
                iteration_end(act)

            def expert(r, i):
                act.wait_ge(egu_sums, i * RING + r + 1)
                nc.scalar.activation(eth[r % 2], banks[2 + r % 2][0:FH, 0:256].rearrange("p (c t) -> p c t", c=2),
                                     ACT.Tanh, scale=0.5).then_inc(etanh, 1)

            def output(r, i):
                act.wait_ge(ey_sums, i * RING + r + 1)
                act.wait_ge(y_out[r], i * 16 + 16)
                nc.scalar.activation(ey[r], banks[4 + r % 2][:, 0:DM], ACT.Copy).then_inc(ey_ready, 1)

            for r in range(RING):
                act.sem_inc(y_out[r], 16)
            expert(0, 0)
            with act.Fori(0, E1 // RING - 1) as i:
                for r in range(RING):
                    if r + 1 < RING:
                        expert(r + 1, i)
                    else:
                        expert(0, i + 1)
                    output(r, i)
            for r in range(RING):
                if r + 1 < RING:
                    expert(r + 1, E1 // RING - 1)
                output(r, E1 // RING - 1)
            def phase_c(S):
                yield "ctx"
                yield "turn"
                for m in range(2):
                    keys(S, m, S.K[:, m, :], None)
                yield from softmax(S, NH, TK, 16)
                S.logits_ready.wait(act)
                S.exp_ready.by(nc.scalar.activation(S.r[0][:, 0:E2], S.r[1][:, 0:E2], ACT.Exp, bias=S.sc[:, 0:1], accum_out=S.sc[:, 1:2]))
                yield "logits"
                yield "route"
                for n in range(E2 // 2 + 2):
                    yield "pair"
                yield "turn"
                for m in range(2):
                    keys(S, m, S.K[:, m, :], col("bk4", m))
                yield from softmax(S, 1, TK, DM)
                tanh(S, 0, 128)
                tanh(S, 1, 128)
                yield "f1"
                down = glu(S, 3, 128)
                for n in range(4):
                    yield next(down)

            restart()
            with act.Fori(0, NB // 2) as i:
                run_pair(phase_c)
                iteration_end(act)

        @block.vector
        def _(v):
            def then(ins):
                vstep.by(ins)
                vstep.wait(v)

            def inverse_std(S, p, n):
                var, hv, y, t = S.mv[0:p, 0:n, 1], S.hv[0:p, 0:n], S.rstd[0:p, 0:n], S.nt[0:p, 0:n]
                then(v.tensor_scalar(hv, var, EPS, 0.5, ALU.add, ALU.mult))
                then(v.tensor_scalar(y.bitcast(I32), hv.bitcast(I32), -0.5, MAGIC, ALU.mult, ALU.add))
                for _ in range(3):
                    if n == 1:
                        then(v.scalar_tensor_tensor(t, y, hv, y, ALU.mult, ALU.mult))
                    else:
                        then(v.tensor_tensor(t, y, y, ALU.mult))
                        then(v.tensor_tensor(t, t, hv, ALU.mult))
                    then(v.scalar_tensor_tensor(y, t, 1.5, y, ALU.subtract, ALU.mult))

            def normalise(S, src, dst):
                then(v.bn_stats(S.st[0:TQ, :], src))
                then(v.bn_aggr(S.mv[0:TQ, 0, :], S.st[0:TQ, :]))
                inverse_std(S, TQ, 1)
                return v.tensor_scalar(dst, src, S.mv[0:TQ, 0, 0:1], S.rstd[0:TQ, 0:1], ALU.subtract, ALU.mult)

            def norm(S, src):
                S.xn_ready.by(normalise(S, src, S.xn[:]))

            def turned_x(S, affine=()):
                S.xnT_sums.wait(v)
                if not affine:
                    last = v.tensor_copy(S.xnT[:], S.T[:, 0:2 * TQ].rearrange("p (c t) -> p c t", c=2))
                for dst, g, b in affine:
                    for c in range(2):
                        last = v.tensor_scalar(dst[:, c, :], S.T[:, c * TQ:(c + 1) * TQ], col(g, c), col(b, c), ALU.mult, ALU.add)
                S.xnT_ready.by(last)

            def queries(S, D, bias, scale):
                S.proj_v_sums.wait(v)
                if D == 16:
                    for g in range(4):
                        lanes = slice(32 * g, 32 * g + 32)
                        for par, side in enumerate(("even", "odd")):
                            side = cols[lanes, CO[side][0]:CO[side][0] + 1]
                            if bias:
                                for c in range(2):
                                    at = CO[bias][0] + c
                                    last = v.tensor_scalar(S.Q[lanes, 2 * par + c, g, :], S.A[lanes, c * TQ:(c + 1) * TQ],
                                                           cols[lanes, at:at + 1], side, ALU.add, ALU.mult)
                            else:
                                last = v.tensor_scalar(S.Q[lanes, 2 * par:2 * par + 2, g, :],
                                                       S.A[lanes, 0:2 * TQ].rearrange("p (c t) -> p c t", c=2), side, None, ALU.mult)
                elif D == 32:
                    for g in range(4):
                        lanes = slice(32 * g, 32 * g + 32)
                        last = v.tensor_scalar(S.Q[lanes, :, g, :], S.A[lanes, 0:4 * TQ].rearrange("p (c t) -> p c t", c=4),
                                               scale, None, ALU.mult)
                else:
                    for c in range(2):
                        last = v.tensor_scalar(S.Q1[:, c, :], S.A[:, c * TQ:(c + 1) * TQ], col(bias, c), None, ALU.add)
                S.proj_v_done.by(last)

            def values(S, js, width, bank, p, bias=None):
                S.proj_v_sums.wait(v)
                src = bank[0:p, 0:len(js) * width].rearrange("p (j n) -> p j n", j=len(js))
                dst = S.V[0:p, js[0]:js[-1] + 1, 0:width]
                if bias is None:
                    last = v.tensor_copy(dst, src)
                else:
                    for n in range(len(js)):
                        last = v.tensor_tensor(dst[:, n, :], src[:, n, :], bias, ALU.add)
                S.proj_v_done.by(last)

            def heads(S, D, nkeys, nheads=NH):
                rows = [(0, nkeys)] if nkeys == TQ else [(j * KP, KP) for j in range(KJ)]
                p = rows[0][1]

                def nmax(h):
                    S.score_sums.wait(v)
                    S.nmax_ready.by(v.tensor_reduce(S.nmax[:, h:h + 1], [S.A, S.B][h % 2][0:TQ, 0:nkeys], AX_X, ALU.max, negate=True))

                def turned(h):
                    S.probsT_sums.wait(v)
                    if nkeys == TQ:
                        last = v.tensor_tensor(S.PT[0:TQ, h % 2, 0, :], S.T[0:TQ, 0:TQ], const("after")[0:TQ, 0:TQ], ALU.mult)
                    else:
                        last = v.tensor_copy(S.PT[0:p, h % 2, :, :], S.T[0:p, 0:KJ * TQ].rearrange("p (j t) -> p j t", j=KJ))
                    S.probsT_ready.by(last)
                by_scalar = scalar_turns(nkeys)
                for h in range(min(nheads, 2)):
                    nmax(h)
                yield "proj"
                for h in range(nheads):
                    if not by_scalar(h):
                        turned(h)
                    if h + 2 < nheads:
                        nmax(h + 2)
                    yield "head"
                S.av_sums.wait(v)
                then(v.reciprocal(S.rinv[:, 0:nheads], S.rs[:, 0:nheads]))

            def attention_end(S, D):
                n = NH * D
                S.o_ready.by(v.tensor_tensor(S.o[:, 0:n].rearrange("p (h d) -> p h d", h=NH),
                                             S.O[0:TQ, 0:n].rearrange("p (h d) -> p h d", h=NH),
                                             S.rinv[:].unsqueeze(2).broadcast_to([TQ, NH, D]), ALU.mult))
                yield "av"
                S.oT_sums.wait(v)
                c = n // 128
                S.oT_ready.by(v.tensor_copy(S.oT[:, 0:c, :], S.T[:, 0:c * TQ].rearrange("p (c t) -> p c t", c=c)))
                yield "turn"
                S.out_sums.wait(v)

            def glu(S, groups, M, per_group, weights=None):
                def added(g):
                    S.down_sums.wait(v)
                    if per_group:
                        ins = v.scalar_tensor_tensor(S.x[:], [S.O, S.T][g % 2][0:TQ, 0:DM], weights[:, g:g + 1], S.x[:], ALU.mult, ALU.add)
                        S.acc_done.by(ins)
                        S.acc_done.wait(v)
                    elif g == groups - 1:
                        then(v.tensor_tensor(S.x[:], S.x[:], S.O[0:TQ, 0:DM], ALU.add))
                for g in range(groups):
                    bank = [S.A, S.B][g % 2]
                    gate, up = [bank[0:M, n * 2 * TQ:(n + 1) * 2 * TQ].rearrange("p (c t) -> p c t", c=2) for n in range(2)]
                    S.tanh_ready.wait(v)
                    a = S.a[g % 2][0:M]
                    then(v.scalar_tensor_tensor(a, S.th[0:M, 2 * (g % 2):2 * (g % 2) + 2, :], 1.0, gate, ALU.add, ALU.mult))
                    S.h_ready.by(v.scalar_tensor_tensor(S.hT[0:M, 2 * (g % 2):2 * (g % 2) + 2, :], a, 0.5, up, ALU.mult, ALU.mult))
                    if g >= 1:
                        added(g - 1)
                    yield "glu"
                added(groups - 1)

            def top_mask(S, src, n, k, mask):
                v8 = S.g8[:]
                if k < 8:
                    then(v.memset(src[:, n:n + 8], -1.0))
                    then(v.max(v8, src[:, 0:n + 8]))
                    then(v.memset(v8[:, k:8], -1.0))
                    width = n + 8
                else:
                    then(v.max(v8, src))
                    width = n
                then(v.match_replace(mask[:, 0:width], v8, src[:, 0:width], -2.0))
                then(v.tensor_scalar(mask[:, 0:n], mask[:, 0:n], -2.0, None, ALU.is_equal))

            def reduce(out, src):
                then(v.tensor_reduce(out, src, AX_X, ALU.add))

            def route0(S):
                r0, r1, r2, r3 = [t[:, 0:E0] for t in S.r]
                c = lambda n: S.sc[:, n:n + 1]
                S.logit_sums.wait(v)
                S.logits_ready.by(v.tensor_scalar(r0, S.O[0:TQ, 0:E0], rtemp[:], None, ALU.mult))
                yield "logits"
                S.exp_ready.wait(v)
                then(v.tensor_scalar(r1, r1, 0.5, 0.5, ALU.mult, ALU.add))
                then(v.tensor_scalar(r2, r1, CENTER, None, ALU.subtract))
                S.logits_ready.by(v.scalar_tensor_tensor(r0, r2, -1.0, r2, ALU.mult, ALU.max))
                then(v.tensor_scalar(S.idf[:], r1, LOWER, None, ALU.is_ge))
                then(v.scalar_tensor_tensor(S.idf[:], r1, UPPER, S.idf[:], ALU.is_le, ALU.mult))
                yield "route"
                S.exp_ready.wait(v)
                then(v.tensor_tensor(S.w8[:], r2, S.idf[:], ALU.mult))
                reduce(c(0), S.w8[:])
                then(v.tensor_scalar(c(0), c(0), 1e-8, None, ALU.is_lt))
                top_mask(S, S.r[3][:], E0, 2, S.r[1][:])
                then(v.tensor_tensor(r3, r3, r1, ALU.mult))
                reduce(c(1), r3)
                then(v.tensor_scalar(c(1), c(1), 1e-8, None, ALU.max))
                then(v.reciprocal(c(1), c(1)))
                then(v.tensor_scalar(r3, r3, c(1), None, ALU.mult))
                then(v.tensor_tensor(r3, r3, S.w8[:], ALU.subtract))
                then(v.scalar_tensor_tensor(S.w8[:], r3, c(0), S.w8[:], ALU.mult, ALU.add))
                reduce(c(2), S.w8[:])
                then(v.tensor_scalar(c(2), c(2), 1e-8, None, ALU.max))
                then(v.reciprocal(c(2), c(2)))
                then(v.tensor_scalar(S.w8[:], S.w8[:], c(2), None, ALU.mult))
                yield "route"

            def route1(S):
                S.logit_sums.wait(v)
                S.logits_ready.by(v.tensor_reduce(S.sc[:, 0:1], S.O[0:TQ, 0:E1], AX_X, ALU.max, negate=True))
                yield "logits"
                S.exp_ready.wait(v)
                then(v.reciprocal(S.sc[:, 2:3], S.sc[:, 1:2]))
                then(v.tensor_scalar(S.r[0][:], S.r[0][:], S.sc[:, 2:3], None, ALU.mult))
                then(v.max(S.g8[:], S.r[0][:]))
                then(v.max_index(S.i8[:], S.g8[:], S.r[0][:]))
                then(v.match_replace(S.r[1][:], S.g8[:], S.r[0][:], -2.0))
                then(v.tensor_scalar(S.r[1][:], S.r[1][:], -2.0, None, ALU.is_equal))
                then(v.tensor_copy(S.r[3][:], taken[:]))
                ins = v.tensor_tensor(taken[:], taken[:], S.r[1][:], ALU.add)
                S.mask_ready.by(ins)
                S.mask_ready.wait(v)
                reduce(S.sc[:, 3:4], S.g8[:])
                then(v.reciprocal(S.sc[:, 3:4], S.sc[:, 3:4]))
                then(v.tensor_scalar(S.w8[:], S.g8[:], S.sc[:, 3:4], None, ALU.mult))
                then(v.tensor_copy(S.idf[:], S.i8[:]))
                yield "route"
                S.pos_sums.wait(v)
                then(v.tensor_scalar(S.r[0][:], S.T[0:TQ, 0:E1], float(CAP), DROPPED, ALU.is_ge, ALU.mult))
                then(v.scalar_tensor_tensor(S.r[2][:], S.T[0:TQ, 0:E1], float(E1), S.r[0][:], ALU.mult, ALU.add))
                then(v.tensor_tensor(S.r[2][:], S.r[2][:], const("iota")[0:TQ, :], ALU.add))
                for k in range(TOP1):
                    then(v.scalar_tensor_tensor(S.r[0][:], const("iota")[0:TQ, :], S.idf[:, k:k + 1], S.r[2][:],
                                                ALU.is_equal, ALU.mult, accum_out=S.slotf[:, k:k + 1]))
                then(v.tensor_copy(S.scat[:], S.slotf[:]))
                then(v.tensor_scalar(S.idf[:], S.slotf[:], float(NSLOT), None, ALU.is_lt))
                then(v.tensor_tensor(S.w8[:], S.w8[:], S.idf[:], ALU.mult))
                then(v.tensor_tensor(S.slotf[:], S.slotf[:], S.idf[:], ALU.mult))
                S.slots_ready.by(v.tensor_copy(S.slot[:], S.slotf[:]))
                yield "route"

            def add_row(S, dst, bank, name, base):
                then(v.tensor_tensor(dst, bank[0:TQ, 0:DM], base, ALU.add))
                if name:
                    then(v.tensor_tensor(dst, dst, row(name), ALU.add))

            def block1(S, n, keys):
                yield from heads(S, 32, keys)
                yield from attention_end(S, 32)
                add_row(S, S.xo[:], S.A, f"o{n}b", S.x1[:])
                norm(S, S.xo[:])
                yield "out"
                turned_x(S, [(S.xnT, f"n{n}g", f"n{n}b")])
                yield "turn"
                yield "f1"
                S.f2_sums.wait(v)
                add_row(S, S.xo[:], S.O, f"g{n}b", S.xo[:])
                then(v.tensor_tensor(S.xo[:], S.xo[:], S.x1[:], ALU.add))

            def own_norm(S, src, g, b):
                then(normalise(S, src, S.x1[:]))
                then(v.tensor_tensor(S.x1[:], S.x1[:], row(g), ALU.mult))
                then(v.tensor_tensor(S.x1[:], S.x1[:], row(b), ALU.add))
                norm(S, S.x1[:])

            def phase_a(S):
                for j in range(KJ):
                    then(v.bn_stats(S.st[0:KP, :], S.ctx[:, j, :]))
                    then(v.bn_aggr(S.mv[0:KP, j, :], S.st[0:KP, :]))
                inverse_std(S, KP, KJ)
                for j in range(KJ):
                    ins = v.tensor_scalar(S.z[:, j, :], S.ctx[:, j, :], S.mv[0:KP, j, 0:1], S.rstd[0:KP, j:j + 1],
                                          ALU.subtract, ALU.mult)
                S.z_ready.by(ins)
                S.ctx_sums.wait(v)
                S.ctxT_ready.by(v.tensor_copy(S.ctxT[:], S.T[:, 0:TK]))
                yield "ctx"
                norm(S, S.xin[:])
                S.ctx_sums.wait(v)
                S.ctxT_ready.by(v.tensor_scalar(S.yT[:], S.T[:, 0:TK], col("y2g"), col("y2b"), ALU.mult, ALU.add))
                yield "end"
                turned_x(S)
                yield "turn"
                v.wait_ge(w_in["attn0"], 32)
                queries(S, 16, "bq0", 0.25)
                values(S, [0, 1], DM, S.O, KP, row("bv0", KP))
                values(S, [2], DM, S.A, KP, row("bv0", KP))
                yield from heads(S, 16, TK)
                yield from attention_end(S, 16)
                S.xin_free.by(v.tensor_tensor(S.x[:], S.A[0:TQ, 0:DM], S.xin[:], ALU.add))
                S.xin_free.wait(v)
                then(v.tensor_tensor(S.x[:], S.x[:], row("bo0"), ALU.add))
                norm(S, S.x[:])
                yield "out"
                turned_x(S)
                yield "turn"
                yield from route0(S)
                yield from glu(S, E0, 128, True, S.w8)
                then(normalise(S, S.x[:], S.xo[:]))
                own_norm(S, S.xo[:], "ln1g", "ln1b")
                yield "end"
                turned_x(S, [(S.xnT, "x1g", "x1b"), (S.ynT, "y1g", "y1b")])
                yield "turn"
                queries(S, 32, None, 32.0 ** -0.5)
                values(S, [0], 512, S.O, TQ)
                yield from block1(S, 1, TQ)
                own_norm(S, S.xo[:], "ln2g", "ln2b")
                yield "f2"
                turned_x(S, [(S.xnT, "x2g", "x2b")])
                yield "turn"
                queries(S, 32, None, 32.0 ** -0.5)
                for j in range(KJ):
                    values(S, [j], 512, [S.O, S.A][j % 2], KP)
                yield from block1(S, 2, TK)
                then(v.tensor_tensor(S.x[:], S.x[:], S.xo[:], ALU.add))
                norm(S, S.x[:])
                yield "f2"
                turned_x(S)
                yield "turn"
                yield from route1(S)
                yield from glu(S, 1, FH, False)
                S.x_ready.by(v.tensor_copy(S.sc[:, 0:1], S.x[:, 0:1]))
                yield "end"

            v.wait_ge(const_in, 32)
            v.wait_ge(first_in, 64)
            v.wait_ge(vconst, 5)
            v.reciprocal(rtemp[:], col("temp", p=TQ)).then_inc(rtemp_ready, 1)
            v.wait_ge(rtemp_ready, 1)
            restart()
            with v.Fori(0, NB // 2) as i:
                run_pair(phase_a)
                iteration_end(v)

            def rows(r, i, n):
                v.wait_ge(eT_sums, i * RING + RING * (n - 1) + r + 1)
                v.tensor_copy(eT[r % 2], banks[r % 2][:, 0:256].rearrange("p (c t) -> p c t", c=2)).then_inc(eT_ready, 1)

            def hidden(r, i):
                gate, up = [banks[2 + r % 2][0:FH, n * 256:(n + 1) * 256].rearrange("p (c t) -> p c t", c=2) for n in range(2)]
                v.wait_ge(etanh, i * RING + r + 1)
                v.scalar_tensor_tensor(ea[r % 2], eth[r % 2], 1.0, gate, ALU.add, ALU.mult).then_inc(ea_ready, 1)
                v.wait_ge(ea_ready, i * RING + r + 1)
                v.scalar_tensor_tensor(eh[r % 2], ea[r % 2], 0.5, up, ALU.mult, ALU.mult).then_inc(eh_ready, 1)

            rows(0, 0, 1)
            rows(1, 0, 1)
            with v.Fori(0, E1 // RING - 1) as i:
                for r in range(RING):
                    hidden(r, i)
                    rows((r + 2) % RING, i, 1 + (r + 2) // RING)
            for r in range(RING):
                hidden(r, E1 // RING - 1)
                if r + 2 < RING:
                    rows(r + 2, E1 // RING - 1, 1)
                if r == 1:
                    v.wait_ge(wi_in, 16)
                    v.tensor_scalar(W[:, FLT0:FLT0 + WI_N], W[:, INT0:INT0 + WI_N].bitcast(I32), 1.0 / 127.0, None,
                                    ALU.mult).then_inc(w3_ready, 1)

            def route2(S):
                r0, r1, r3 = S.r[0], S.r[1], S.r[3]
                S.logit_sums.wait(v)
                then(v.tensor_tensor(r1[:, 0:E2], S.O[0:TQ, 0:E2], row("ebias", TQ, RC, RC0)[:, 0:E2], ALU.add))
                S.logits_ready.by(v.tensor_reduce(S.sc[:, 0:1], r1[:, 0:E2], AX_X, ALU.max, negate=True))
                yield "logits"
                S.exp_ready.wait(v)
                then(v.reciprocal(S.sc[:, 2:3], S.sc[:, 1:2]))
                then(v.tensor_scalar(r0[:, 0:E2], r0[:, 0:E2], S.sc[:, 2:3], None, ALU.mult))
                top_mask(S, r0[:], E2, 2, r3[:])
                S.gate_ready.by(v.tensor_tensor(r3[:, 0:E2], r3[:, 0:E2], r0[:, 0:E2], ALU.mult))
                S.gate_ready.wait(v)
                S.gateT_sums.wait(v)
                S.gateT_ready.by(v.tensor_copy(S.gT[:], S.T[0:E2, 0:TQ]))
                then(v.tensor_tensor(S.x[:], S.x[:], S.xn[:], ALU.add))
                yield "route"

            def phase_c(S, i):
                v.wait_ge(S.gathered, i * 16 * TOP1 + 16 * TOP1)
                S.xin_free.by(v.scalar_tensor_tensor(S.x[:], S.y8[:, 0, :], S.myw[:, 0:1], S.xin[:], ALU.mult, ALU.add))
                S.xin_free.wait(v)
                for k in range(1, TOP1):
                    ins = v.scalar_tensor_tensor(S.x[:], S.y8[:, k, :], S.myw[:, k:k + 1], S.x[:], ALU.mult, ALU.add)
                    if k < TOP1 - 1:
                        then(ins)
                S.y8_free.by(ins)
                S.y8_free.wait(v)
                S.ctx_sums.wait(v)
                S.ctxT_ready.by(v.tensor_copy(S.yT[:], S.T[:, 0:TK]))
                norm(S, S.x[:])
                yield "ctx"
                turned_x(S)
                yield "turn"
                queries(S, 16, None, 0.25)
                values(S, [0, 1], DM, S.O, KP)
                values(S, [2], DM, S.A, KP)
                yield from heads(S, 16, TK)
                yield from attention_end(S, 16)
                add_row(S, S.x[:], S.A, None, S.x[:])
                norm(S, S.x[:])
                yield "out"
                turned_x(S)
                yield "turn"
                yield from route2(S)
                x = S.x[:]
                for n in range(E2 // 2 + 2):
                    bank = [S.B, S.A, S.O, S.T][n % 4][0:TQ, :]
                    S.pair_sums.wait(v)
                    if n < E2 // 2:
                        e = 2 * n
                        then(v.scalar_tensor_tensor(x, bank[:, 0:DM], S.r[3][:, e:e + 1], x, ALU.mult, ALU.add))
                        S.pair_done.by(v.scalar_tensor_tensor(x, bank[:, DM:], S.r[3][:, e + 1:e + 2], x, ALU.mult, ALU.add))
                        S.pair_done.wait(v)
                    elif n == E2 // 2:
                        S.pair_done.by(v.tensor_tensor(S.xo[:], bank[:, 0:DM], row("bs0", TQ, RC, RC0), ALU.add))
                        S.pair_done.wait(v)
                        then(v.tensor_tensor(S.xo[:], S.xo[:], row("bs1", TQ, RC, RC0), ALU.add))
                        then(v.scalar_tensor_tensor(x, S.xo[:], 0.5, x, ALU.mult, ALU.add))
                    else:
                        S.pair_done.by(v.tensor_tensor(x, x, bank[:, 0:DM], ALU.add))
                        S.pair_done.wait(v)
                        norm(S, x)
                    yield "pair"
                turned_x(S)
                yield "turn"
                queries(S, DM, "bq4", None)
                values(S, [0, 1], DM, S.O, KP, row("bv4", KP, RC, RC0))
                values(S, [2], DM, S.A, KP, row("bv4", KP, RC, RC0))
                yield from heads(S, DM, TK, 1)
                then(v.scalar_tensor_tensor(S.x[:], S.O[0:TQ, 0:DM], S.rinv[:, 0:1], S.x[:], ALU.mult, ALU.add))
                norm(S, S.x[:])
                yield "out"
                turned_x(S)
                yield "turn"
                yield "f1"
                yield from glu(S, 3, 128, False)
                S.x_ready.by(v.tensor_copy(S.sc[:, 0:1], S.x[:, 0:1]))
                yield "end"

            v.wait_ge(first_in, 128)
            v.wait_ge(wc_in, 32)
            restart()
            with v.Fori(0, NB // 2) as i:
                run_pair(phase_c, i)
                iteration_end(v)


def kernel(**inputs):
    import numpy as np
    import concourse.bacc as bacc
    from concourse.bass_utils import run_bass_kernel_spmd as run

    g = {n: np.ascontiguousarray(a) for n, a in inputs.items()}

    def chunks(a, p=128):
        k, n = a.shape
        out = np.zeros((128, (k // p) * n), a.dtype)
        out[0:p] = a.reshape(k // p, p, n).transpose(1, 0, 2).reshape(p, -1)
        return out

    def heads(a):
        return a.transpose(1, 0, 2).reshape(a.shape[1], -1)

    def column(a):
        return a.reshape(-1, 128).T

    def wide(a, n):
        out = np.zeros((a.shape[0], n), a.dtype)
        out[:, 0:a.shape[1]] = a
        return out

    wa = [chunks(g["L0_xattn_Wq"]), g["L0_xattn_Wk"], g["L0_xattn_Wv"], chunks(g["L0_xattn_Wo"]), chunks(g["L0_ffn_Wr"])]
    for e in range(E0):
        wa += [chunks(g[f"L0_ffn_W{n}"][e]) for n in "gud"]
    for a in ("a1", "a2"):
        wa += [chunks(heads(g[f"L1_xattn_{a}_w{n}"])) for n in "qkv"]
        wa += [chunks(g[f"L1_xattn_{a}_li{n}_w"]) for n in (1, 2, 3)]
    wa += [chunks(g["L1_ffn_router_w"].T), chunks(g["L1_ffn_ws_gate_up"]), chunks(g["L1_ffn_ws_down"], FH)]
    wr = g["L2_ffn_Wr"].transpose(0, 2, 1)
    wc = [chunks(g["L2_xattn_Wq"].T), chunks(g["L2_xattn_Wkv"].T[:, 0:DM]), chunks(g["L2_xattn_Wkv"].T[:, DM:]),
          chunks(g["L2_xattn_Wo"].T), chunks(g["L2_ffn_centroids"].T)]
    wc += [chunks(np.concatenate([wr[2 * e], wr[2 * e + 1]], 1)) for e in range(E2 // 2)]
    wc += [chunks(g["L2_ffn_Ws"][n].T) for n in range(2)]
    br = np.zeros((128, DM), np.float32)
    br[0:E2] = g["L2_ffn_br"]
    wc += [br, chunks(g["L3_xattn_Wq"]), g["L3_xattn_Wk"], g["L3_xattn_Wv"]]
    wi = [chunks(g["L3_ffn_w_gate"].T), chunks(g["L3_ffn_w_up"].T), chunks(g["L3_ffn_w_down"].T)]
    L1 = "L1_xattn_"
    ra = [g["L0_xattn_bv"], g["L0_xattn_bo"]] + [g[L1 + n] for n in (
        "ln1_g", "ln1_b", "ln2_g", "ln2_b", "a1_li1_b", "a1_li3_b", "a2_li1_b", "a2_li3_b")]
    rc = [g["L2_ffn_bs"][0], g["L2_ffn_bs"][1], g["L3_xattn_bv"], wide(g["L2_ffn_expert_biases"].reshape(1, -1), DM)[0]]
    even = np.zeros((128, 1), np.float32)
    even.reshape(4, 2, 16)[:, 0] = 0.25
    odd = np.zeros((128, 1), np.float32)
    odd.reshape(4, 2, 16)[:, 1] = 0.25
    cols = [column(g["L0_xattn_bq"]), column(g["L0_xattn_bk"])]
    for a in ("a1", "a2"):
        cols += [column(g[L1 + f"{a}_{n}"]) for n in ("lnx_g", "lnx_b", "lny_g", "lny_b", "ln3_g", "ln3_b", "li2_b")]
    cols += [column(g["L3_xattn_bq"]), column(g["L3_xattn_bk"]), even, odd,
             np.broadcast_to(g["L0_ffn_temperature"].reshape(1, 1), (128, 1))]
    n = np.arange(128)
    consts = [np.eye(128), n[:, None] < n[None, :], n[:, None] > n[None, :], np.tile(np.arange(E1), (128, 1))]
    arrays = {
        "x": np.concatenate([g["x"], np.zeros_like(g["x"][0:2])]),
        "ctx": np.concatenate([g["ctx_512"], np.zeros_like(g["ctx_512"][0:2])]),
        "wa": np.concatenate(wa, 1), "wc": np.concatenate(wc, 1), "wi": np.concatenate(wi, 1),
        "ra": np.concatenate(ra), "rc": np.concatenate(rc), "cols": np.concatenate(cols, 1),
        "consts": np.concatenate([c.astype(np.float32) for c in consts], 1),
        "eg": np.concatenate([g["L1_ffn_w_gate"].reshape(E1, 2, 128, F1), g["L1_ffn_w_up"].reshape(E1, 2, 128, F1)], 3)
                .transpose(0, 2, 1, 3).reshape(E1, 128, 4 * F1),
        "ed": g["L1_ffn_w_down"].reshape(E1, 2, FH, DM).transpose(0, 2, 1, 3).reshape(E1, FH, 2 * DM),
        "tokens": np.arange(NT, dtype=np.uint32)[:, None],
    }
    arrays = {n: np.ascontiguousarray(a) for n, a in arrays.items()}
    assert arrays["wa"].shape[1] == WA_N and arrays["wc"].shape[1] == WC_N and arrays["cols"].shape[1] == CO_N
    nc = bacc.Bacc("TRN2", target_bir_lowering=False, num_devices=1)
    arrays = {f"in_{n}": a for n, a in arrays.items()}
    tensors = {n[3:]: nc.dram_tensor(n, a.shape, mybir.dt.from_np(a.dtype), kind="ExternalInput").ap() for n, a in arrays.items()}
    tensors["out"] = nc.dram_tensor("out", (NB, TQ, DM), F32, kind="ExternalOutput").ap()
    build(nc, tensors)
    return run(nc, [arrays], core_ids=[0]).results[0]["out"]
```

```python
from contextlib import ExitStack

import concourse.bass as bass
from concourse import mybir

ALU = mybir.AluOpType
ACT = mybir.ActivationFunctionType
F32 = mybir.dt.float32
I32 = mybir.dt.int32
U32 = mybir.dt.uint32
AX_X = mybir.AxisListType.X

NB, TQ, DM = 8, 112, 256
TK, DC, KP = 375, 128, 125
KJ = TK // KP
NT = NB * TQ
NH = 16
E0, E1, E2 = 8, 64, 16
TOP1 = 8
F1 = 192
FH = F1 // 2
CAP = 128
NSLOT = E1 * CAP
DROPPED = float(1 << 20)
RING = 4
EPS = 1e-5
MAGIC = float(0x5f3759df - (1 << 22) - (1 << 31))
CENTER = 0.36787944117144233
LOWER, UPPER = 0.21231792754821915, 0.5


TURN = "turn to the other slot"


def head_order(D):
    return list(range(NH)) if D == 32 else [8 * c + 2 * g + p for c in range(2) for p in range(2) for g in range(4)]


def layout(fields):
    at, out = 0, {}
    for name, n in fields:
        out[name] = (at, n)
        at += n
    return out, at


WA, WA_N = layout([("q0", 512), ("k0", 256), ("v0", 256), ("o0", 512), ("r0", 16)]
                  + [(f"e{e}", 1536) for e in range(E0)]
                  + [("q1", 1024), ("k1", 1024), ("v1", 1024), ("o1", 1024), ("f1", 2048), ("g1", 2048)]
                  + [("q2", 1024), ("k2", 512), ("v2", 512), ("o2", 1024), ("f2", 2048), ("g2", 2048)]
                  + [("r1", 128), ("s1", 768), ("d1", 512)])
WC, WC_N = layout([("q3", 512), ("k3", 256), ("v3", 256), ("o3", 512), ("c2", 32)]
                  + [(f"p{e}", 1024) for e in range(E2 // 2)]
                  + [("ws", 1024), ("br", 256), ("q4", 512), ("k4", 256), ("v4", 256)])
WI_N = 3 * 1536
RING_N = 1280
RA, RA_N = layout([(n, DM) for n in ("bv0", "bo0", "ln1g", "ln1b", "ln2g", "ln2b", "o1b", "g1b", "o2b", "g2b")])
RC, RC_N = layout([(n, DM) for n in ("bs0", "bs1", "bv4")] + [("ebias", DM)])
CO, CO_N = layout([("bq0", 2), ("bk0", 2), ("x1g", 2), ("x1b", 2), ("y1g", 2), ("y1b", 2), ("n1g", 2), ("n1b", 2),
                   ("f1b", 8), ("x2g", 2), ("x2b", 2), ("y2g", 1), ("y2b", 1), ("n2g", 2), ("n2b", 2), ("f2b", 8),
                   ("bq4", 2), ("bk4", 2), ("even", 1), ("odd", 1), ("temp", 1)])
CS, CS_N = layout([("ident", 128), ("before", 128), ("after", 128), ("iota", E1)])


class Signal:

    def __init__(self, sem, step=1):
        self.sem, self.step = sem, step
        self.restart()

    def restart(self):
        self.sent, self.seen = 0, {}

    def by(self, ins):
        self.sent += 1
        ins.then_inc(self.sem, self.step)

    def wait(self, eng, n=1):
        self.skip(eng, n)
        eng.wait_ge(self.sem, self.seen[eng.engine] * self.step)

    def skip(self, eng, n=1):
        self.seen[eng.engine] = self.seen.get(eng.engine, 0) + n



class Slot:
    pass


def build(nc, T):
    x_d = T["x"].rearrange("b t d -> (b t) d")
    ctx_d = T["ctx"].rearrange("b (j p) d -> b p j d", p=KP)
    out_d = T["out"].rearrange("b t d -> (b t) d")

    with ExitStack() as ctx:
        def sb(name, shape, dt=F32):
            return ctx.enter_context(nc.sbuf_tensor(name, shape, dt))

        def sem(name):
            return ctx.enter_context(nc.semaphore(name))

        def dram(name, shape, dt=F32):
            return nc.dram_tensor(name, shape, dt, kind="Internal").ap()

        xmid_d = dram("xmid", [NT + 2 * TQ, DM])
        xn1_d = dram("xn1", [NT, DM])
        token_d = dram("token", [NSLOT, 1], U32)
        y_d = dram("y", [NSLOT, DM])

        W = sb("W", [128, WA_N + RA_N])
        cols = sb("cols", [128, CO_N])
        consts = sb("consts", [128, CS_N])
        taken = sb("taken", [TQ, E1])
        ones = sb("ones", [TQ, TQ])
        rtemp = sb("rtemp", [TQ, 1])
        bqside = sb("bqside", [128, 2])
        slot_all = sb("slot_all", [TQ, (NB + 2) * TOP1], U32)
        gate_all = sb("gate_all", [TQ, (NB + 2) * TOP1])

        def w(name, a=None, table=WA):
            at, n = table[name]
            v = W[:, at:at + n]
            return v if a is None else v.rearrange("p (a b) -> p a b", a=a)

        def wc(name, a=None):
            return w(name, a, WC)

        def row(name, p=TQ, table=RA, base=WA_N):
            at, n = table[name]
            return W[0:p, base + at:base + at + n]

        INT0 = WC_N
        FLT0 = INT0 + WI_N
        RC0 = FLT0 + WI_N
        RING0 = RC0 + RC_N
        TOK0 = RING0 + RING * RING_N
        B0 = TOK0 + E1

        def work(n):
            nonlocal B0
            B0 += n
            assert B0 <= WA_N + RA_N
            return W[:, B0 - n:B0]
        ewg = [W[:, RING0 + r * RING_N:RING0 + r * RING_N + 768].rearrange("p (c n) -> p c n", c=2) for r in range(RING)]
        ewd = [W[0:FH, RING0 + r * RING_N + 768:RING0 + (r + 1) * RING_N].rearrange("p (c n) -> p c n", c=2) for r in range(RING)]
        expert_tokens = W[:, TOK0:TOK0 + E1].bitcast(U32)
        xg = [work(DM) for r in range(RING)]
        xidx = [work(1).bitcast(U32) for r in range(RING)]
        ey = [work(DM) for r in range(RING)]
        eT = [work(2 * CAP).rearrange("p (c t) -> p c t", c=2) for r in range(2)]
        eth, eh = [[work(2 * CAP)[0:FH].rearrange("p (c t) -> p c t", c=2) for r in range(2)] for _ in range(2)]
        ea = [work(2 * CAP)[0:FH].rearrange("p (c t) -> p c t", c=2) for r in range(2)]
        w3 = [W[:, FLT0 + 1536 * n:FLT0 + 1536 * (n + 1)] for n in range(3)]

        def col(name, c=0, p=128):
            at = CO[name][0] + c
            return cols[0:p, at:at + 1]

        def const(name):
            at, n = CS[name]
            return consts[:, at:at + n]
        ident = const("ident")

        banks = [ctx.enter_context(nc.psum_tensor(f"bank{n}", [128, 512], F32)) for n in range(8)]

        slots = []
        loop_sems = []
        for s in range(2):
            S = Slot()
            S.s = s
            slots.append(S)

            def signal(name, step=1):
                loop_sems.append(Signal(sem(f"{name}_{s}"), step))
                return loop_sems[-1]
            S.ctx_sums, S.ctxT_ready, S.z_ready, S.xn_ready = [
                signal(n) for n in ("ctx_sums", "ctxT_ready", "z_ready", "xn_ready")]
            S.xnT_sums, S.xnT_ready, S.proj_v_sums, S.proj_v_done = [
                signal(n) for n in ("xnT_sums", "xnT_ready", "proj_v_sums", "proj_v_done")]
            S.proj_s_sums, S.proj_s_done, S.score_sums, S.nmax_ready = [
                signal(n) for n in ("proj_s_sums", "proj_s_done", "score_sums", "nmax_ready")]
            S.probs_ready, S.probsT_sums, S.probsT_ready, S.av_sums = [
                signal(n) for n in ("probs_ready", "probsT_sums", "probsT_ready", "av_sums")]
            S.o_ready, S.oT_sums, S.oT_ready, S.out_sums = [
                signal(n) for n in ("o_ready", "oT_sums", "oT_ready", "out_sums")]
            S.gu_sums, S.tanh_ready, S.h_ready, S.down_sums = [
                signal(n) for n in ("gu_sums", "tanh_ready", "h_ready", "down_sums")]
            S.acc_done, S.f1_sums, S.gelu_ready, S.f2_sums = [
                signal(n) for n in ("acc_done", "f1_sums", "gelu_ready", "f2_sums")]
            S.logit_sums, S.logits_ready, S.exp_ready, S.mask_ready = [
                signal(n) for n in ("logit_sums", "logits_ready", "exp_ready", "mask_ready")]
            S.pos_sums, S.slots_ready, S.gate_ready, S.gateT_sums = [
                signal(n) for n in ("pos_sums", "slots_ready", "gate_ready", "gateT_sums")]
            S.gateT_ready, S.pair_sums, S.pair_done, S.x_ready = [
                signal(n) for n in ("gateT_ready", "pair_sums", "pair_done", "x_ready")]
            S.probsT_s_sums, S.probsT_s_ready = [signal(n) for n in ("probsT_s_sums", "probsT_s_ready")]
            S.xin_free, S.y8_free = [signal(n) for n in ("xin_free", "y8_free")]
            S.noted = signal("noted")
            S.vstep = signal("vector_chain")
            S.loaded, S.stored, S.tok_in = signal("loaded", 16), signal("stored", 16), signal("tok_in", 16)
            S.A, S.B, S.O, S.T = [banks[4 * s + n] for n in range(4)]
            f = lambda n, shape, dt=F32: sb(f"{n}_{s}", shape, dt)
            S.xin = f("xin", [TQ, DM])
            S.x, S.xn, S.x1, S.xo = f("x", [TQ, DM]), f("xn", [TQ, DM]), f("x1", [TQ, DM]), f("xo", [TQ, DM])
            S.xnT, S.ynT = f("xnT", [128, 2, TQ]), f("ynT", [128, 2, TQ])
            S.oc = f("oc", [128, 512])
            S.ctx = S.oc[0:KP, 0:KJ * DC].rearrange("p (j d) -> p j d", j=KJ)
            S.o = S.oc[0:TQ, :]
            S.yT = f("yT", [128, TK])
            S.kv = f("kv", [128, 4 * TK + KJ * 512])
            S.K = S.kv[:, 0:4 * TK].rearrange("p (c k) -> p c k", c=4)
            S.V = S.kv[:, 4 * TK:].rearrange("p (j n) -> p j n", j=KJ)
            S.hT = S.kv[:, 0:8 * TQ].rearrange("p (c t) -> p c t", c=8)
            S.th = S.kv[:, 8 * TQ:12 * TQ].rearrange("p (c t) -> p c t", c=4)
            S.a = [S.kv[:, n * TQ:(n + 2) * TQ].rearrange("p (c t) -> p c t", c=2) for n in (12, 14)]
            y0 = INT0 + s * TOP1 * DM
            S.y8 = W[0:TQ, y0:y0 + TOP1 * DM].rearrange("p (k d) -> p k d", k=TOP1)
            S.Q = f("Q", [128, 4, 4, TQ])
            S.P = f("P", [128, 2, TK])
            S.z = S.P[0:KP, :, :].rearrange("p a b -> p (a b)")[:, 0:KJ * DC].rearrange("p (j d) -> p j d", j=KJ)
            pt = f("PT", [128, 2 * KJ * TQ])
            S.PT = pt[:].rearrange("p (a j t) -> p a j t", a=2, j=KJ)
            S.ctxT = pt[:, 0:TK]
            S.Q1 = pt[:, TK:TK + 2 * TQ].rearrange("p (c t) -> p c t", c=2)
            S.oT = S.kv[:, 4 * TK + KJ * 512 - 4 * TQ:].rearrange("p (c t) -> p c t", c=4)
            S.st, S.mv, S.hv = f("st", [128, 6]), f("mv", [128, KJ + 1, 2]), f("hv", [128, KJ + 1])
            S.rstd, S.nt = f("rstd", [128, KJ + 1]), f("nt", [128, KJ + 1])
            S.nmax, S.rs, S.rinv = f("nmax", [TQ, NH]), f("rs", [TQ, NH]), f("rinv", [TQ, NH])
            S.r = [f(f"r{n}", [TQ, E1]) for n in range(4)]
            S.g8 = f("g8", [TQ, 8])
            S.i8 = f("i8", [TQ, 8], U32)
            S.slotf, S.idf, S.w8 = f("slotf", [TQ, 8]), f("idf", [TQ, 8]), f("w8", [TQ, 8])
            S.scat, S.slot = f("scat", [TQ, 8], U32), f("slotu", [TQ, 8], U32)
            S.tok = f("tok", [TQ, 1], U32)
            S.myscat = f("myscat", [TQ, 8], U32)
            S.myslot, S.myw = f("myslot", [TQ, 8], U32), f("myw", [TQ, 8])
            S.sc = f("sc", [TQ, 8])
            S.gT = f("gT", [E2, TQ])

        def scalar_turns(keys):
            return lambda h: keys == TK and h % 3 == 2

        def K_self(S):
            return S.kv[:, 0:4 * TQ].rearrange("p (c t) -> p c t", c=4)
        vstep = Signal(sem("vector_step"))
        arrived = Signal(sem("arrived"))
        loop_sems += [vstep, arrived]
        lo, hi = min(g.sem.num for g in loop_sems), max(g.sem.num for g in loop_sems)
        assert hi - lo + 1 == len(loop_sems)
        go = {e.engine: sem(f"go{n}") for n, e in enumerate((nc.sync, nc.tensor, nc.vector, nc.scalar))}
        const_in, vconst = sem("const_in"), sem("vconst")
        first_in, spare_in, notes = sem("first_in"), sem("spare_in"), sem("notes")
        w_in = {n: sem(f"w_in_{n}") for n in ("attn0", "ffn0", "attn1", "attn2", "route1")}
        wc_in, wi_in, w3_ready = sem("wc_in"), sem("wi_in"), sem("w3_ready")
        for S in slots:
            S.scattered, S.gathered = sem(f"scattered_{S.s}"), sem(f"gathered_{S.s}")
        rtemp_ready, bqside_ready = sem("rtemp_ready"), sem("bqside_ready")
        fetch_notes = [sem(f"fetch_notes{n}") for n in range(2)]
        slots_in = sem("slots_in")
        idx_ready = sem("idx_ready")
        ew_in = [sem(f"expert_w_in{r}") for r in range(RING)]
        xg_in = [sem(f"rows_in{r}") for r in range(RING)]
        rows_used = [sem(f"rows_used{r}") for r in range(RING)]
        y_out = [sem(f"y_out{r}") for r in range(RING)]
        eT_sums, eT_ready, egu_sums, etanh, eh_ready, ey_sums, ey_ready, ea_ready = [
            sem(n) for n in ("expert_xT_sums", "expert_xT_ready", "expert_gu_sums", "expert_tanh", "expert_h_ready",
                             "expert_y_sums", "expert_y_ready", "expert_a_ready")]

        steps = {}

        def restart():
            for g in loop_sems:
                g.restart()

        def iteration_end(eng):
            eng.drain().then_inc(arrived.sem, 1)
            eng.wait_ge(go[eng.engine], 1)
            eng.sem_clear(go[eng.engine])

        def run_pair(program, *args):
            programs = [program(S, *args) for S in slots]
            kinds = [[] for S in slots]
            while not kinds[0] or kinds[0][-1] is not None:
                todo = [S.s for S in slots]
                while todo:
                    for s in list(todo):
                        kind = next(programs[s], None)
                        if kind != TURN:
                            todo.remove(s)
                            kinds[s].append(kind)
            same = steps.setdefault(program.__name__, kinds)
            assert same == kinds, [(n, a, b) for n, (a, b) in enumerate(zip(same[0], kinds[0])) if a != b][:3]

        block = ctx.enter_context(nc.Block())

        @block.sync
        def _(sp):
            def refill(S, src, i, attentions):
                S.oT_ready.wait(sp, attentions)
                S.loaded.by(sp.dma_start(S.ctx, ctx_d[bass.ds(i * 2 + (2 + S.s), 1)].rearrange("o p j d -> (o p) j d")))
                S.xin_free.wait(sp)
                S.loaded.by(sp.dma_start(S.xin[:], src[bass.ds(i * 2 * TQ + (2 + S.s) * TQ, TQ), :]))

            def first(S, src):
                sp.dma_start(S.ctx, ctx_d[S.s]).then_inc(first_in, 16)
                sp.dma_start(S.xin[:], src[S.s * TQ:(S.s + 1) * TQ, :]).then_inc(first_in, 16)

            for S in slots:
                first(S, x_d)
            sp.dma_start(consts[:], T["consts"]).then_inc(const_in, 16)
            sp.dma_start(cols[:], T["cols"]).then_inc(const_in, 16)
            sp.dma_start(xmid_d[NT:NT + 2 * TQ, :], x_d[NT:NT + 2 * TQ, :]).then_inc(spare_in, 16)
            sp.wait_ge(spare_in, 16)
            restart()
            with sp.Fori(0, NB // 2) as i:
                for S in slots:
                    sp.wait_ge(S.scattered, i * 16 * TOP1 + 16)
                    S.tok_in.by(sp.dma_start(S.tok[:], T["tokens"][bass.ds(i * 2 * TQ + S.s * TQ, TQ), :]))
                for S in slots:
                    refill(S, x_d, i, 3)
                for S in slots:
                    S.slots_ready.wait(sp)
                    S.stored.by(sp.dma_start(xn1_d[bass.ds(i * 2 * TQ + S.s * TQ, TQ), :], S.xn[:]))
                for S in slots:
                    S.x_ready.wait(sp)
                    S.stored.by(sp.dma_start(xmid_d[bass.ds(i * 2 * TQ + S.s * TQ, TQ), :], S.x[:]))
                for S in slots:
                    S.loaded.wait(sp, 2)
                    S.stored.wait(sp, 2)
                iteration_end(sp)
            def expert_weights(r, e):
                one = not isinstance(e, int)
                for dst, src in ((ewg[r], T["eg"]), (ewd[r], T["ed"])):
                    src = src[bass.ds(e, 1)].rearrange("o p n -> (o p) n") if one else src[e]
                    sp.dma_start(dst.rearrange("p c n -> p (c n)"), src).then_inc(ew_in[r], 16)

            def store_y(r, i):
                sp.wait_ge(ey_ready, i * RING + r + 1)
                y3 = y_d.rearrange("(p e) d -> p e d", e=E1)
                e = i * RING + r
                dst = y3[:, e, :] if isinstance(i, int) else y3[:, bass.ds(e, 1), :].rearrange("p o d -> p (o d)")
                sp.dma_start(dst, ey[r]).then_inc(y_out[r], 16)
            for r in range(RING):
                expert_weights(r, r)
            sp.dma_start(W[:, INT0:INT0 + WI_N].bitcast(I32), T["wi"]).then_inc(wi_in, 16)
            sp.dma_start(W[:, 0:WC_N], T["wc"]).then_inc(wc_in, 16)
            sp.dma_start(W[:, RC0:RC0 + RC_N], T["rc"].partition_broadcast(128)).then_inc(wc_in, 16)
            for S in slots:
                first(S, xmid_d)
            with sp.Fori(0, E1 // RING - 1) as i:
                for r in range(RING):
                    sp.wait_ge(ey_sums, i * RING + r + 1)
                    expert_weights(r, i * RING + RING + r)
                    store_y(r, i)
            for r in range(RING):
                store_y(r, E1 // RING - 1)
            restart()
            with sp.Fori(0, NB // 2) as i:
                for S in slots:
                    refill(S, xmid_d, i, 1)
                for S in slots:
                    S.x_ready.wait(sp)
                    S.stored.by(sp.dma_start(out_d[bass.ds(i * 2 * TQ + S.s * TQ, TQ), :], S.x[:]))
                for S in slots:
                    S.loaded.wait(sp, 2)
                    S.stored.wait(sp)
                iteration_end(sp)

        @block.gpsimd
        def _(pool):
            def release():
                pool.drain()
                pool.wait_ge(arrived.sem, 4)
                pool.sem_clear(range(lo, hi + 1))
                for g in go.values():
                    pool.sem_inc(g, 1)

            zero = slots[0].P[:, 0, 0:NSLOT // 128].bitcast(U32)
            pool.memset(zero, 0).then_inc(vconst, 1)
            pool.memset(ones[:], 1.0).then_inc(vconst, 1)
            pool.wait_ge(vconst, 1)
            for S in slots:
                half = slice(S.s * NSLOT // 2, (S.s + 1) * NSLOT // 2)
                pool.dma_start(token_d[half].rearrange("(p c) o -> p (c o)", p=128), zero[:, 0:NSLOT // 256]).then_inc(S.scattered, 16)
            for S in slots:
                pool.wait_ge(S.scattered, 16)
            pool.memset(taken[:], 0.0).then_inc(vconst, 1)
            for S in slots:
                pool.memset(S.mv[:], 1.0).then_inc(vconst, 1)
                pool.memset(S.Q[:], 0.0).then_inc(vconst, 1)
            pool.memset(slot_all[:], 0).then_inc(notes, 1)
            pool.memset(gate_all[:], 0.0).then_inc(notes, 1)
            pool.wait_ge(notes, 2)

            def note(S, i):
                S.slots_ready.wait(pool)
                S.tok_in.wait(pool)
                at = bass.ds(i * 2 * TOP1 + S.s * TOP1, TOP1)
                pool.tensor_copy(slot_all[:, at], S.slot[:])
                pool.tensor_copy(gate_all[:, at], S.w8[:])
                S.noted.by(pool.tensor_copy(S.myscat[:], S.scat[:]))
                S.noted.wait(pool)

            def scatter(S):
                for k in range(TOP1):
                    pool.indirect_dma_start(
                        token_d, bass.IndirectOffsetOnAxis(ap=S.myscat[:, k:k + 1], axis=0), S.tok[:], None,
                        bounds_check=NSLOT - 1, oob_is_err=False).then_inc(S.scattered, 16)
            restart()
            with pool.Fori(0, NB // 2) as i:
                for S in slots:
                    note(S, i)
                release()
                for S in slots:
                    scatter(S)

            for S in slots:
                pool.wait_ge(S.scattered, 16 * TOP1 * (NB // 2) + 16)
            pool.dma_start(expert_tokens, token_d.rearrange("(p e) o -> p (e o)", e=E1)).then_inc(slots_in, 16)
            pool.wait_ge(slots_in, 16)

            def gather(r, at):
                pool.indirect_dma_start(xg[r], None, xn1_d, bass.IndirectOffsetOnAxis(ap=at, axis=0)).then_inc(xg_in[r], 16)
            for r in range(RING):
                gather(r, expert_tokens[:, r:r + 1])
            with pool.Fori(0, E1 // RING - 1) as i:
                for r in range(RING):
                    pool.tensor_copy(xidx[r], W[:, bass.ds(i * RING + (TOK0 + RING + r), 1)].bitcast(U32)).then_inc(idx_ready, 1)
                    pool.wait_ge(idx_ready, 1)
                    pool.sem_clear(idx_ready)
                    pool.wait_ge(rows_used[r], 1)
                    pool.sem_clear(rows_used[r])
                    gather(r, xidx[r])
            for r in range(RING):
                pool.wait_ge(y_out[r], 16 * (E1 // RING + 1))
            def fetch(S, batch):
                at = bass.ds(batch * TOP1, TOP1) if not isinstance(batch, int) else slice(batch * TOP1, (batch + 1) * TOP1)
                pool.tensor_copy(S.myslot[:], slot_all[:, at]).then_inc(fetch_notes[S.s], 1)
                pool.tensor_copy(S.myw[:], gate_all[:, at]).then_inc(fetch_notes[S.s], 1)
                pool.wait_ge(fetch_notes[S.s], 2)
                pool.sem_clear(fetch_notes[S.s])
                for k in range(TOP1):
                    pool.indirect_dma_start(
                        S.y8[:, k, :], None, y_d, bass.IndirectOffsetOnAxis(ap=S.myslot[:, k:k + 1], axis=0)
                    ).then_inc(S.gathered, 16)
            pool.wait_ge(w3_ready, 1)
            for S in slots:
                fetch(S, S.s)
            restart()
            with pool.Fori(0, NB // 2) as i:
                for S in slots:
                    S.y8_free.wait(pool)
                    fetch(S, i * 2 + (2 + S.s))
                release()
            for S in slots:
                pool.wait_ge(S.gathered, 16 * TOP1 * (NB // 2 + 1))

        @block.tensor
        def _(pe):
            def mm(out, pairs, close=True):
                last = None
                for n, (l, r) in enumerate(pairs):
                    last = nc.tensor.matmul(out, l, r, start=n == 0, stop=n == len(pairs) - 1)
                return last

            def keep_warm(S, bank, count):
                if S is slots[0]:
                    for _ in range(count):
                        nc.tensor.matmul(bank[:, 0:224], ident, consts[:, 0:224], start=True, stop=True)

            def transpose_x(S):
                S.xn_ready.wait(pe)
                for c in range(2):
                    last = nc.tensor.transpose(S.T[:, c * TQ:(c + 1) * TQ], S.xn[:, c * 128:(c + 1) * 128], ident[0:TQ, 0:TQ])
                S.xnT_sums.by(last)

            def transpose_context(S, rows, ready, n):
                if ready:
                    ready.wait(pe, n)
                for j in range(KJ):
                    last = nc.tensor.transpose(S.T[:, j * KP:(j + 1) * KP], rows[:, j, :], ident[0:KP, 0:KP])
                S.ctx_sums.by(last)

            def from_context(S, k, v):
                S.proj_s_sums.by(k([0])(S.A))
                S.proj_s_sums.by(k([1])(S.B))
                S.proj_v_sums.by(v([0, 1])(S.O))

            def queries(S, q, bank):
                S.proj_v_sums.by(q(bank, 0))
                S.proj_s_sums.by(q(S.T, 1))

            def from_rows(S, q, v, one=False):
                S.xnT_ready.wait(pe)
                S.proj_s_done.wait(pe)
                if one:
                    S.proj_v_sums.by(q(S.A))
                else:
                    queries(S, q, S.A)
                S.proj_s_done.wait(pe)
                S.proj_v_sums.by(v([2])(S.B))
                S.proj_v_done.wait(pe, 2)

            def from_context_wide(S, k, v):
                for n, make in enumerate([k([0]), k([1]), k([2]), k([3]), v([0]), v([1]), v([2])]):
                    if n >= 3:
                        S.proj_s_done.wait(pe)
                    S.proj_s_sums.by(make([S.A, S.B, S.T][n % 3]))
                S.proj_s_done.wait(pe, 2)

            def attention_weights(S, D, wq, wk, wv, wo, context, keys):
                nc_ = NH * D // 128
                rows = [(0, keys)] if keys == TQ else [(j * KP, KP) for j in range(KJ)]
                cchunks = 1 if wk.shape[1] == NH * D else 2
                wk3 = wk.rearrange("p (c n) -> p c n", c=cchunks)
                wv3 = wv.rearrange("p (c n) -> p c n", c=cchunks)
                wq3 = wq.rearrange("p (c n) -> p c n", c=2)
                con = (lambda c, a, n: context[:, a:a + n]) if cchunks == 1 else (lambda c, a, n: context[:, c, a:a + n])

                def q(bank, half):
                    for n, m in enumerate(range(half * nc_ // 2, (half + 1) * nc_ // 2)):
                        last = mm(bank[:, n * TQ:(n + 1) * TQ],
                                  [(wq3[:, c, m * 128:(m + 1) * 128], S.xnT[:, c, :]) for c in range(2)])
                    return last

                def k(ms):
                    def make(bank):
                        for n, m in enumerate(ms):
                            last = mm(bank[:, n * keys:(n + 1) * keys],
                                      [(wk3[:, c, m * 128:(m + 1) * 128], con(c, 0, keys)) for c in range(cchunks)])
                        return last
                    return make

                def v(js):
                    def make(bank):
                        for n, j in enumerate(js):
                            a, cnt = rows[j]
                            last = mm(bank[0:cnt, n * NH * D:(n + 1) * NH * D],
                                      [(con(c, a, cnt), wv3[:, c, :]) for c in range(cchunks)])
                        return last
                    return make
                return q, k, v

            def attention(S, D, wq, wk, wv, wo, context, keys):
                nc_ = NH * D // 128
                rows = [(0, keys)] if keys == TQ else [(j * KP, KP) for j in range(KJ)]
                q, k, v = attention_weights(S, D, wq, wk, wv, wo, context, keys)
                if keys == TQ:
                    S.xnT_ready.wait(pe)
                    S.proj_v_sums.by(q(S.A, 0))
                    S.proj_s_sums.by(k(range(nc_))(S.B))
                    S.proj_s_sums.by(q(S.T, 1))
                    S.proj_v_sums.by(v([0])(S.O))
                    S.proj_v_done.wait(pe)
                    S.proj_s_done.wait(pe)
                elif D == 16:
                    from_rows(S, q, v)
                else:
                    S.xnT_ready.wait(pe)
                    queries(S, q, S.B)
                    S.proj_v_done.wait(pe)
                    S.proj_s_done.wait(pe)

                order = head_order(D)

                def score(n):
                    h = order[n]
                    c, g, par = (h // 8, (h % 8) // 2, h % 2) if D == 16 else (h // 4, h % 4, 0)
                    bank = [S.A, S.B][n % 2]
                    S.score_sums.by(nc.tensor.matmul(bank[0:TQ, 0:keys], S.Q[:, 2 * par + c, g, :],
                                                     S.K[:, c, 0:keys] if keys == TK else K_self(S)[:, c, :],
                                                     start=True, stop=True))
                by_scalar = scalar_turns(keys)

                def turn(n):
                    S.probs_ready.wait(pe)
                    for j, (a, cnt) in enumerate(rows):
                        last = nc.tensor.transpose(S.T[0:cnt, j * TQ:(j + 1) * TQ], S.P[0:TQ, n % 2, a:a + cnt], ident[0:TQ, 0:TQ])
                    (S.probsT_s_sums if by_scalar(n) else S.probsT_sums).by(last)

                def av(n):
                    h = order[n]
                    (S.probsT_s_ready if by_scalar(n) else S.probsT_ready).wait(pe)
                    last = mm(S.O[0:TQ, h * D:(h + 1) * D],
                              [(S.PT[0:cnt, n % 2, j, :], S.V[0:cnt, j, h * D:(h + 1) * D]) for j, (a, cnt) in enumerate(rows)])
                    if n == NH - 1:
                        S.av_sums.by(last)
                score(0)
                if D == 16 or keys == TQ:
                    S.proj_v_done.wait(pe)
                score(1)
                S.proj_s_done.wait(pe)
                yield "proj"
                for n in range(NH):
                    if n >= 1:
                        av(n - 1)
                    turn(n)
                    if n + 2 < NH:
                        score(n + 2)
                    yield "head"
                av(NH - 1)
                yield "av"
                S.o_ready.wait(pe)
                for c in range(nc_):
                    last = nc.tensor.transpose(S.T[:, c * TQ:(c + 1) * TQ], S.o[:, c * 128:(c + 1) * 128], ident[0:TQ, 0:TQ])
                S.oT_sums.by(last)
                yield "turn"
                S.oT_ready.wait(pe)
                wo3 = wo.rearrange("p (c n) -> p c n", c=nc_)
                S.out_sums.by(mm(S.A[0:TQ, 0:DM], [(S.oT[:, c, :], wo3[:, c, :]) for c in range(nc_)]))
                yield "out"
                keep_warm(S, S.B, 7)
                transpose_x(S)
                yield "turn"

            def gate_up(S, groups, M, g):
                bank = [S.A, S.B][g % 2]
                for n in range(4):
                    wx = groups[g][n // 2]
                    last = mm(bank[0:M, n * TQ:(n + 1) * TQ],
                              [(wx[:, c, (n % 2) * M:(n % 2 + 1) * M], S.xnT[:, c, :]) for c in range(2)])
                S.gu_sums.by(last)

            def glu(S, groups, M, per_group):
                for g in range(len(groups)):
                    S.h_ready.wait(pe)
                    if per_group:
                        if g >= 2:
                            S.acc_done.wait(pe)
                        bank = [S.O, S.T][g % 2]
                        last = mm(bank[0:TQ, 0:DM], [(S.hT[0:M, 2 * (g % 2) + c, :], groups[g][2][0:M, c, :]) for c in range(2)])
                    else:
                        for c in range(2):
                            last = nc.tensor.matmul(S.O[0:TQ, 0:DM], S.hT[0:M, 2 * (g % 2) + c, :], groups[g][2][0:M, c, :],
                                                    start=g == 0 and c == 0, stop=g == len(groups) - 1 and c == 1)
                    S.down_sums.by(last)
                    if g + 2 < len(groups):
                        gate_up(S, groups, M, g + 2)
                    yield "glu"
                if per_group:
                    S.acc_done.skip(pe, 2)
                yield "end"
                if per_group:
                    keep_warm(S, S.B, 24)
                transpose_x(S)
                yield "turn"

            def mlp(S, w1, w2, context=None):
                S.xnT_ready.wait(pe)
                w13, w23 = w1.rearrange("p (c n) -> p c n", c=2), w2.rearrange("p (c n) -> p c n", c=8)
                for half in range(2):
                    for n in range(4):
                        m = 4 * half + n
                        last = mm([S.A, S.B][half][:, n * TQ:(n + 1) * TQ],
                                  [(w13[:, c, m * 128:(m + 1) * 128], S.xnT[:, c, :]) for c in range(2)])
                    S.f1_sums.by(last)
                yield "f1"
                for half in range(2):
                    S.gelu_ready.wait(pe)
                    for n in range(4):
                        m = 4 * half + n
                        last = nc.tensor.matmul(S.O[0:TQ, 0:DM], S.hT[:, m, :], w23[:, m, :], start=m == 0, stop=m == 7)
                S.f2_sums.by(last)
                yield "f2"
                if context:
                    pe.wait_ge(w_in["attn2"], 16)
                    from_context_wide(S, *attention_weights(S, *context)[1:])
                yield "context"
                if not context:
                    keep_warm(S, S.B, 7)
                transpose_x(S)
                yield "turn"

            def logits(S, wr, n):
                S.xnT_ready.wait(pe)
                w3_ = wr.rearrange("p (c n) -> p c n", c=2)
                S.logit_sums.by(mm(S.O[0:TQ, 0:n], [(S.xnT[:, c, :], w3_[:, c, :]) for c in range(2)]))

            def pair3(v, a):
                return v.rearrange("p (a b) -> p a b", a=a)

            def phase_a(S):
                transpose_context(S, S.ctx, None, 0)
                yield "ctx"
                S.ctxT_ready.wait(pe)
                pe.wait_ge(w_in["attn0"], 32)
                layer0 = 16, w("q0"), w("k0"), w("v0"), w("o0"), S.ctxT, TK
                from_context(S, *attention_weights(S, *layer0)[1:])
                yield "context"
                transpose_context(S, S.z, S.z_ready, 1)
                yield "end"
                S.ctxT_ready.wait(pe)
                transpose_x(S)
                yield "turn"
                yield from attention(S, *layer0)
                pe.wait_ge(w_in["ffn0"], 16)
                logits(S, w("r0"), E0)
                groups = [tuple(pair3(w(f"e{e}")[:, n * 512:(n + 1) * 512], 2) for n in range(3)) for e in range(E0)]
                gate_up(S, groups, 128, 0)
                gate_up(S, groups, 128, 1)
                yield "logits"
                yield "route"
                yield "route"
                yield from glu(S, groups, 128, True)
                pe.wait_ge(w_in["attn1"], 16)
                yield from attention(S, 32, w("q1"), w("k1"), w("v1"), w("o1"), S.ynT[:], TQ)
                cross = 32, w("q2"), w("k2"), w("v2"), w("o2"), S.yT, TK
                yield from mlp(S, w("f1"), w("g1"), cross)
                yield from attention(S, *cross)
                yield from mlp(S, w("f2"), w("g2"))
                pe.wait_ge(w_in["route1"], 16)
                logits(S, w("r1"), E1)
                s3, d3 = w("s1", 2), w("d1", 2)
                shared = [(s3[:, :, 0:F1], s3[:, :, F1:2 * F1], d3)]
                gate_up(S, shared, FH, 0)
                yield "logits"
                yield "route"
                S.mask_ready.wait(pe)
                S.pos_sums.by(mm(S.T[0:TQ, 0:E1], [(const("before")[0:TQ, 0:TQ], S.r[1][:]), (ones[:], S.r[3][:])]))
                yield "route"
                g = glu(S, shared, FH, False)
                yield next(g)
                yield next(g)

            pe.wait_ge(const_in, 32)
            pe.wait_ge(first_in, 64)
            pe.wait_ge(vconst, 7)
            restart()
            with pe.Fori(0, NB // 2) as i:
                run_pair(phase_a)
                iteration_end(pe)

            def turn_rows(r, i, n):
                pe.wait_ge(xg_in[r], i * 16 + 16 * n)
                bank = banks[r % 2]
                for c in range(2):
                    last = nc.tensor.transpose(bank[:, c * 128:(c + 1) * 128], xg[r][:, c * 128:(c + 1) * 128], ident)
                last.then_inc(eT_sums, 1)

            def free_rows(r, i):
                pe.wait_ge(eT_ready, i * RING + r + 1)
                nc.tensor.nop().then_inc(rows_used[r], 1)

            def expert_gate_up(r, i, n):
                pe.wait_ge(eT_ready, i * RING + RING * (n - 1) + r + 1)
                pe.wait_ge(ew_in[r], i * 32 + 32 * n)
                bank = banks[2 + r % 2]
                for m in range(4):
                    last = mm(bank[0:FH, m * 128:(m + 1) * 128],
                              [(ewg[r][:, c, m * FH:(m + 1) * FH], eT[r % 2][:, c, :]) for c in range(2)])
                last.then_inc(egu_sums, 1)

            def down(r, i, n):
                pe.wait_ge(eh_ready, i * RING + RING * (n - 1) + r + 1)
                last = mm(banks[4 + r % 2][:, 0:DM], [(eh[r % 2][:, c, :], ewd[r][:, c, :]) for c in range(2)])
                last.then_inc(ey_sums, 1)

            turn_rows(0, 0, 1)
            expert_gate_up(0, 0, 1)
            turn_rows(1, 0, 1)
            with pe.Fori(0, E1 // RING - 1) as i:
                for r in range(RING):
                    expert_gate_up((r + 1) % RING, i, 1 + (r + 1) // RING)
                    turn_rows((r + 2) % RING, i, 1 + (r + 2) // RING)
                    down(r, i, 1)
                    free_rows(r, i)
            for r in range(RING):
                if r + 1 < RING:
                    expert_gate_up(r + 1, E1 // RING - 1, 1)
                if r + 2 < RING:
                    turn_rows(r + 2, E1 // RING - 1, 1)
                down(r, E1 // RING - 1, 1)

            def experts2(S, n):
                if n == 3:
                    S.gateT_ready.wait(pe)
                if n >= 4:
                    S.pair_done.wait(pe)
                bank = [S.B, S.A, S.O, S.T][n % 4]
                if n < E2 // 2:
                    p3 = wc(f"p{n}", 2)
                    S.pair_sums.by(mm(bank[0:TQ, :], [(S.xnT[:, c, :], p3[:, c, :]) for c in range(2)]))
                elif n == E2 // 2:
                    ws = wc("ws", 4)
                    S.pair_sums.by(mm(bank[0:TQ, 0:DM], [(S.xnT[:, c % 2, :], ws[:, c, :]) for c in range(4)]))
                else:
                    S.pair_sums.by(mm(bank[0:TQ, 0:DM], [(S.gT[:], wc("br")[0:E2, :])]))

            def one_head_weights(S):
                wq, wk, wv = wc("q4", 2), wc("k4"), wc("v4")

                def q(bank):
                    for m in range(2):
                        last = mm(bank[:, m * TQ:(m + 1) * TQ],
                                  [(wq[:, c, m * 128:(m + 1) * 128], S.xnT[:, c, :]) for c in range(2)])
                    return last
                k = lambda ms: lambda bank: mm(bank[:, 0:TK], [(wk[:, ms[0] * 128:(ms[0] + 1) * 128], S.yT[:])])

                def v(js):
                    def make(bank):
                        for n, j in enumerate(js):
                            last = mm(bank[0:KP, n * DM:(n + 1) * DM], [(S.yT[:, j * KP:(j + 1) * KP], wv)])
                        return last
                    return make
                return q, k, v

            def attention_one(S):
                q, k, v = one_head_weights(S)
                from_rows(S, q, v, True)
                S.score_sums.by(mm(S.A[0:TQ, 0:TK], [(S.Q1[:, c, :], S.K[:, c, :]) for c in range(2)]))
                S.proj_v_done.wait(pe)
                yield "proj"
                S.probs_ready.wait(pe)
                for j in range(KJ):
                    last = nc.tensor.transpose(S.T[0:KP, j * TQ:(j + 1) * TQ], S.P[0:TQ, 0, j * KP:(j + 1) * KP], ident[0:TQ, 0:TQ])
                S.probsT_sums.by(last)
                yield "head"
                S.probsT_ready.wait(pe)
                S.av_sums.by(mm(S.O[0:TQ, 0:DM], [(S.PT[0:KP, 0, j, :], S.V[0:KP, j, 0:DM]) for j in range(KJ)]))
                yield "out"
                transpose_x(S)
                yield "turn"

            def phase_c(S):
                transpose_context(S, S.ctx, None, 0)
                yield "ctx"
                S.ctxT_ready.wait(pe)
                layer2 = 16, wc("q3"), wc("k3"), wc("v3"), wc("o3"), S.yT, TK
                from_context(S, *attention_weights(S, *layer2)[1:])
                yield "context"
                transpose_x(S)
                yield "turn"
                yield from attention(S, *layer2)
                logits(S, wc("c2"), E2)
                experts2(S, 0)
                experts2(S, 1)
                yield "logits"
                S.gate_ready.wait(pe)
                S.gateT_sums.by(nc.tensor.transpose(S.T[0:E2, 0:TQ], S.r[3][:, 0:E2], ident[0:TQ, 0:TQ]))
                yield "route"
                for n in range(E2 // 2 + 2):
                    if n + 2 < E2 // 2 + 2:
                        experts2(S, n + 2)
                    yield "pair"
                S.pair_done.wait(pe, 4)
                from_context(S, *one_head_weights(S)[1:])
                yield "context"
                transpose_x(S)
                yield "turn"
                yield from attention_one(S)
                pe.wait_ge(w3_ready, 1)
                S.xnT_ready.wait(pe)
                g3, u3 = w3[0].rearrange("p (c n) -> p c n", c=2), w3[1].rearrange("p (c n) -> p c n", c=2)
                d3 = w3[2].rearrange("p (c n) -> p c n", c=6)
                groups = [(g3[:, :, 256 * g:256 * g + 256], u3[:, :, 256 * g:256 * g + 256], d3[:, 2 * g:2 * g + 2, :])
                          for g in range(3)]
                gate_up(S, groups, 128, 0)
                gate_up(S, groups, 128, 1)
                yield "f1"
                down = glu(S, groups, 128, False)
                for n in range(4):
                    yield next(down)

            pe.wait_ge(first_in, 128)
            pe.wait_ge(wc_in, 32)
            restart()
            with pe.Fori(0, NB // 2) as i:
                run_pair(phase_c)
                iteration_end(pe)

        @block.scalar
        def _(act):
            def load(name, a, b):
                act.dma_start(W[:, a:b], T["wa"][:, a:b]).then_inc(w_in[name], 16)
            load("attn0", 0, WA["r0"][0])
            act.dma_start(W[:, WA_N:WA_N + RA_N], T["ra"].partition_broadcast(128)).then_inc(w_in["attn0"], 16)
            act.wait_ge(first_in, 64)
            act.wait_ge(const_in, 32)
            load("ffn0", WA["r0"][0], WA["q1"][0])
            load("attn1", WA["q1"][0], WA["q2"][0])
            load("attn2", WA["q2"][0], WA["r1"][0])
            load("route1", WA["r1"][0], WA_N)

            def keys(S, bank, out, bias):
                S.proj_s_sums.wait(act)
                if bias is None:
                    S.proj_s_done.by(nc.scalar.activation(out, bank[:, 0:TK], ACT.Copy))
                else:
                    S.proj_s_done.by(nc.scalar.activation(out, bank[:, 0:TK], ACT.Identity, bias=bias))

            def softmax(S, heads, nkeys, D):
                order = head_order(D) if heads == NH else [0]

                def exp(n):
                    S.nmax_ready.wait(act)
                    S.probs_ready.by(nc.scalar.activation(
                        S.P[0:TQ, n % 2, 0:nkeys], [S.A, S.B][n % 2][0:TQ, 0:nkeys], ACT.Exp,
                        bias=S.nmax[:, n:n + 1], accum_out=S.rs[:, order[n]:order[n] + 1]))
                by_scalar = scalar_turns(nkeys)
                for n in range(min(heads, 2)):
                    exp(n)
                yield "proj"
                for n in range(heads):
                    if by_scalar(n):
                        S.probsT_s_sums.wait(act)
                        S.probsT_s_ready.by(nc.scalar.activation(
                            S.PT[0:KP, n % 2, :, :], S.T[0:KP, 0:KJ * TQ].rearrange("p (j t) -> p j t", j=KJ), ACT.Copy))
                    if n + 2 < heads:
                        exp(n + 2)
                    yield "head"
                if heads == NH:
                    yield "av"
                    yield "turn"
                yield "out"
                yield "turn"

            def tanh(S, g, M):
                S.gu_sums.wait(act)
                bank = [S.A, S.B][g % 2]
                S.tanh_ready.by(nc.scalar.activation(S.th[0:M, 2 * (g % 2):2 * (g % 2) + 2, :],
                                                     bank[0:M, 0:2 * TQ].rearrange("p (c t) -> p c t", c=2), ACT.Tanh, scale=0.5))

            def glu(S, groups, M):
                for g in range(groups):
                    if g + 2 < groups:
                        tanh(S, g + 2, M)
                    yield "glu"
                yield "end"
                yield "turn"

            def queries(S, D, scale=None, bias=None):
                S.proj_s_sums.wait(act)
                for g in range(4):
                    lanes = slice(32 * g, 32 * g + 32)
                    if D == 32:
                        last = nc.scalar.activation(S.Q[lanes, 2:4, g, :], S.T[lanes, 0:2 * TQ].rearrange("p (c t) -> p c t", c=2),
                                                    ACT.Copy, scale=scale)
                    else:
                        for par, side in enumerate(("even", "odd")):
                            side = cols[lanes, CO[side][0]:CO[side][0] + 1]
                            out, src = S.Q[lanes, 2 * par + 1, g, :], S.T[lanes, 0:TQ]
                            if bias is not None:
                                last = nc.scalar.activation(out, src, ACT.Identity, scale=side, bias=bias[lanes, par:par + 1])
                            else:
                                last = nc.scalar.activation(out, src, ACT.Copy, scale=side)
                S.proj_s_done.by(last)

            def both_keys(S, bias):
                for m in range(2):
                    keys(S, [S.A, S.B][m], S.K[:, m, :], bias and col(bias, m))
                yield "context"

            def gelu(S, bias, context=False):
                for half in range(2):
                    S.f1_sums.wait(act)
                    for n in range(4):
                        m = 4 * half + n
                        last = nc.scalar.activation(S.hT[:, m, :], [S.A, S.B][half][:, n * TQ:(n + 1) * TQ], ACT.Gelu,
                                                    bias=col(bias, m))
                    S.gelu_ready.by(last)
                yield "f1"
                yield "f2"
                if context:
                    for m in range(4):
                        keys(S, [S.A, S.B, S.T][m % 3], S.K[:, m, :], None)
                    for j in range(KJ):
                        S.proj_s_sums.wait(act)
                        S.proj_s_done.by(nc.scalar.activation(
                            S.V[0:KP, j, :], [S.A, S.B, S.T][(4 + j) % 3][0:KP, :], ACT.Copy))
                yield "context"
                yield "turn"

            def phase_a(S):
                yield "ctx"
                yield from both_keys(S, "bk0")
                yield "end"
                yield "turn"
                queries(S, 16, None, bqside)
                yield from softmax(S, NH, TK, 16)
                S.logits_ready.wait(act)
                S.exp_ready.by(nc.scalar.activation(S.r[1][:, 0:E0], S.r[0][:, 0:E0], ACT.Tanh, scale=0.5))
                tanh(S, 0, 128)
                tanh(S, 1, 128)
                yield "logits"
                S.logits_ready.wait(act)
                nc.scalar.activation(S.r[2][:, 0:E0], S.r[0][:, 0:E0], ACT.Exp, scale=-1.0 / 0.1)
                S.exp_ready.by(nc.scalar.activation(S.r[3][:, 0:E0], S.r[0][:, 0:E0], ACT.Exp, scale=-1.0 / 0.3))
                yield "route"
                yield "route"
                yield from glu(S, E0, 128)
                S.proj_s_sums.wait(act)
                S.proj_s_done.by(nc.scalar.activation(K_self(S), S.B[:, 0:4 * TQ].rearrange("p (c t) -> p c t", c=4), ACT.Copy))
                queries(S, 32, 32.0 ** -0.5)
                yield from softmax(S, NH, TQ, 32)
                yield from gelu(S, "f1b", True)
                queries(S, 32, 32.0 ** -0.5)
                yield from softmax(S, NH, TK, 32)
                yield from gelu(S, "f2b")
                S.logits_ready.wait(act)
                S.exp_ready.by(nc.scalar.activation(S.r[0][:], S.O[0:TQ, 0:E1], ACT.Exp, bias=S.sc[:, 0:1], accum_out=S.sc[:, 1:2]))
                tanh(S, 0, FH)
                yield "logits"
                yield "route"
                yield "route"
                yield "glu"
                yield "end"

            act.wait_ge(const_in, 32)
            act.wait_ge(bqside_ready, 2)
            restart()
            with act.Fori(0, NB // 2) as i:
                run_pair(phase_a)
                iteration_end(act)

            def expert(r, i):
                act.wait_ge(egu_sums, i * RING + r + 1)
                nc.scalar.activation(eth[r % 2], banks[2 + r % 2][0:FH, 0:256].rearrange("p (c t) -> p c t", c=2),
                                     ACT.Tanh, scale=0.5).then_inc(etanh, 1)

            def output(r, i):
                act.wait_ge(ey_sums, i * RING + r + 1)
                act.wait_ge(y_out[r], i * 16 + 16)
                nc.scalar.activation(ey[r], banks[4 + r % 2][:, 0:DM], ACT.Copy).then_inc(ey_ready, 1)

            for r in range(RING):
                act.sem_inc(y_out[r], 16)
            expert(0, 0)
            with act.Fori(0, E1 // RING - 1) as i:
                for r in range(RING):
                    if r + 1 < RING:
                        expert(r + 1, i)
                    else:
                        expert(0, i + 1)
                    output(r, i)
            for r in range(RING):
                if r + 1 < RING:
                    expert(r + 1, E1 // RING - 1)
                output(r, E1 // RING - 1)
            def phase_c(S):
                yield "ctx"
                yield from both_keys(S, None)
                yield "turn"
                queries(S, 16)
                yield from softmax(S, NH, TK, 16)
                S.logits_ready.wait(act)
                S.exp_ready.by(nc.scalar.activation(S.r[0][:, 0:E2], S.r[1][:, 0:E2], ACT.Exp, bias=S.sc[:, 0:1], accum_out=S.sc[:, 1:2]))
                yield "logits"
                yield "route"
                for n in range(E2 // 2 + 2):
                    yield "pair"
                yield from both_keys(S, "bk4")
                yield "turn"
                yield from softmax(S, 1, TK, DM)
                tanh(S, 0, 128)
                tanh(S, 1, 128)
                yield "f1"
                down = glu(S, 3, 128)
                for n in range(4):
                    yield next(down)

            restart()
            with act.Fori(0, NB // 2) as i:
                run_pair(phase_c)
                iteration_end(act)

        @block.vector
        def _(v):
            def now(ins):
                vstep.by(ins)
                vstep.wait(v)

            def then(S, ins):
                S.vstep.by(ins)
                yield TURN
                S.vstep.wait(v)

            def inverse_std(S, p, n):
                var, hv, y, t = S.mv[0:p, 0:n, 1], S.hv[0:p, 0:n], S.rstd[0:p, 0:n], S.nt[0:p, 0:n]
                yield from then(S, v.tensor_scalar(hv, var, EPS, 0.5, ALU.add, ALU.mult))
                yield from then(S, v.tensor_scalar(y.bitcast(I32), hv.bitcast(I32), -0.5, MAGIC, ALU.mult, ALU.add))
                for _ in range(3):
                    if n == 1:
                        yield from then(S, v.scalar_tensor_tensor(t, y, hv, y, ALU.mult, ALU.mult))
                    else:
                        yield from then(S, v.tensor_tensor(t, y, y, ALU.mult))
                        yield from then(S, v.tensor_tensor(t, t, hv, ALU.mult))
                    yield from then(S, v.scalar_tensor_tensor(y, t, 1.5, y, ALU.subtract, ALU.mult))

            def normalise(S, src, dst):
                yield from then(S, v.bn_stats(S.st[0:TQ, :], src))
                yield from then(S, v.bn_aggr(S.mv[0:TQ, 0, :], S.st[0:TQ, :]))
                yield from inverse_std(S, TQ, 1)
                return v.tensor_scalar(dst, src, S.mv[0:TQ, 0, 0:1], S.rstd[0:TQ, 0:1], ALU.subtract, ALU.mult)

            def norm(S, src):
                S.xn_ready.by((yield from normalise(S, src, S.xn[:])))

            def turned_x(S, affine=()):
                S.xnT_sums.wait(v)
                if not affine:
                    last = v.tensor_copy(S.xnT[:], S.T[:, 0:2 * TQ].rearrange("p (c t) -> p c t", c=2))
                for dst, g, b in affine:
                    for c in range(2):
                        last = v.tensor_scalar(dst[:, c, :], S.T[:, c * TQ:(c + 1) * TQ], col(g, c), col(b, c), ALU.mult, ALU.add)
                S.xnT_ready.by(last)

            def queries(S, D, bias, scale, bank=None):
                bank = S.A if bank is None else bank
                S.proj_v_sums.wait(v)
                if D == 16:
                    for g in range(4):
                        lanes = slice(32 * g, 32 * g + 32)
                        for par, side in enumerate(("even", "odd")):
                            side = cols[lanes, CO[side][0]:CO[side][0] + 1]
                            out, src = S.Q[lanes, 2 * par, g, :], bank[lanes, 0:TQ]
                            if bias:
                                at = CO[bias][0]
                                last = v.tensor_scalar(out, src, cols[lanes, at:at + 1], side, ALU.add, ALU.mult)
                            else:
                                last = v.tensor_scalar(out, src, side, None, ALU.mult)
                elif D == 32:
                    for g in range(4):
                        lanes = slice(32 * g, 32 * g + 32)
                        last = v.tensor_scalar(S.Q[lanes, 0:2, g, :], bank[lanes, 0:2 * TQ].rearrange("p (c t) -> p c t", c=2),
                                               scale, None, ALU.mult)
                else:
                    for c in range(2):
                        last = v.tensor_scalar(S.Q1[:, c, :], bank[:, c * TQ:(c + 1) * TQ], col(bias, c), None, ALU.add)
                S.proj_v_done.by(last)

            def values(S, js, width, bank, p, bias=None):
                S.proj_v_sums.wait(v)
                src = bank[0:p, 0:len(js) * width].rearrange("p (j n) -> p j n", j=len(js))
                dst = S.V[0:p, js[0]:js[-1] + 1, 0:width]
                if bias is None:
                    last = v.tensor_copy(dst, src)
                else:
                    for n in range(len(js)):
                        last = v.tensor_tensor(dst[:, n, :], src[:, n, :], bias, ALU.add)
                S.proj_v_done.by(last)

            def heads(S, D, nkeys, nheads=NH):
                rows = [(0, nkeys)] if nkeys == TQ else [(j * KP, KP) for j in range(KJ)]
                p = rows[0][1]

                def nmax(h):
                    S.score_sums.wait(v)
                    S.nmax_ready.by(v.tensor_reduce(S.nmax[:, h:h + 1], [S.A, S.B][h % 2][0:TQ, 0:nkeys], AX_X, ALU.max, negate=True))

                def turned(h):
                    S.probsT_sums.wait(v)
                    if nkeys == TQ:
                        last = v.tensor_tensor(S.PT[0:TQ, h % 2, 0, :], S.T[0:TQ, 0:TQ], const("after")[0:TQ, 0:TQ], ALU.mult)
                    else:
                        last = v.tensor_copy(S.PT[0:p, h % 2, :, :], S.T[0:p, 0:KJ * TQ].rearrange("p (j t) -> p j t", j=KJ))
                    S.probsT_ready.by(last)
                by_scalar = scalar_turns(nkeys)
                for h in range(min(nheads, 2)):
                    nmax(h)
                yield "proj"
                for h in range(nheads):
                    if not by_scalar(h):
                        turned(h)
                    if h + 2 < nheads:
                        nmax(h + 2)
                    yield "head"
                S.av_sums.wait(v)
                now(v.reciprocal(S.rinv[:, 0:nheads], S.rs[:, 0:nheads]))

            def attention_end(S, D):
                n = NH * D
                S.o_ready.by(v.tensor_tensor(S.o[:, 0:n].rearrange("p (h d) -> p h d", h=NH),
                                             S.O[0:TQ, 0:n].rearrange("p (h d) -> p h d", h=NH),
                                             S.rinv[:].unsqueeze(2).broadcast_to([TQ, NH, D]), ALU.mult))
                yield "av"
                S.oT_sums.wait(v)
                c = n // 128
                S.oT_ready.by(v.tensor_copy(S.oT[:, 0:c, :], S.T[:, 0:c * TQ].rearrange("p (c t) -> p c t", c=c)))
                yield "turn"
                S.out_sums.wait(v)

            def gated(S, g, M):
                bank = [S.A, S.B][g % 2]
                gate, up = [bank[0:M, n * 2 * TQ:(n + 1) * 2 * TQ].rearrange("p (c t) -> p c t", c=2) for n in range(2)]
                chunks = slice(2 * (g % 2), 2 * (g % 2) + 2)
                a = S.a[g % 2][0:M]
                S.tanh_ready.wait(v)
                now(v.scalar_tensor_tensor(a, S.th[0:M, chunks, :], 1.0, gate, ALU.add, ALU.mult))
                S.h_ready.by(v.scalar_tensor_tensor(S.hT[0:M, chunks, :], a, 0.5, up, ALU.mult, ALU.mult))

            def glu(S, groups, M, per_group, weights=None, ahead=0):
                def added(g):
                    S.down_sums.wait(v)
                    if per_group:
                        ins = v.scalar_tensor_tensor(S.x[:], [S.O, S.T][g % 2][0:TQ, 0:DM], weights[:, g:g + 1], S.x[:], ALU.mult, ALU.add)
                        S.acc_done.by(ins)
                        S.acc_done.wait(v)
                    elif g == groups - 1:
                        now(v.tensor_tensor(S.x[:], S.x[:], S.O[0:TQ, 0:DM], ALU.add))
                for g in range(groups):
                    if g >= ahead:
                        gated(S, g, M)
                    if g >= 1:
                        added(g - 1)
                    yield "glu"
                added(groups - 1)

            def top_mask(S, src, n, k, mask):
                v8 = S.g8[:]
                if k < 8:
                    yield from then(S, v.memset(src[:, n:n + 8], -1.0))
                    yield from then(S, v.max(v8, src[:, 0:n + 8]))
                    yield from then(S, v.memset(v8[:, k:8], -1.0))
                    width = n + 8
                else:
                    yield from then(S, v.max(v8, src))
                    width = n
                yield from then(S, v.match_replace(mask[:, 0:width], v8, src[:, 0:width], -2.0))
                yield from then(S, v.tensor_scalar(mask[:, 0:n], mask[:, 0:n], -2.0, None, ALU.is_equal))

            def reduce(S, out, src):
                yield from then(S, v.tensor_reduce(out, src, AX_X, ALU.add))

            def route0(S):
                r0, r1, r2, r3 = [t[:, 0:E0] for t in S.r]
                c = lambda n: S.sc[:, n:n + 1]
                S.logit_sums.wait(v)
                S.logits_ready.by(v.tensor_scalar(r0, S.O[0:TQ, 0:E0], rtemp[:], None, ALU.mult))
                yield "logits"
                S.exp_ready.wait(v)
                yield from then(S, v.tensor_scalar(r1, r1, 0.5, 0.5, ALU.mult, ALU.add))
                yield from then(S, v.tensor_scalar(r2, r1, CENTER, None, ALU.subtract))
                S.logits_ready.by(v.scalar_tensor_tensor(r0, r2, -1.0, r2, ALU.mult, ALU.max))
                yield from then(S, v.tensor_scalar(S.idf[:], r1, LOWER, None, ALU.is_ge))
                yield from then(S, v.scalar_tensor_tensor(S.idf[:], r1, UPPER, S.idf[:], ALU.is_le, ALU.mult))
                gated(S, 0, 128)
                gated(S, 1, 128)
                yield "route"
                S.exp_ready.wait(v)
                yield from then(S, v.tensor_tensor(S.w8[:], r2, S.idf[:], ALU.mult))
                yield from reduce(S, c(0), S.w8[:])
                yield from then(S, v.tensor_scalar(c(0), c(0), 1e-8, None, ALU.is_lt))
                yield from top_mask(S, S.r[3][:], E0, 2, S.r[1][:])
                yield from then(S, v.tensor_tensor(r3, r3, r1, ALU.mult))
                yield from reduce(S, c(1), r3)
                yield from then(S, v.tensor_scalar(c(1), c(1), 1e-8, None, ALU.max))
                yield from then(S, v.reciprocal(c(1), c(1)))
                yield from then(S, v.tensor_scalar(r3, r3, c(1), None, ALU.mult))
                yield from then(S, v.tensor_tensor(r3, r3, S.w8[:], ALU.subtract))
                yield from then(S, v.scalar_tensor_tensor(S.w8[:], r3, c(0), S.w8[:], ALU.mult, ALU.add))
                yield from reduce(S, c(2), S.w8[:])
                yield from then(S, v.tensor_scalar(c(2), c(2), 1e-8, None, ALU.max))
                yield from then(S, v.reciprocal(c(2), c(2)))
                yield from then(S, v.tensor_scalar(S.w8[:], S.w8[:], c(2), None, ALU.mult))
                yield "route"

            def route1(S):
                S.logit_sums.wait(v)
                S.logits_ready.by(v.tensor_reduce(S.sc[:, 0:1], S.O[0:TQ, 0:E1], AX_X, ALU.max, negate=True))
                yield "logits"
                S.exp_ready.wait(v)
                yield from then(S, v.reciprocal(S.sc[:, 2:3], S.sc[:, 1:2]))
                yield from then(S, v.tensor_scalar(S.r[0][:], S.r[0][:], S.sc[:, 2:3], None, ALU.mult))
                yield from then(S, v.max(S.g8[:], S.r[0][:]))
                yield from then(S, v.match_replace(S.r[1][:], S.g8[:], S.r[0][:], -2.0))
                yield from then(S, v.tensor_scalar(S.r[1][:], S.r[1][:], -2.0, None, ALU.is_equal))
                now(v.tensor_copy(S.r[3][:], taken[:]))
                ins = v.tensor_tensor(taken[:], taken[:], S.r[1][:], ALU.add)
                S.mask_ready.by(ins)
                S.mask_ready.wait(v)
                yield from then(S, v.max_index(S.i8[:], S.g8[:], S.r[0][:]))
                yield from reduce(S, S.sc[:, 3:4], S.g8[:])
                yield from then(S, v.reciprocal(S.sc[:, 3:4], S.sc[:, 3:4]))
                yield from then(S, v.tensor_scalar(S.w8[:], S.g8[:], S.sc[:, 3:4], None, ALU.mult))
                yield from then(S, v.tensor_copy(S.idf[:], S.i8[:]))
                yield "route"
                S.pos_sums.wait(v)
                yield from then(S, v.tensor_scalar(S.r[0][:], S.T[0:TQ, 0:E1], float(CAP), DROPPED, ALU.is_ge, ALU.mult))
                yield from then(S, v.scalar_tensor_tensor(S.r[2][:], S.T[0:TQ, 0:E1], float(E1), S.r[0][:], ALU.mult, ALU.add))
                yield from then(S, v.tensor_tensor(S.r[2][:], S.r[2][:], const("iota")[0:TQ, :], ALU.add))
                for k in range(TOP1):
                    yield from then(S, v.scalar_tensor_tensor(S.r[0][:], const("iota")[0:TQ, :], S.idf[:, k:k + 1], S.r[2][:],
                                                ALU.is_equal, ALU.mult, accum_out=S.slotf[:, k:k + 1]))
                yield from then(S, v.tensor_copy(S.scat[:], S.slotf[:]))
                yield from then(S, v.tensor_scalar(S.idf[:], S.slotf[:], float(NSLOT), None, ALU.is_lt))
                yield from then(S, v.tensor_tensor(S.w8[:], S.w8[:], S.idf[:], ALU.mult))
                yield from then(S, v.tensor_tensor(S.slotf[:], S.slotf[:], S.idf[:], ALU.mult))
                S.slots_ready.by(v.tensor_copy(S.slot[:], S.slotf[:]))
                yield "route"

            def block1(S, n, keys):
                S.vstep.wait(v)
                yield from heads(S, 32, keys)
                yield from attention_end(S, 32)
                yield from then(S, v.tensor_tensor(S.xo[:], S.xo[:], S.A[0:TQ, 0:DM], ALU.add))
                yield from norm(S, S.xo[:])
                yield "out"
                turned_x(S, [(S.xnT, f"n{n}g", f"n{n}b")])
                yield "turn"
                now(v.tensor_tensor(S.xo[:], S.xo[:], S.x1[:], ALU.add))
                now(v.tensor_tensor(S.xo[:], S.xo[:], row(f"g{n}b"), ALU.add))
                yield "f1"
                S.f2_sums.wait(v)
                yield from then(S, v.tensor_tensor(S.xo[:], S.xo[:], S.O[0:TQ, 0:DM], ALU.add))

            def own_norm(S, src, g, b):
                yield from then(S, (yield from normalise(S, src, S.x1[:])))
                yield from then(S, v.tensor_tensor(S.x1[:], S.x1[:], row(g), ALU.mult))
                yield from then(S, v.tensor_tensor(S.x1[:], S.x1[:], row(b), ALU.add))
                yield from norm(S, S.x1[:])

            def phase_a(S):
                S.ctx_sums.wait(v)
                S.ctxT_ready.by(v.tensor_copy(S.ctxT[:], S.T[:, 0:TK]))
                for j in range(KJ):
                    yield from then(S, v.bn_stats(S.st[0:KP, :], S.ctx[:, j, :]))
                    yield from then(S, v.bn_aggr(S.mv[0:KP, j, :], S.st[0:KP, :]))
                yield from then(S, v.bn_stats(S.st[0:TQ, :], S.xin[:]))
                yield from then(S, v.bn_aggr(S.mv[0:TQ, KJ, :], S.st[0:TQ, :]))
                yield from inverse_std(S, KP, KJ + 1)
                for j in range(KJ):
                    ins = v.tensor_scalar(S.z[:, j, :], S.ctx[:, j, :], S.mv[0:KP, j, 0:1], S.rstd[0:KP, j:j + 1],
                                          ALU.subtract, ALU.mult)
                S.z_ready.by(ins)
                S.xn_ready.by(v.tensor_scalar(S.xn[:], S.xin[:], S.mv[0:TQ, KJ, 0:1], S.rstd[0:TQ, KJ:KJ + 1],
                                              ALU.subtract, ALU.mult))
                yield "ctx"
                yield "context"
                S.ctx_sums.wait(v)
                S.ctxT_ready.by(v.tensor_scalar(S.yT[:], S.T[:, 0:TK], col("y2g"), col("y2b"), ALU.mult, ALU.add))
                yield "end"
                turned_x(S)
                yield "turn"
                v.wait_ge(w_in["attn0"], 32)
                S.xin_free.by(v.tensor_tensor(S.x[:], S.xin[:], row("bo0"), ALU.add))
                S.xin_free.wait(v)
                values(S, [0, 1], DM, S.O, KP, row("bv0", KP))
                queries(S, 16, "bq0", 0.25)
                values(S, [2], DM, S.B, KP, row("bv0", KP))
                yield from heads(S, 16, TK)
                yield from attention_end(S, 16)
                yield from then(S, v.tensor_tensor(S.x[:], S.x[:], S.A[0:TQ, 0:DM], ALU.add))
                yield from norm(S, S.x[:])
                yield "out"
                turned_x(S)
                yield "turn"
                yield from route0(S)
                yield from glu(S, E0, 128, True, S.w8, 2)
                yield from then(S, (yield from normalise(S, S.x[:], S.xo[:])))
                yield from own_norm(S, S.xo[:], "ln1g", "ln1b")
                yield "end"
                turned_x(S, [(S.xnT, "x1g", "x1b"), (S.ynT, "y1g", "y1b")])
                yield "turn"
                S.vstep.by(v.tensor_tensor(S.xo[:], S.x1[:], row("o1b"), ALU.add))
                queries(S, 32, None, 32.0 ** -0.5)
                values(S, [0], 512, S.O, TQ)
                yield from block1(S, 1, TQ)
                yield from own_norm(S, S.xo[:], "ln2g", "ln2b")
                yield "f2"
                yield "context"
                turned_x(S, [(S.xnT, "x2g", "x2b")])
                yield "turn"
                S.vstep.by(v.tensor_tensor(S.xo[:], S.x1[:], row("o2b"), ALU.add))
                queries(S, 32, None, 32.0 ** -0.5, S.B)
                yield from block1(S, 2, TK)
                yield from then(S, v.tensor_tensor(S.x[:], S.x[:], S.xo[:], ALU.add))
                yield from norm(S, S.x[:])
                yield "f2"
                yield "context"
                turned_x(S)
                yield "turn"
                yield from route1(S)
                yield from glu(S, 1, FH, False)
                S.x_ready.by(v.tensor_copy(S.sc[:, 0:1], S.x[:, 0:1]))
                yield "end"

            v.wait_ge(const_in, 32)
            v.wait_ge(first_in, 64)
            v.wait_ge(vconst, 7)
            for n, side in enumerate(("even", "odd")):
                v.tensor_scalar(bqside[:, n:n + 1], col("bq0", 1), col(side), None, ALU.mult).then_inc(bqside_ready, 1)
            v.reciprocal(rtemp[:], col("temp", p=TQ)).then_inc(rtemp_ready, 1)
            v.wait_ge(rtemp_ready, 1)
            restart()
            with v.Fori(0, NB // 2) as i:
                run_pair(phase_a)
                iteration_end(v)

            def rows(r, i, n):
                v.wait_ge(eT_sums, i * RING + RING * (n - 1) + r + 1)
                v.tensor_copy(eT[r % 2], banks[r % 2][:, 0:256].rearrange("p (c t) -> p c t", c=2)).then_inc(eT_ready, 1)

            def hidden(r, i):
                gate, up = [banks[2 + r % 2][0:FH, n * 256:(n + 1) * 256].rearrange("p (c t) -> p c t", c=2) for n in range(2)]
                v.wait_ge(etanh, i * RING + r + 1)
                v.scalar_tensor_tensor(ea[r % 2], eth[r % 2], 1.0, gate, ALU.add, ALU.mult).then_inc(ea_ready, 1)
                v.wait_ge(ea_ready, i * RING + r + 1)
                v.scalar_tensor_tensor(eh[r % 2], ea[r % 2], 0.5, up, ALU.mult, ALU.mult).then_inc(eh_ready, 1)

            rows(0, 0, 1)
            rows(1, 0, 1)
            with v.Fori(0, E1 // RING - 1) as i:
                for r in range(RING):
                    hidden(r, i)
                    rows((r + 2) % RING, i, 1 + (r + 2) // RING)
            for r in range(RING):
                hidden(r, E1 // RING - 1)
                if r + 2 < RING:
                    rows(r + 2, E1 // RING - 1, 1)
                if r == 1:
                    v.wait_ge(wi_in, 16)
                    v.tensor_scalar(W[:, FLT0:FLT0 + WI_N], W[:, INT0:INT0 + WI_N].bitcast(I32), 1.0 / 127.0, None,
                                    ALU.mult).then_inc(w3_ready, 1)

            def route2(S):
                r0, r1, r3 = S.r[0], S.r[1], S.r[3]
                S.logit_sums.wait(v)
                yield from then(S, v.tensor_tensor(r1[:, 0:E2], S.O[0:TQ, 0:E2], row("ebias", TQ, RC, RC0)[:, 0:E2], ALU.add))
                S.logits_ready.by(v.tensor_reduce(S.sc[:, 0:1], r1[:, 0:E2], AX_X, ALU.max, negate=True))
                yield "logits"
                S.exp_ready.wait(v)
                yield from then(S, v.reciprocal(S.sc[:, 2:3], S.sc[:, 1:2]))
                yield from then(S, v.tensor_scalar(r0[:, 0:E2], r0[:, 0:E2], S.sc[:, 2:3], None, ALU.mult))
                yield from top_mask(S, r0[:], E2, 2, r3[:])
                S.gate_ready.by(v.tensor_tensor(r3[:, 0:E2], r3[:, 0:E2], r0[:, 0:E2], ALU.mult))
                S.gate_ready.wait(v)
                S.gateT_sums.wait(v)
                S.gateT_ready.by(v.tensor_copy(S.gT[:], S.T[0:E2, 0:TQ]))
                yield from then(S, v.tensor_tensor(S.x[:], S.x[:], S.xn[:], ALU.add))
                yield "route"

            def phase_c(S, i):
                S.ctx_sums.wait(v)
                S.ctxT_ready.by(v.tensor_copy(S.yT[:], S.T[:, 0:TK]))
                v.wait_ge(S.gathered, i * 16 * TOP1 + 16 * TOP1)
                S.xin_free.by(v.scalar_tensor_tensor(S.x[:], S.y8[:, 0, :], S.myw[:, 0:1], S.xin[:], ALU.mult, ALU.add))
                S.xin_free.wait(v)
                for k in range(1, TOP1):
                    ins = v.scalar_tensor_tensor(S.x[:], S.y8[:, k, :], S.myw[:, k:k + 1], S.x[:], ALU.mult, ALU.add)
                    if k < TOP1 - 1:
                        yield from then(S, ins)
                S.y8_free.by(ins)
                S.y8_free.wait(v)
                yield from norm(S, S.x[:])
                yield "ctx"
                yield "context"
                turned_x(S)
                yield "turn"
                values(S, [0, 1], DM, S.O, KP)
                queries(S, 16, None, 0.25)
                values(S, [2], DM, S.B, KP)
                yield from heads(S, 16, TK)
                yield from attention_end(S, 16)
                yield from then(S, v.tensor_tensor(S.x[:], S.x[:], S.A[0:TQ, 0:DM], ALU.add))
                yield from norm(S, S.x[:])
                yield "out"
                turned_x(S)
                yield "turn"
                yield from route2(S)
                x = S.x[:]
                for n in range(E2 // 2 + 2):
                    bank = [S.B, S.A, S.O, S.T][n % 4][0:TQ, :]
                    S.pair_sums.wait(v)
                    if n < E2 // 2:
                        e = 2 * n
                        yield from then(S, v.scalar_tensor_tensor(x, bank[:, 0:DM], S.r[3][:, e:e + 1], x, ALU.mult, ALU.add))
                        S.pair_done.by(v.scalar_tensor_tensor(x, bank[:, DM:], S.r[3][:, e + 1:e + 2], x, ALU.mult, ALU.add))
                        S.pair_done.wait(v)
                    elif n == E2 // 2:
                        S.pair_done.by(v.tensor_tensor(S.xo[:], bank[:, 0:DM], row("bs0", TQ, RC, RC0), ALU.add))
                        S.pair_done.wait(v)
                        yield from then(S, v.tensor_tensor(S.xo[:], S.xo[:], row("bs1", TQ, RC, RC0), ALU.add))
                        yield from then(S, v.scalar_tensor_tensor(x, S.xo[:], 0.5, x, ALU.mult, ALU.add))
                    else:
                        S.pair_done.by(v.tensor_tensor(x, x, bank[:, 0:DM], ALU.add))
                        S.pair_done.wait(v)
                        yield from norm(S, x)
                    yield "pair"
                yield "context"
                turned_x(S)
                yield "turn"
                values(S, [0, 1], DM, S.O, KP, row("bv4", KP, RC, RC0))
                queries(S, DM, "bq4", None)
                values(S, [2], DM, S.B, KP, row("bv4", KP, RC, RC0))
                yield from heads(S, DM, TK, 1)
                yield from then(S, v.scalar_tensor_tensor(S.x[:], S.O[0:TQ, 0:DM], S.rinv[:, 0:1], S.x[:], ALU.mult, ALU.add))
                yield from norm(S, S.x[:])
                yield "out"
                turned_x(S)
                yield "turn"
                yield "f1"
                yield from glu(S, 3, 128, False)
                S.x_ready.by(v.tensor_copy(S.sc[:, 0:1], S.x[:, 0:1]))
                yield "end"

            v.wait_ge(first_in, 128)
            v.wait_ge(wc_in, 32)
            restart()
            with v.Fori(0, NB // 2) as i:
                run_pair(phase_c, i)
                iteration_end(v)


def kernel(**inputs):
    import numpy as np
    import concourse.bacc as bacc
    from concourse.bass_utils import run_bass_kernel_spmd as run

    g = {n: np.ascontiguousarray(a) for n, a in inputs.items()}

    def chunks(a, p=128):
        k, n = a.shape
        out = np.zeros((128, (k // p) * n), a.dtype)
        out[0:p] = a.reshape(k // p, p, n).transpose(1, 0, 2).reshape(p, -1)
        return out

    def heads(a):
        return a.transpose(1, 0, 2).reshape(a.shape[1], -1)

    def column(a):
        return a.reshape(-1, 128).T

    def wide(a, n):
        out = np.zeros((a.shape[0], n), a.dtype)
        out[:, 0:a.shape[1]] = a
        return out

    wa = [chunks(g["L0_xattn_Wq"]), g["L0_xattn_Wk"], g["L0_xattn_Wv"], chunks(g["L0_xattn_Wo"]), chunks(g["L0_ffn_Wr"])]
    for e in range(E0):
        wa += [chunks(g[f"L0_ffn_W{n}"][e]) for n in "gud"]
    for a in ("a1", "a2"):
        wa += [chunks(heads(g[f"L1_xattn_{a}_w{n}"])) for n in "qkv"]
        wa += [chunks(g[f"L1_xattn_{a}_li{n}_w"]) for n in (1, 2, 3)]
    wa += [chunks(g["L1_ffn_router_w"].T), chunks(g["L1_ffn_ws_gate_up"]), chunks(g["L1_ffn_ws_down"], FH)]
    wr = g["L2_ffn_Wr"].transpose(0, 2, 1)
    wc = [chunks(g["L2_xattn_Wq"].T), chunks(g["L2_xattn_Wkv"].T[:, 0:DM]), chunks(g["L2_xattn_Wkv"].T[:, DM:]),
          chunks(g["L2_xattn_Wo"].T), chunks(g["L2_ffn_centroids"].T)]
    wc += [chunks(np.concatenate([wr[2 * e], wr[2 * e + 1]], 1)) for e in range(E2 // 2)]
    wc += [chunks(g["L2_ffn_Ws"][n].T) for n in range(2)]
    br = np.zeros((128, DM), np.float32)
    br[0:E2] = g["L2_ffn_br"]
    wc += [br, chunks(g["L3_xattn_Wq"]), g["L3_xattn_Wk"], g["L3_xattn_Wv"]]
    wi = [chunks(g["L3_ffn_w_gate"].T), chunks(g["L3_ffn_w_up"].T), chunks(g["L3_ffn_w_down"].T)]
    L1 = "L1_xattn_"
    ra = [g["L0_xattn_bv"], g["L0_xattn_bo"]] + [g[L1 + n] for n in (
        "ln1_g", "ln1_b", "ln2_g", "ln2_b", "a1_li1_b", "a1_li3_b", "a2_li1_b", "a2_li3_b")]
    rc = [g["L2_ffn_bs"][0], g["L2_ffn_bs"][1], g["L3_xattn_bv"], wide(g["L2_ffn_expert_biases"].reshape(1, -1), DM)[0]]
    even = np.zeros((128, 1), np.float32)
    even.reshape(4, 2, 16)[:, 0] = 0.25
    odd = np.zeros((128, 1), np.float32)
    odd.reshape(4, 2, 16)[:, 1] = 0.25
    cols = [column(g["L0_xattn_bq"]), column(g["L0_xattn_bk"])]
    for a in ("a1", "a2"):
        cols += [column(g[L1 + f"{a}_{n}"]) for n in ("lnx_g", "lnx_b", "lny_g", "lny_b", "ln3_g", "ln3_b", "li2_b")]
    cols += [column(g["L3_xattn_bq"]), column(g["L3_xattn_bk"]), even, odd,
             np.broadcast_to(g["L0_ffn_temperature"].reshape(1, 1), (128, 1))]
    n = np.arange(128)
    consts = [np.eye(128), n[:, None] < n[None, :], n[:, None] > n[None, :], np.tile(np.arange(E1), (128, 1))]
    arrays = {
        "x": np.concatenate([g["x"], np.zeros_like(g["x"][0:2])]),
        "ctx": np.concatenate([g["ctx_512"], np.zeros_like(g["ctx_512"][0:2])]),
        "wa": np.concatenate(wa, 1), "wc": np.concatenate(wc, 1), "wi": np.concatenate(wi, 1),
        "ra": np.concatenate(ra), "rc": np.concatenate(rc), "cols": np.concatenate(cols, 1),
        "consts": np.concatenate([c.astype(np.float32) for c in consts], 1),
        "eg": np.concatenate([g["L1_ffn_w_gate"].reshape(E1, 2, 128, F1), g["L1_ffn_w_up"].reshape(E1, 2, 128, F1)], 3)
                .transpose(0, 2, 1, 3).reshape(E1, 128, 4 * F1),
        "ed": g["L1_ffn_w_down"].reshape(E1, 2, FH, DM).transpose(0, 2, 1, 3).reshape(E1, FH, 2 * DM),
        "tokens": np.arange(NT, dtype=np.uint32)[:, None],
    }
    arrays = {n: np.ascontiguousarray(a) for n, a in arrays.items()}
    assert arrays["wa"].shape[1] == WA_N and arrays["wc"].shape[1] == WC_N and arrays["cols"].shape[1] == CO_N
    nc = bacc.Bacc("TRN2", target_bir_lowering=False, num_devices=1)
    arrays = {f"in_{n}": a for n, a in arrays.items()}
    tensors = {n[3:]: nc.dram_tensor(n, a.shape, mybir.dt.from_np(a.dtype), kind="ExternalInput").ap() for n, a in arrays.items()}
    tensors["out"] = nc.dram_tensor("out", (NB, TQ, DM), F32, kind="ExternalOutput").ap()
    build(nc, tensors)
    return run(nc, [arrays], core_ids=[0]).results[0]["out"]
```
